# Optimizing a Trainium2 kernel written in Bass

```python
import numpy as np
import jax
import jax.numpy as jnp

def _softmax(x, axis=-1):
    return jax.nn.softmax(x, axis=axis)

def _gelu(x):
    return jax.nn.gelu(x, approximate=True)

def _silu(x):
    return jax.nn.silu(x)

def _sigmoid(x):
    return jax.nn.sigmoid(x)

def _layernorm(x, axis=-1, eps=1e-05):
    m = jnp.mean(x, axis=axis, keepdims=True)
    v = jnp.var(x, axis=axis, keepdims=True)
    return (x - m) / jnp.sqrt(v + eps)

def _scatter_add(tgt, idx, src, axis=0):
    return tgt.at[idx].add(src)

def _segment_sum(src, seg, n):
    return jax.ops.segment_sum(src, seg, n)
kernel_name = 'mk_macaron_d1_jaxref_r8_0fcd1f'

def setup_inputs(seed: int=0):
    np.random.seed(seed)
    _w = jnp.asarray

    def _L0_attn_setup():
        import jax, jax.numpy as jnp
        import numpy as np
        D_MODEL = 128
        D_STATE = 128
        D_CONV = 4
        EXPAND = 2
        HEADDIM = 64
        NGROUPS = 1
        D_INNER = EXPAND * D_MODEL
        NHEADS = D_INNER // HEADDIM
        D_IN_PROJ = 2 * D_INNER + 2 * NGROUPS * D_STATE + NHEADS
        CONV_DIM = D_INNER + 2 * NGROUPS * D_STATE
        BATCH = 2
        SEQLEN = 64
        EPS = 1e-05

        def _silu(x):
            return x * jax.nn.sigmoid(x)
        key = jax.random.key(seed)
        ks = jax.random.split(key, 8)
        u = jax.random.normal(ks[0], (BATCH, SEQLEN, D_MODEL), jnp.float32)
        W_in = jax.random.normal(ks[1], (D_IN_PROJ, D_MODEL), jnp.float32) * D_MODEL ** (-0.5)
        conv_w = jax.random.normal(ks[2], (CONV_DIM, 1, D_CONV), jnp.float32) * D_CONV ** (-0.5)
        conv_b = jnp.zeros((CONV_DIM,), jnp.float32)
        dt = jnp.exp(jax.random.uniform(ks[3], (NHEADS,), jnp.float32) * (np.log(0.1) - np.log(0.001)) + np.log(0.001))
        dt = jnp.clip(dt, 0.0001, None)
        dt_bias = dt + jnp.log(-jnp.expm1(-dt))
        A_log = jnp.log(jax.random.uniform(ks[4], (NHEADS,), jnp.float32, minval=1.0, maxval=16.0))
        D_param = jnp.ones((NHEADS,), jnp.float32)
        norm_w = jnp.ones((D_INNER,), jnp.float32)
        W_out = jax.random.normal(ks[5], (D_MODEL, D_INNER), jnp.float32) * D_INNER ** (-0.5)
        return dict(u=u, W_in=W_in, conv_w=conv_w, conv_b=conv_b, dt_bias=dt_bias, A_log=A_log, D_param=D_param, norm_w=norm_w, W_out=W_out)
    _L0_attn_in = _L0_attn_setup()

    def _L0_ffn_setup():
        import jax, jax.numpy as jnp
        import numpy as np
        B, S, D = (4, 64, 128)
        E, K, H = (64, 8, 32)
        ES, HS = (2, 256)
        key = jax.random.key(seed)
        ks = jax.random.split(key, 8)
        scale = 0.02
        rn = lambda k, shape, s: jax.random.normal(k, shape, jnp.float32) * s
        return {'x': rn(ks[0], (B, S, D), 1.0), 'router_w': rn(ks[1], (D, E), scale), 'router_b': jnp.zeros((E,), jnp.float32), 'w1': rn(ks[2], (E, D, H), scale), 'b1': jnp.zeros((E, H), jnp.float32), 'w2': rn(ks[3], (E, H, D), scale), 'b2': jnp.zeros((E, D), jnp.float32), 'sw1': rn(ks[4], (ES, D, HS), scale), 'sb1': jnp.zeros((ES, HS), jnp.float32), 'sw2': rn(ks[5], (ES, HS, D), scale), 'sb2': jnp.zeros((ES, D), jnp.float32)}
    _L0_ffn_in = _L0_ffn_setup()
    _d = {'L0_attn_u': _L0_attn_in['u'], 'L0_attn_W_in': _L0_attn_in['W_in'], 'L0_attn_conv_w': _L0_attn_in['conv_w'], 'L0_attn_conv_b': _L0_attn_in['conv_b'], 'L0_attn_dt_bias': _L0_attn_in['dt_bias'], 'L0_attn_A_log': _L0_attn_in['A_log'], 'L0_attn_D_param': _L0_attn_in['D_param'], 'L0_attn_norm_w': _L0_attn_in['norm_w'], 'L0_attn_W_out': _L0_attn_in['W_out'], 'L0_ffn_router_w': _L0_ffn_in['router_w'], 'L0_ffn_router_b': _L0_ffn_in['router_b'], 'L0_ffn_w1': _L0_ffn_in['w1'], 'L0_ffn_b1': _L0_ffn_in['b1'], 'L0_ffn_w2': _L0_ffn_in['w2'], 'L0_ffn_b2': _L0_ffn_in['b2'], 'L0_ffn_sw1': _L0_ffn_in['sw1'], 'L0_ffn_sb1': _L0_ffn_in['sb1'], 'L0_ffn_sw2': _L0_ffn_in['sw2'], 'L0_ffn_sb2': _L0_ffn_in['sb2']}
    _x0 = _d['L0_attn_u']
    _d['L0_attn_u'] = jax.random.normal(jax.random.fold_in(jax.random.key(seed), 1), (8, 512, 128), dtype=_x0.dtype)
    del _x0
    return _d

def reference(L0_attn_u, L0_attn_W_in, L0_attn_conv_w, L0_attn_conv_b, L0_attn_dt_bias, L0_attn_A_log, L0_attn_D_param, L0_attn_norm_w, L0_attn_W_out, L0_ffn_router_w, L0_ffn_router_b, L0_ffn_w1, L0_ffn_b1, L0_ffn_w2, L0_ffn_b2, L0_ffn_sw1, L0_ffn_sb1, L0_ffn_sw2, L0_ffn_sb2):

    def _L0_attn_ref(u, W_in, conv_w, conv_b, dt_bias, A_log, D_param, norm_w, W_out):
        import jax, jax.numpy as jnp
        import numpy as np
        D_MODEL = 128
        D_STATE = 128
        D_CONV = 4
        EXPAND = 2
        HEADDIM = 64
        NGROUPS = 1
        D_INNER = EXPAND * D_MODEL
        NHEADS = D_INNER // HEADDIM
        D_IN_PROJ = 2 * D_INNER + 2 * NGROUPS * D_STATE + NHEADS
        CONV_DIM = D_INNER + 2 * NGROUPS * D_STATE
        BATCH = 2
        SEQLEN = 64
        EPS = 1e-05

        def _silu(x):
            return x * jax.nn.sigmoid(x)
        B, L, _ = u.shape
        zxbcdt = jnp.einsum('bld,ed->ble', u, W_in)
        z = zxbcdt[..., :D_INNER]
        xBC = zxbcdt[..., D_INNER:D_INNER + CONV_DIM]
        dt = zxbcdt[..., D_INNER + CONV_DIM:]
        xc = jnp.transpose(xBC, (0, 2, 1))
        xc = jax.lax.conv_general_dilated(xc, conv_w, window_strides=(1,), padding=[(D_CONV - 1, 0)], dimension_numbers=('NCH', 'OIH', 'NCH'), feature_group_count=CONV_DIM)
        xc = xc + conv_b[None, :, None]
        xBC = _silu(jnp.transpose(xc, (0, 2, 1)))
        x = xBC[..., :D_INNER].reshape(B, L, NHEADS, HEADDIM)
        Bv = xBC[..., D_INNER:D_INNER + NGROUPS * D_STATE].reshape(B, L, NGROUPS, D_STATE)
        Cv = xBC[..., D_INNER + NGROUPS * D_STATE:].reshape(B, L, NGROUPS, D_STATE)
        A = -jnp.exp(A_log)
        dt = jax.nn.softplus(dt + dt_bias)

        def step(state, inp):
            dt_t, x_t, B_t, C_t = inp
            dA = jnp.exp(dt_t * A)
            dBx = jnp.einsum('bh,bgn,bhp->bhpn', dt_t, B_t, x_t)
            state = state * dA[:, :, None, None] + dBx
            y = jnp.einsum('bhpn,bgn->bhp', state, C_t) + D_param[:, None] * x_t
            return (state, y)
        state0 = jnp.zeros((B, NHEADS, HEADDIM, D_STATE), u.dtype)
        xs = (jnp.moveaxis(dt, 1, 0), jnp.moveaxis(x, 1, 0), jnp.moveaxis(Bv, 1, 0), jnp.moveaxis(Cv, 1, 0))
        _, ys = jax.lax.scan(step, state0, xs)
        y = jnp.moveaxis(ys, 0, 1).reshape(B, L, D_INNER)
        yg = y * _silu(z)
        yn = yg * jax.lax.rsqrt(jnp.mean(yg * yg, axis=-1, keepdims=True) + EPS) * norm_w
        return jnp.einsum('bld,ed->ble', yn, W_out)

    def _L0_ffn_ref(x, router_w, router_b, w1, b1, w2, b2, sw1, sb1, sw2, sb2):
        import jax, jax.numpy as jnp
        import numpy as np
        B, S, D = (4, 64, 128)
        E, K, H = (64, 8, 32)
        ES, HS = (2, 256)
        b_, s_, d_ = x.shape
        xf = x.reshape(-1, d_)
        probs = jax.nn.softmax(xf @ router_w + router_b, axis=-1)
        tw, ti = jax.lax.top_k(probs, K)
        tw = tw / jnp.sum(tw, axis=-1, keepdims=True)

        def body(acc, p):
            W1, B1, W2, B2, e = p
            h = jax.nn.silu(xf @ W1 + B1) @ W2 + B2
            cw = jnp.sum(jnp.where(ti == e, tw, 0.0), axis=-1)
            return (acc + cw[:, None] * h, None)
        routed, _ = jax.lax.scan(body, jnp.zeros_like(xf), (w1, b1, w2, b2, jnp.arange(w1.shape[0])))

        def shared_mlp(W1, B1, W2, B2):
            return jax.nn.silu(xf @ W1 + B1) @ W2 + B2
        shared = jnp.sum(jax.vmap(shared_mlp)(sw1, sb1, sw2, sb2), axis=0)
        return (routed + shared).reshape(b_, s_, d_)
    x = L0_attn_u
    x = x + 0.5 * _L0_ffn_ref(_layernorm(x, axis=-1), L0_ffn_router_w, L0_ffn_router_b, L0_ffn_w1, L0_ffn_b1, L0_ffn_w2, L0_ffn_b2, L0_ffn_sw1, L0_ffn_sb1, L0_ffn_sw2, L0_ffn_sb2)
    x = x + _L0_attn_ref(_layernorm(x, axis=-1), L0_attn_W_in, L0_attn_conv_w, L0_attn_conv_b, L0_attn_dt_bias, L0_attn_A_log, L0_attn_D_param, L0_attn_norm_w, L0_attn_W_out)
    x = x + 0.5 * _L0_ffn_ref(_layernorm(x, axis=-1), L0_ffn_router_w, L0_ffn_router_b, L0_ffn_w1, L0_ffn_b1, L0_ffn_w2, L0_ffn_b2, L0_ffn_sw1, L0_ffn_sb1, L0_ffn_sw2, L0_ffn_sb2)
    return x

_drawn_inputs = setup_inputs


def setup_inputs(seed=0):
    import zlib

    import numpy as np

    out = dict(_drawn_inputs(seed))
    spreads = {'L0_attn_conv_b': (0.0, 0.1),
     'L0_attn_D_param': (1.0, 0.2),
     'L0_attn_norm_w': (1.0, 0.2),
     'L0_ffn_router_b': (0.0, 0.414),
     'L0_ffn_b1': (0.0, 0.8),
     'L0_ffn_b2': (0.0, 0.1),
     'L0_ffn_sb1': (0.0, 0.342),
     'L0_ffn_sb2': (0.0, 0.1)}
    factors = {'L0_ffn_w1': 8.0, 'L0_ffn_w2': 8.0}
    for name, (base, spread) in spreads.items():
        noise = np.random.default_rng([zlib.crc32(name.encode()), seed]).standard_normal(out[name].shape)
        drawn = base * np.exp(spread * noise) if base else spread * noise
        out[name] = jnp.asarray(drawn.astype(out[name].dtype))
    for name, factor in factors.items():
        out[name] = (out[name] * factor).astype(out[name].dtype)
    return out
```

```python
import numpy as np
import concourse.bass as bass
from concourse import mybir
from contextlib import ExitStack

F32 = mybir.dt.float32
F32R = mybir.dt.float32r
ALU = mybir.AluOpType
ACT = mybir.ActivationFunctionType
AX = mybir.AxisListType

P = 128
D = 128
BATCHES, SEQ = 8, 512
TOKENS = BATCHES * SEQ
TILES = TOKENS // P
TPB = SEQ // P
E, HE = 64, 32
ES, HS = 2, 256
TOPK = 8
EPS = 1e-5
ROUTED = E * HE // P
SHARED = ES * HS // P
BLOCKS = ROUTED + SHARED
EPB = P // HE
GROUP = 1024
GROUPS = TOKENS // GROUP
HALF = 512
RING = 4
LAG = 3

DI = 256
NH, HD = 4, 64
NS = 128
ZW = DI
CB = (DI + 2 * NS) // P
TAPS = 4

ORDER = []
for _q in range(SHARED):
    ORDER += [("routed", _q * (ROUTED // SHARED) + _r) for _r in range(ROUTED // SHARED)]
    ORDER.append(("shared", ROUTED + _q))


class Signal:

    def __init__(self, sem, credit):
        self.sem, self.credit = sem, credit

    def at(self, n):
        return n + (1 + self.credit)


def done(signal, n):
    return signal.sem, signal.at(n)


class Signals:

    def __init__(self, nc, ctx, phase, names, credits=()):
        self.all = {}
        for name in names:
            self.all[name] = Signal(ctx.enter_context(nc.semaphore(f"{phase}_{name}")), 0)
        for name, credit in dict(credits).items():
            self.all[name] = Signal(ctx.enter_context(nc.semaphore(f"{phase}_{name}")), credit)

    def __getitem__(self, name):
        return self.all[name]

    def give_credits(self, eng):
        for s in self.all.values():
            if s.credit:
                eng.sem_inc(s.sem, s.credit)


class Tensors:
    pass


def ffn_phase(nc, m, phase, out):
    with ExitStack() as ctx:
        def sb(name, shape, dt):
            return ctx.enter_context(nc.sbuf_tensor(f"{phase}_{name}", shape, dt))

        hidden = sb("hidden", [P, RING, GROUP], F32)
        hid_hi = sb("hid_hi", [P, RING, GROUP], F32R)
        hid_lo = sb("hid_lo", [P, RING, GROUP], F32R)
        weights = sb("weights", [P, GROUP], F32)
        yT = sb("yT", [P, GROUP], F32)
        up_ps = ctx.enter_context(nc.psum_tensor(f"{phase}_up_ps", [P, 2, GROUP], F32))
        acc_ps = ctx.enter_context(nc.psum_tensor(f"{phase}_acc_ps", [P, GROUP], F32))
        cw_ps = ctx.enter_context(nc.psum_tensor(f"{phase}_cw_ps", [P, GROUP], F32))
        s = Signals(nc, ctx, phase,
                    ["dve_held", "up_ready", "hi_ready", "shuffled", "weights_ready",
                     "yT_ready", "y_ready", "stored"],
                    {"silu_done": 2, "gated": 1, "lo_ready": RING, "down_done": RING, "x_updated": 1})
        xh = m.xn_hi[:, :].rearrange("p (g n) -> p g n", g=GROUPS)
        xl = m.xn_lo[:, :].rearrange("p (g n) -> p g n", g=GROUPS)
        cwT = m.cwT[:, :].rearrange("p (g n) -> p g n", g=GROUPS)
        x_res = m.x[:, :].rearrange("p (g n) -> p g n", g=GROUPS)
        out_v = out.rearrange("b (t p) d -> p (b t) d", p=P)
        tpg = GROUP // P

        with nc.Block() as block:
            @block.sync
            def _(sp):
                if phase == "ffn2":
                    with sp.Fori(0, GROUPS) as g:
                        sp.wait_ge(*done(s["x_updated"], g))
                        sp.dma_start(out_v[:, bass.ts(g, tpg), :],
                                     m.x[:, bass.ts(g, GROUP)].rearrange("p (t d) -> p t d", d=D)
                                     ).then_inc(s["stored"].sem, 16)
                    sp.wait_ge(s["stored"].sem, 16 * GROUPS)

            @block.tensor
            def _(pe):
                with pe.Fori(0, GROUPS) as g:
                    g0 = pe.snap(g * BLOCKS)
                    for n in range(BLOCKS + LAG):
                        if n < BLOCKS:
                            j = ORDER[n][1]
                            wh = m.w1_hi[:, j * P:(j + 1) * P]
                            wl = m.w1_lo[:, j * P:(j + 1) * P]
                            pe.wait_ge(*done(s["silu_done"], g0 + (n - 2)))
                            for h in range(GROUP // HALF):
                                cols = slice(h * HALF, (h + 1) * HALF)
                                o = up_ps[:, n % 2, cols]
                                nc.tensor.matmul(o, wh, xh[:, g, cols], start=True, stop=False)
                                nc.tensor.matmul(o, wh, xl[:, g, cols], start=False, stop=False)
                                last = nc.tensor.matmul(o, wl, xh[:, g, cols], start=False, stop=True)
                            last.then_inc(s["up_ready"].sem, 1)
                        k = n - LAG
                        if k == 0:
                            pe.wait_ge(*done(s["x_updated"], g - 1))
                            pe.wait_ge(*done(s["weights_ready"], g))
                            for h in range(GROUP // HALF):
                                cols = slice(h * HALF, (h + 1) * HALF)
                                nc.tensor.matmul(acc_ps[:, cols], m.b2q[:, :], weights[:, cols],
                                                 start=True, stop=False)
                        if k >= 0:
                            j = ORDER[k][1]
                            wh = m.w2_hi[:, j * P:(j + 1) * P]
                            wl = m.w2_lo[:, j * P:(j + 1) * P]
                            pe.wait_ge(*done(s["lo_ready"], g0 + k))
                            for h in range(GROUP // HALF):
                                cols = slice(h * HALF, (h + 1) * HALF)
                                o = acc_ps[:, cols]
                                nc.tensor.matmul(o, wh, hid_hi[:, k % RING, cols], start=False, stop=False)
                                nc.tensor.matmul(o, wh, hid_lo[:, k % RING, cols], start=False, stop=False)
                                last = nc.tensor.matmul(o, wl, hid_hi[:, k % RING, cols], start=False,
                                                        stop=k == BLOCKS - 1)
                            last.then_inc(s["down_done"].sem, 1)
                    pe.wait_ge(*done(s["yT_ready"], g))
                    for t in range(tpg):
                        last = nc.tensor.transpose(acc_ps[:, t * P:(t + 1) * P],
                                                   yT[:, t * P:(t + 1) * P], m.ident[:, :])
                    last.then_inc(s["y_ready"].sem, 1)

            @block.scalar
            def _(act):
                nc.scalar.preload_act_table(ACT.Silu)
                with act.Fori(0, GROUPS) as g:
                    g0 = act.snap(g * BLOCKS)
                    nc.scalar.activation(weights[:, :], cwT[:, g, :], ACT.Copy
                                         ).then_inc(s["weights_ready"].sem, 1)
                    for n in range(BLOCKS + 1):
                        if n < BLOCKS:
                            j = ORDER[n][1]
                            act.wait_ge(*done(s["lo_ready"], g0 + (n - RING)))
                            act.wait_ge(*done(s["up_ready"], g0 + n))
                            nc.scalar.activation(hidden[:, n % RING, :], up_ps[:, n % 2, :], ACT.Silu,
                                                 bias=m.cols[:, j:j + 1]
                                                 ).then_inc(s["silu_done"].sem, 1)
                        k = n - 1
                        if k >= 0:
                            r = sum(kind == "routed" for kind, _ in ORDER[:k + 1])
                            if ORDER[k][0] == "routed":
                                act.wait_ge(*done(s["gated"], g * ROUTED + (r - 1)))
                            else:
                                act.wait_ge(*done(s["silu_done"], g0 + k))
                            act.wait_ge(*done(s["down_done"], g0 + (k - RING)))
                            nc.scalar.activation(hid_hi[:, k % RING, :], hidden[:, k % RING, :], ACT.Copy
                                                 ).then_inc(s["hi_ready"].sem, 1)
                    act.wait_ge(*done(s["down_done"], g0 + (BLOCKS - 1)))
                    nc.scalar.activation(yT[:, :], acc_ps[:, :], ACT.Identity, bias=m.half_sb2[:, 0:1],
                                         scale=0.5).then_inc(s["yT_ready"].sem, 1)

            @block.vector
            def _(dve):
                with dve.Fori(0, GROUPS) as g:
                    g0 = dve.snap(g * BLOCKS)
                    r = 0
                    dve.wait_ge(*done(s["weights_ready"], g))
                    for n, (kind, j) in enumerate(ORDER):
                        if kind == "shared":
                            continue
                        dve.wait_ge(*done(s["gated"], g * ROUTED + (r - 1)))
                        dve.sem_inc(s["dve_held"].sem, 1)
                        nc.vector.stream_shuffle(cw_ps[:, :], weights[:, :], [j] * 32
                                                 ).then_inc(s["shuffled"].sem, 1)
                        dve.wait_ge(*done(s["shuffled"], g * ROUTED + r))
                        dve.wait_ge(*done(s["silu_done"], g0 + n))
                        nc.vector.tensor_tensor(hidden[:, n % RING, :], hidden[:, n % RING, :], cw_ps[:, :],
                                                ALU.mult).then_inc(s["gated"].sem, 1)
                        r += 1
                    dve.wait_ge(*done(s["y_ready"], g))
                    nc.vector.tensor_tensor(x_res[:, g, :], acc_ps[:, :], x_res[:, g, :], ALU.add
                                            ).then_inc(s["x_updated"].sem, 1)

            @block.gpsimd
            def _(pool):
                s.give_credits(pool)
                with pool.Fori(0, GROUPS) as g:
                    g0 = pool.snap(g * BLOCKS)
                    for n in range(BLOCKS):
                        pool.wait_ge(*done(s["hi_ready"], g0 + n))
                        nc.gpsimd.tensor_tensor(hid_lo[:, n % RING, :], hidden[:, n % RING, :],
                                                hid_hi[:, n % RING, :].bitcast(F32), ALU.subtract
                                                ).then_inc(s["lo_ready"].sem, 1)


N_COLS = BLOCKS + CB + DI // P
N_ROWS = E + 3 * NH


def prepare_phase(nc, m, a):
    with ExitStack() as ctx:
        def sb(name, shape, dt=F32):
            return ctx.enter_context(nc.sbuf_tensor(f"prep_{name}", shape, dt))

        w1_raw = sb("w1_raw", [P, BLOCKS * P])
        w2_raw = sb("w2_raw", [P, BLOCKS * P])
        col_rows = sb("col_rows", [N_COLS, P])
        row_vals = sb("row_vals", [1, N_ROWS])
        sb2_rows = sb("sb2_rows", [ES, D])
        win = sb("win", [P, 2 + CB, D])
        win_dt = sb("win_dt", [NH, D])
        conv_w = sb("conv_w", [P, CB, TAPS])
        win_tap = sb("win_tap", [P, CB, TAPS, D])
        wout_raw = sb("wout_raw", [P, DI])
        sb2_sum = sb("sb2_sum", [P, 1])
        ps = ctx.enter_context(nc.psum_tensor("prep_ps", [P, 8, 512], F32))
        s = Signals(nc, ctx, "prep", [
            "x_in", "small_in", "win_in", "w1_in", "w2_in", "zeroed", "consts", "b2q_zeroed", "b2q_in",
            "cols_ps", "cols", "rows_ps", "rows", "exp_a", "sb2_ps", "sb2", "z_ps", "z_hi", "taps",
            "taps_ps", "taps_hi", "wout_ps", "w1_hi", "w2_hi"])

        with nc.Block() as block:
            @block.sync
            def _(sp):
                sp.dma_start(win[:, :, :], a["W_in"][0:(2 + CB) * P, :].rearrange("(b p) d -> p b d", p=P)
                             ).then_inc(s["win_in"].sem, 16)
                sp.dma_start(win_dt[:, :], a["W_in"][(2 + CB) * P:, :]).then_inc(s["win_in"].sem, 16)
                sp.dma_start(m.x[:, :].rearrange("p (t d) -> p t d", d=D),
                             a["u"].rearrange("b (t p) d -> p (b t) d", p=P)).then_inc(s["x_in"].sem, 16)
                sp.dma_start(w2_raw[:, 0:ROUTED * P].rearrange("p (b d) -> p b d", d=D),
                             a["w2"].rearrange("e h d -> (e h) d").rearrange("(b p) d -> p b d", p=P)
                             ).then_inc(s["w2_in"].sem, 16)
                sp.dma_start(w2_raw[:, ROUTED * P:].rearrange("p (b d) -> p b d", d=D),
                             a["sw2"].rearrange("e h d -> (e h) d").rearrange("(b p) d -> p b d", p=P)
                             ).then_inc(s["w2_in"].sem, 16)
                sp.wait_ge(s["x_in"].sem, 16)
                sp.wait_ge(s["b2q_in"].sem, 64)

            @block.scalar
            def _(act):
                def rows_in(lo, hi, src):
                    act.dma_start(col_rows[lo:hi, :], src).then_inc(s["small_in"].sem, 16)

                rows_in(0, ROUTED, a["b1"].rearrange("(b e) h -> b (e h)", e=EPB))
                rows_in(ROUTED, BLOCKS, a["sb1"].rearrange("e (b h) -> (e b) h", h=P))
                rows_in(BLOCKS, BLOCKS + CB, a["conv_b"].rearrange("(b p) -> b p", p=P))
                rows_in(BLOCKS + CB, N_COLS, a["norm_w"].rearrange("(b p) -> b p", p=P))

                def vals_in(lo, hi, src):
                    act.dma_start(row_vals[0:1, lo:hi], src.rearrange("(a n) -> a n", a=1)
                                  ).then_inc(s["small_in"].sem, 16)

                vals_in(0, E, a["router_b"])
                vals_in(E, E + NH, a["dt_bias"])
                vals_in(E + NH, E + 2 * NH, a["A_log"])
                vals_in(E + 2 * NH, N_ROWS, a["D_param"])
                act.dma_start(sb2_rows[:, :], a["sb2"]).then_inc(s["small_in"].sem, 16)
                act.dma_start(conv_w[:, :, :], a["conv_w"].rearrange("(b p) o k -> p b (o k)", p=P)
                              ).then_inc(s["small_in"].sem, 16)
                act.dma_start(wout_raw[:, :], a["W_out"]).then_inc(s["small_in"].sem, 16)
                act.dma_start(m.router_w[:, :], a["router_w"]).then_inc(s["small_in"].sem, 16)
                act.dma_start(w1_raw[:, 0:ROUTED * P].rearrange("p (e h) -> p e h", h=HE),
                              a["w1"].rearrange("e d h -> d e h")).then_inc(s["w1_in"].sem, 16)
                act.dma_start(w1_raw[:, ROUTED * P:].rearrange("p (e h) -> p e h", h=HS),
                              a["sw1"].rearrange("e d h -> d e h")).then_inc(s["w1_in"].sem, 16)
                act.wait_ge(s["cols_ps"].sem, 1)
                nc.scalar.activation(m.cols[:, :], ps[:, 0, 0:N_COLS], ACT.Copy).then_inc(s["cols"].sem, 1)
                act.wait_ge(s["rows_ps"].sem, 1)
                nc.scalar.activation(m.rows[:, :], ps[:, 1, 0:N_ROWS], ACT.Copy).then_inc(s["rows"].sem, 1)
                act.wait_ge(s["rows"].sem, 1)
                nc.scalar.activation(m.a_neg[:, :], m.rows[:, E + NH:E + 2 * NH], ACT.Exp
                                     ).then_inc(s["exp_a"].sem, 1)
                act.wait_ge(s["z_ps"].sem, 1)
                nc.scalar.activation(m.wz_hi[:, :], ps[:, 2, 0:ZW + NH], ACT.Copy).then_inc(s["z_hi"].sem, 1)
                act.wait_ge(s["taps_ps"].sem, 1)
                nc.scalar.activation(m.wc_hi[:, :], ps[:, 3:3 + CB, :], ACT.Copy
                                     ).then_inc(s["taps_hi"].sem, 1)
                act.wait_ge(s["w2_in"].sem, 32)
                nc.scalar.activation(m.w2_hi[:, :], w2_raw[:, :], ACT.Copy).then_inc(s["w2_hi"].sem, 1)
                act.wait_ge(s["w1_in"].sem, 32)
                nc.scalar.activation(m.w1_hi[:, :], w1_raw[:, :], ACT.Copy).then_inc(s["w1_hi"].sem, 1)

            @block.gpsimd
            def _(pool):
                nc.gpsimd.memset(m.b2q[:, :], 0.0).then_inc(s["b2q_zeroed"].sem, 1)
                nc.gpsimd.memset(m.minus_half[:, :], -0.5)
                nc.gpsimd.memset(m.ones[:, :], 1.0).then_inc(s["zeroed"].sem, 1)
                pool.wait_ge(s["zeroed"].sem, 1)
                nc.gpsimd.affine_select(out=m.ident[:, :], in_=m.ones[:, :], compare_op=ALU.is_equal,
                                        fill=0.0, base=0, pattern=[[-1, P]], channel_multiplier=1
                                        ).then_inc(s["consts"].sem, 1)
                nc.gpsimd.affine_select(out=m.upto[:, :], in_=m.ones[:, :], compare_op=ALU.is_ge,
                                        fill=0.0, base=0, pattern=[[1, P]], channel_multiplier=-1
                                        ).then_inc(s["consts"].sem, 1)
                nc.gpsimd.affine_select(out=m.after[:, :], in_=m.ones[:, :], compare_op=ALU.is_gt,
                                        fill=0.0, base=0, pattern=[[-1, P]], channel_multiplier=1
                                        ).then_inc(s["consts"].sem, 1)
                pool.wait_ge(s["b2q_zeroed"].sem, 1)
                b2_v = a["b2"].rearrange("(j q) d -> q j d", q=4)
                for q in range(4):
                    pool.dma_start(m.b2q[32 * q:32 * q + E // 4, :], b2_v[q, :, :]
                                   ).then_inc(s["b2q_in"].sem, 16)

            @block.tensor
            def _(pe):
                pe.wait_ge(s["consts"].sem, 3)
                pe.wait_ge(s["small_in"].sem, 16 * 12)
                nc.tensor.transpose(ps[:, 0, 0:N_COLS], col_rows[:, :], m.ident[0:N_COLS, 0:N_COLS]
                                    ).then_inc(s["cols_ps"].sem, 1)
                nc.tensor.matmul(ps[:, 1, 0:N_ROWS], m.ones[0:1, :], row_vals[:, :], start=True, stop=True
                                 ).then_inc(s["rows_ps"].sem, 1)
                pe.wait_ge(s["win_in"].sem, 32)
                for b in range(ZW // P):
                    nc.tensor.transpose(ps[:, 2, b * P:(b + 1) * P], win[:, b, :], m.ident[:, :])
                nc.tensor.transpose(ps[:, 2, ZW:ZW + NH], win_dt[:, :], m.ident[0:NH, 0:NH]
                                    ).then_inc(s["z_ps"].sem, 1)
                pe.wait_ge(s["taps"].sem, 1)
                for b in range(CB):
                    for k in range(TAPS):
                        last = nc.tensor.transpose(ps[:, 3 + b, k * P:(k + 1) * P], win_tap[:, b, k, :],
                                                   m.ident[:, :])
                last.then_inc(s["taps_ps"].sem, 1)
                for b in range(DI // P):
                    last = nc.tensor.transpose(ps[:, 7, b * P:(b + 1) * P], wout_raw[:, b * P:(b + 1) * P],
                                               m.ident[:, :])
                last.then_inc(s["wout_ps"].sem, 1)
                pe.wait_ge(s["cols"].sem, 1)
                nc.tensor.matmul(ps[:, 0, 0:1], sb2_rows[:, :], m.ones[0:ES, 0:1], start=True, stop=True
                                 ).then_inc(s["sb2_ps"].sem, 1)

            @block.vector
            def _(dve):
                dve.wait_ge(s["small_in"].sem, 16 * 12)
                dve.wait_ge(s["win_in"].sem, 32)
                for b in range(CB):
                    for k in range(TAPS):
                        last = nc.vector.tensor_scalar(win_tap[:, b, k, :], win[:, 2 + b, :],
                                                       conv_w[:, b, k:k + 1], None, ALU.mult)
                last.then_inc(s["taps"].sem, 1)
                dve.wait_ge(s["exp_a"].sem, 1)
                nc.vector.tensor_scalar(m.a_neg[:, :], m.a_neg[:, :], -1.0, None, ALU.mult)
                dve.wait_ge(s["z_hi"].sem, 1)
                nc.vector.tensor_tensor(m.wz_lo[:, :], ps[:, 2, 0:ZW + NH], m.wz_hi[:, :].bitcast(F32),
                                        ALU.subtract)
                dve.wait_ge(s["taps_hi"].sem, 1)
                nc.vector.tensor_tensor(m.wc_lo[:, :], ps[:, 3:3 + CB, :], m.wc_hi[:, :].bitcast(F32),
                                        ALU.subtract)
                dve.wait_ge(s["wout_ps"].sem, 1)
                dve.wait_ge(s["cols"].sem, 1)
                for b in range(DI // P):
                    c = BLOCKS + CB + b
                    nc.vector.tensor_scalar(m.wout[:, b, :], ps[:, 7, b * P:(b + 1) * P],
                                            m.cols[:, c:c + 1], None, ALU.mult)
                dve.wait_ge(s["sb2_ps"].sem, 1)
                nc.vector.tensor_scalar(m.half_sb2[:, :], ps[:, 0, 0:1], 0.5, None, ALU.mult)
                dve.wait_ge(s["w2_hi"].sem, 1)
                nc.vector.tensor_tensor(m.w2_lo[:, :], w2_raw[:, :], m.w2_hi[:, :].bitcast(F32), ALU.subtract)
                dve.wait_ge(s["w1_hi"].sem, 1)
                nc.vector.tensor_tensor(m.w1_lo[:, :], w1_raw[:, :], m.w1_hi[:, :].bitcast(F32), ALU.subtract)


def router_phase(nc, m, phase):
    with ExitStack() as ctx:
        def sb(name, shape, dt=F32):
            return ctx.enter_context(nc.sbuf_tensor(f"{phase}_{name}", shape, dt))

        def bank(name):
            return ctx.enter_context(nc.psum_tensor(f"{phase}_{name}", [P, 512], F32))

        stats = sb("stats", [P, TPB, 6])
        moments = sb("moments", [P, TPB, 2])
        var_eps = sb("var_eps", [P, TPB])
        rstd = sb("rstd", [P, TPB])
        xn = sb("xn", [P, TPB, D])
        xT = sb("xT", [P, SEQ])
        logits = sb("logits", [P, TPB, E])
        peak = sb("peak", [P, TPB])
        probs = sb("probs", [P, TPB, E])
        top = sb("top", [P, TPB, TOPK])
        rest = sb("rest", [P, TPB, E])
        top_sum = sb("top_sum", [P, TPB])
        top_inv = sb("top_inv", [P, TPB])
        cwq = sb("cwq", [P, TPB, 4, 32])
        xnT_ps, logit_ps, cwT_ps = bank("xnT_ps"), bank("logit_ps"), bank("cwT_ps")
        s = Signals(nc, ctx, phase, [
            "dve_held", "pool_held", "zeroed", "stats", "moments", "var_eps", "rstd", "xn", "xT", "logits_ps", "peak",
            "shifted", "probs", "top", "rest", "top_sum", "top_inv", "top_probs", "cwq"],
            {"xnT_ps": 1, "xn_hi": 1, "logits": 1, "cwT_ps": 1, "cwT": 1})

        def cols_of(c):
            return bass.ts(c, SEQ)

        with nc.Block() as block:
            @block.tensor
            def _(pe):
                def norm_and_logits(c):
                    pe.wait_ge(*done(s["xn_hi"], c - 1))
                    pe.wait_ge(*done(s["xn"], c))
                    for t in range(TPB):
                        last = nc.tensor.transpose(xnT_ps[:, t * P:(t + 1) * P], xn[:, t, :], m.ident[:, :])
                    last.then_inc(s["xnT_ps"].sem, 1)
                    pe.wait_ge(*done(s["logits"], c - 1))
                    pe.wait_ge(*done(s["xT"], c))
                    for t in range(TPB):
                        last = nc.tensor.matmul(logit_ps[:, t * E:(t + 1) * E], xT[:, t * P:(t + 1) * P],
                                                m.router_w[:, :], start=True, stop=True)
                    last.then_inc(s["logits_ps"].sem, 1)

                def weights_out(c):
                    pe.wait_ge(*done(s["cwT"], c - 1))
                    pe.wait_ge(*done(s["cwq"], c))
                    for t in range(TPB):
                        last = nc.tensor.transpose(cwT_ps[:, t * P:(t + 1) * P],
                                                   cwq[:, t, :, :].rearrange("p q j -> p (q j)"),
                                                   m.ident[:, :])
                    last.then_inc(s["cwT_ps"].sem, 1)

                norm_and_logits(0)
                with pe.Fori(0, BATCHES - 1) as c:
                    norm_and_logits(c + 1)
                    weights_out(c)
                weights_out(BATCHES - 1)

            @block.scalar
            def _(act):
                nc.scalar.preload_act_table(ACT.Exp)

                def norm_and_logits(c):
                    act.wait_ge(*done(s["xnT_ps"], c))
                    nc.scalar.activation(xT[:, :], xnT_ps[:, :], ACT.Copy).then_inc(s["xT"].sem, 1)
                    nc.scalar.activation(m.xn_hi[:, cols_of(c)], xnT_ps[:, :], ACT.Copy
                                         ).then_inc(s["xn_hi"].sem, 1)

                def weights_out(c):
                    act.wait_ge(*done(s["shifted"], c))
                    nc.scalar.activation(probs[:, :, :], logits[:, :, :], ACT.Exp).then_inc(s["probs"].sem, 1)
                    act.wait_ge(*done(s["cwT_ps"], c))
                    nc.scalar.activation(m.cwT[:, cols_of(c)], cwT_ps[:, :], ACT.Copy
                                         ).then_inc(s["cwT"].sem, 1)

                norm_and_logits(0)
                with act.Fori(0, BATCHES - 1) as c:
                    norm_and_logits(c + 1)
                    weights_out(c)
                weights_out(BATCHES - 1)

            @block.vector
            def _(dve):
                def norm_and_logits(c):
                    for t in range(TPB):
                        last = nc.vector.bn_stats(stats[:, t, :], m.x[:, bass.ds(c * SEQ + t * D, D)])
                    last.then_inc(s["stats"].sem, 1)
                    dve.wait_ge(*done(s["stats"], c))
                    dve.sem_inc(s["dve_held"].sem, 1)
                    for t in range(TPB):
                        last = nc.vector.bn_aggr(moments[:, t, :], stats[:, t, :])
                    last.then_inc(s["moments"].sem, 1)
                    dve.wait_ge(*done(s["xnT_ps"], c - 1))
                    dve.wait_ge(*done(s["rstd"], c))
                    for t in range(TPB):
                        last = nc.vector.tensor_scalar(xn[:, t, :], m.x[:, bass.ds(c * SEQ + t * D, D)],
                                                       moments[:, t, 0:1], rstd[:, t:t + 1],
                                                       ALU.subtract, ALU.mult)
                    last.then_inc(s["xn"].sem, 1)

                def weights_out(c):
                    dve.wait_ge(*done(s["logits_ps"], c))
                    nc.vector.tensor_tensor(logits[:, :, :],
                                            logit_ps[:, 0:TPB * E].rearrange("p (t e) -> p t e", e=E),
                                            m.rows[:, 0:E].unsqueeze(1).to_broadcast([P, TPB, E]), ALU.add
                                            ).then_inc(s["logits"].sem, 1)
                    dve.wait_ge(*done(s["logits"], c))
                    nc.vector.tensor_reduce(peak[:, :], logits[:, :, :], AX.X, ALU.max
                                            ).then_inc(s["peak"].sem, 1)
                    dve.wait_ge(*done(s["probs"], c))
                    dve.sem_inc(s["dve_held"].sem, 1)
                    for t in range(TPB):
                        last = nc.vector.max(top[:, t, :], probs[:, t, :])
                    last.then_inc(s["top"].sem, 1)
                    dve.wait_ge(*done(s["top"], c))
                    dve.sem_inc(s["dve_held"].sem, 1)
                    for t in range(TPB):
                        last = nc.vector.match_replace(rest[:, t, :], top[:, t, :], probs[:, t, :], 0.0)
                    last.then_inc(s["rest"].sem, 1)
                    nc.vector.tensor_reduce(top_sum[:, :], top[:, :, :], AX.X, ALU.add
                                            ).then_inc(s["top_sum"].sem, 1)
                    dve.wait_ge(*done(s["top_sum"], c))
                    nc.vector.reciprocal(top_inv[:, :], top_sum[:, :]).then_inc(s["top_inv"].sem, 1)

                norm_and_logits(0)
                with dve.Fori(0, BATCHES - 1) as c:
                    norm_and_logits(c + 1)
                    weights_out(c)
                weights_out(BATCHES - 1)

            @block.gpsimd
            def _(pool):
                s.give_credits(pool)
                nc.gpsimd.memset(cwq[:, :, :, :], 0.0).then_inc(s["zeroed"].sem, 1)
                pool.wait_ge(s["zeroed"].sem, 1)

                def norm_and_logits(c):
                    pool.wait_ge(*done(s["moments"], c))
                    pool.sem_inc(s["pool_held"].sem, 1)
                    nc.gpsimd.tensor_scalar(var_eps[:, :], moments[:, :, 1], 1.0, EPS, ALU.mult, ALU.add
                                            ).then_inc(s["var_eps"].sem, 1)
                    pool.wait_ge(*done(s["var_eps"], c))
                    nc.gpsimd.tensor_tensor(rstd[:, :], var_eps[:, :], m.minus_half[:, 0:TPB], ALU.pow
                                            ).then_inc(s["rstd"].sem, 1)
                    pool.wait_ge(*done(s["xn_hi"], c))
                    nc.gpsimd.tensor_tensor(m.xn_lo[:, cols_of(c)], xT[:, :],
                                            m.xn_hi[:, cols_of(c)].bitcast(F32), ALU.subtract)

                def weights_out(c):
                    pool.wait_ge(*done(s["peak"], c))
                    nc.gpsimd.tensor_tensor(logits[:, :, :], logits[:, :, :],
                                            peak[:, :].unsqueeze(2).to_broadcast([P, TPB, E]), ALU.subtract
                                            ).then_inc(s["shifted"].sem, 1)
                    pool.wait_ge(*done(s["rest"], c))
                    nc.gpsimd.tensor_tensor(probs[:, :, :], probs[:, :, :], rest[:, :, :], ALU.subtract
                                            ).then_inc(s["top_probs"].sem, 1)
                    pool.wait_ge(*done(s["top_inv"], c))
                    pool.wait_ge(*done(s["cwT_ps"], c - 1))
                    pool.wait_ge(*done(s["top_probs"], c))
                    for t in range(TPB):
                        last = nc.gpsimd.tensor_tensor(
                            cwq[:, t, :, 0:E // 4], probs[:, t, :].rearrange("p (j q) -> p q j", q=4),
                            top_inv[:, t:t + 1].unsqueeze(2).to_broadcast([P, 4, E // 4]), ALU.mult)
                    last.then_inc(s["cwq"].sem, 1)

                norm_and_logits(0)
                with pool.Fori(0, BATCHES - 1) as c:
                    norm_and_logits(c + 1)
                    weights_out(c)
                weights_out(BATCHES - 1)


FILLS = 2 + CB
SHARED_USES = [("pre", 0), ("pre", 1), ("pre", 2), ("post", 0), ("pre", 3), ("post", 1), ("post", 2),
               ("post", 3)]
USES = len(SHARED_USES)


def ssm_phase(nc, m):
    with ExitStack() as ctx:
        def sb(name, shape, dt=F32):
            return ctx.enter_context(nc.sbuf_tensor(f"ssm_{name}", shape, dt))

        def bank(name):
            return ctx.enter_context(nc.psum_tensor(f"ssm_{name}", [P, 512], F32))

        pad = TAPS
        stats = sb("stats", [P, TPB, 6])
        moments = sb("moments", [P, TPB, 2])
        var_eps = sb("var_eps", [P, TPB])
        rstd = sb("rstd", [P, TPB])
        xn = sb("xn", [P, TPB, D])
        xT_hi = sb("xT_hi", [P, pad + SEQ], F32R)
        xT_lo = sb("xT_lo", [P, pad + SEQ], F32R)
        gate = sb("gate", [P, 2, TPB, DI])
        chan = sb("chan", [P, 2, CB, SEQ])
        dt_raw = sb("dt_raw", [P, 2, TPB * NH])
        neg_abs = sb("neg_abs", [P, TPB * NH])
        exp_na = sb("exp_na", [P, TPB * NH])
        u = sb("u", [P, TPB * NH])
        u_err = sb("u_err", [P, TPB * NH])
        u_inv = sb("u_inv", [P, TPB * NH])
        ln_u = sb("ln_u", [P, TPB * NH])
        dt = sb("dt", [P, TPB, NH])
        dA = sb("dA", [P, TPB, NH])
        decay = sb("decay", [P, 3, TPB, NH])
        dt_after = sb("dt_after", [P, TPB, NH])
        seg_rhs = sb("seg_rhs", [P, 2, NH, P])
        seg = sb("seg", [P, TPB, NH, P])
        cb_mask = sb("cb_mask", [P, 2, P])
        mix = sb("mix", [P, 2, NH, P])
        tok = sb("tok", [P, 2, DI + NS])
        dx = sb("dx", [P, 2, DI])
        dx_after = sb("dx_after", [P, 2, DI])
        skip = sb("skip", [P, 2, DI])
        y_in = sb("y_in", [P, DI])
        y = sb("y", [P, 2, DI])
        square = sb("square", [P, DI])
        sum_sq = sb("sum_sq", [P, 2])
        mean_sq = sb("mean_sq", [P, 2])
        inv_rms = sb("inv_rms", [P, 2])
        yT = sb("yT", [P, 2, DI])
        state = sb("state", [P, 2, DI])
        state_dec = sb("state_dec", [P, DI])

        front_ps = bank("front_ps")
        fill_ps = [bank("fill0_ps"), bank("fill1_ps")]
        seg_ps = bank("seg_ps")
        cb_ps = bank("cb_ps")
        tok_ps = bank("tok_ps")
        y_ps = bank("y_ps")
        state_ps = bank("state_ps")

        s = Signals(nc, ctx, "ssm", [
            "dve_held", "pool_held", "padded", "stats", "moments", "var_eps", "rstd", "xn", "xT_hi", "xT_lo",
            "dt_ps", "filled", "neg_abs", "exp_na", "ln_u", "u", "u_inv", "u_fix", "ln1p", "dt", "dA",
            "decay_ps", "decay", "dt_after", "seg_rhs", "seg", "tok", "cb_ready", "tok_ready",
            "dx", "dx_after", "y_ready", "y_sum", "yg", "state_ready", "state_dec",
            "mean_sq", "inv_rms", "out_ready"],
            {"xnT_ps": 1, "dt_raw": 1, "filled_read": 2, "sum_sq": 1, "skip": 2, "seg_ps": 2, "mix": TPB, "cb_read": 1,
             "tok_read": 1, "y_read": 2, "state": 1})

        def use_of(kind, t):
            return SHARED_USES.index((kind, t))

        def heads(ap):
            return ap.unsqueeze(2).to_broadcast([P, NH, HD])

        def by_head(ap):
            return ap.rearrange("p (h d) -> p h d", h=NH)

        def x_of(b, t):
            return m.x[:, bass.ds(b * SEQ + t * D, D)]

        def schedule(front, back):
            def run(eng):
                front(0, 0, None)
                with eng.Fori(0, BATCHES - 2, 2) as b:
                    back(b, 0, lambda fill: front(b + 1, 1, fill))
                    back(b + 1, 1, lambda fill: front(b + 2, 0, fill))
                back(BATCHES - 2, 0, lambda fill: front(BATCHES - 1, 1, fill))
                back(BATCHES - 1, 1, None)
            return run

        with nc.Block() as block:
            @block.tensor
            def _(pe):
                def head(b, q):
                    pe.wait_ge(*done(s["dt_raw"], b - 1))
                    pe.wait_ge(*done(s["xn"], b))
                    for t in range(TPB):
                        last = nc.tensor.transpose(front_ps[:, t * P:(t + 1) * P], xn[:, t, :], m.ident[:, :])
                    last.then_inc(s["xnT_ps"].sem, 1)
                    pe.wait_ge(*done(s["xT_lo"], b))
                    for t in range(TPB):
                        c = slice(pad + t * P, pad + (t + 1) * P)
                        o = front_ps[:, t * NH:(t + 1) * NH]
                        nc.tensor.matmul(o, xT_hi[:, c], m.wz_hi[:, ZW:], start=True, stop=False)
                        nc.tensor.matmul(o, xT_lo[:, c], m.wz_hi[:, ZW:], start=False, stop=False)
                        last = nc.tensor.matmul(o, xT_hi[:, c], m.wz_lo[:, ZW:], start=False, stop=True)
                    last.then_inc(s["dt_ps"].sem, 1)

                def fill(b, q, f):
                    pe.wait_ge(*done(s["filled_read"], b * FILLS + (f - 2)))
                    o = fill_ps[f % 2]
                    if f < 2:
                        for i in range(2):
                            t = 2 * f + i
                            c = slice(pad + t * P, pad + (t + 1) * P)
                            oi = o[:, i * ZW:(i + 1) * ZW]
                            nc.tensor.matmul(oi, xT_hi[:, c], m.wz_hi[:, 0:ZW], start=True, stop=False)
                            nc.tensor.matmul(oi, xT_lo[:, c], m.wz_hi[:, 0:ZW], start=False, stop=False)
                            last = nc.tensor.matmul(oi, xT_hi[:, c], m.wz_lo[:, 0:ZW], start=False, stop=True)
                    else:
                        for k in range(TAPS):
                            w = slice(((f - 2) * TAPS + k) * P, ((f - 2) * TAPS + k + 1) * P)
                            c = slice(pad - (TAPS - 1) + k, pad - (TAPS - 1) + k + SEQ)
                            nc.tensor.matmul(o[:, :], m.wc_hi[:, w], xT_hi[:, c], start=k == 0, stop=False)
                            nc.tensor.matmul(o[:, :], m.wc_hi[:, w], xT_lo[:, c], start=False, stop=False)
                            last = nc.tensor.matmul(o[:, :], m.wc_lo[:, w], xT_hi[:, c], start=False,
                                                    stop=k == TAPS - 1)
                    last.then_inc(s["filled"].sem, 1)

                def segments(b, q):
                    pe.wait_ge(*done(s["seg"], b * TPB - 1)) if not isinstance(b, int) or b else None
                    pe.wait_ge(*done(s["dA"], b))
                    dA16 = dA[:, :, :].rearrange("p t h -> p (t h)")
                    for i, w in enumerate((m.upto, m.after, m.ones)):
                        last = nc.tensor.matmul(seg_ps[:, i * 16:(i + 1) * 16], w[:, :], dA16,
                                                start=True, stop=True)
                    last.then_inc(s["decay_ps"].sem, 1)
                    for t in range(TPB):
                        if t == 0:
                            pe.wait_ge(*done(s["decay"], b))
                        else:
                            pe.wait_ge(*done(s["seg"], b * TPB + (t - 1)))
                        pe.wait_ge(*done(s["seg_rhs"], b * TPB + t))
                        nc.tensor.matmul(seg_ps[:, :], m.after[:, :],
                                         seg_rhs[:, t % 2, :, :].rearrange("p h t -> p (h t)"),
                                         start=True, stop=True).then_inc(s["seg_ps"].sem, 1)

                def pre(b, q, t):
                    c = slice(t * P, (t + 1) * P)
                    pe.wait_ge(*done(s["cb_read"], b * USES + (use_of("pre", t) - 1)))
                    pe.wait_ge(*done(s["filled_read"], b * FILLS + (FILLS - 1)))
                    nc.tensor.matmul(cb_ps[:, 0:P], chan[:, q, 2, c], chan[:, q, 3, c], start=True, stop=True
                                     ).then_inc(s["cb_ready"].sem, 1)
                    pe.wait_ge(*done(s["tok_read"], b * USES + (use_of("pre", t) - 1)))
                    for i in range(3):
                        last = nc.tensor.transpose(tok_ps[:, i * P:(i + 1) * P], chan[:, q, i, c],
                                                   m.ident[:, :])
                    last.then_inc(s["tok_ready"].sem, 1)

                def main(b, q, t):
                    c = slice(t * P, (t + 1) * P)
                    n = b * TPB + t
                    if t < TPB - 1:
                        pe.wait_ge(*done(s["state"], b * (TPB - 1) + (t - 1)))
                        pe.wait_ge(*done(s["dx_after"], b * (TPB - 1) + t))
                        nc.tensor.matmul(state_ps[:, 0:DI], tok[:, t % 2, DI:], dx_after[:, t % 2, :],
                                         start=True, stop=True).then_inc(s["state_ready"].sem, 1)
                    pe.wait_ge(*done(s["y_read"], n - 1))
                    if t:
                        pe.wait_ge(*done(s["state"], b * (TPB - 1) + (t - 1)))
                        nc.tensor.matmul(y_ps[:, DI:], chan[:, q, 3, c], state[:, (t - 1) % 2, :],
                                         start=True, stop=True)
                    pe.wait_ge(*done(s["dx"], n))
                    pe.wait_ge(*done(s["mix"], n))
                    for h in range(NH):
                        last = nc.tensor.matmul(y_ps[:, h * HD:(h + 1) * HD], mix[:, t % 2, h, :],
                                                dx[:, t % 2, h * HD:(h + 1) * HD], start=True, stop=True)
                    last.then_inc(s["y_ready"].sem, 1)

                def post(b, q, t):
                    pe.wait_ge(*done(s["tok_read"], b * USES + (use_of("post", t) - 1)))
                    pe.wait_ge(*done(s["yg"], b * TPB + t))
                    for i in range(DI // P):
                        last = nc.tensor.transpose(tok_ps[:, i * P:(i + 1) * P],
                                                   y[:, t % 2, i * P:(i + 1) * P], m.ident[:, :])
                    last.then_inc(s["tok_ready"].sem, 1)
                    pe.wait_ge(*done(s["cb_read"], b * USES + (use_of("post", t) - 1)))
                    pe.wait_ge(*done(s["tok_read"], b * USES + use_of("post", t)))
                    for i in range(DI // P):
                        last = nc.tensor.matmul(cb_ps[:, 0:D], yT[:, t % 2, i * P:(i + 1) * P],
                                                m.wout[:, i, :], start=i == 0, stop=i == DI // P - 1)
                    last.then_inc(s["cb_ready"].sem, 1)

                def front(b, q, f):
                    if f is None or f == "head":
                        head(b, q)
                    if f is None:
                        for i in range(FILLS):
                            fill(b, q, i)
                    elif f != "head":
                        fill(b, q, f)

                def back(b, q, beside):
                    if beside:
                        beside("head")
                    segments(b, q)
                    for step in range(TPB + 2):
                        if step < TPB:
                            pre(b, q, step)
                        if beside:
                            beside(step)
                        if 1 <= step <= TPB:
                            main(b, q, step - 1)
                        if step >= 2:
                            post(b, q, step - 2)

                schedule(front, back)(pe)

            @block.scalar
            def _(act):
                def front(b, q, f):
                    if f is None or f == "head":
                        act.wait_ge(*done(s["xnT_ps"], b))
                        nc.scalar.activation(xT_hi[:, pad:], front_ps[:, :], ACT.Copy
                                             ).then_inc(s["xT_hi"].sem, 1)
                    for i in range(FILLS) if f is None else () if f == "head" else (f,):
                        act.wait_ge(*done(s["filled"], b * FILLS + i))
                        if i < 2:
                            nc.scalar.activation(gate[:, q, 2 * i:2 * i + 2, :].rearrange("p t c -> p (t c)"),
                                                 fill_ps[i % 2][:, :], ACT.Silu
                                                 ).then_inc(s["filled_read"].sem, 1)
                        else:
                            c = BLOCKS + i - 2
                            nc.scalar.activation(chan[:, q, i - 2, :], fill_ps[i % 2][:, :], ACT.Silu,
                                                 bias=m.cols[:, c:c + 1]).then_inc(s["filled_read"].sem, 1)

                def back(b, q, beside):
                    if beside:
                        beside("head")
                    act.wait_ge(*done(s["neg_abs"], b))
                    nc.scalar.activation(exp_na[:, :], neg_abs[:, :], ACT.Exp).then_inc(s["exp_na"].sem, 1)
                    act.wait_ge(*done(s["exp_na"], b))
                    nc.scalar.activation(ln_u[:, :], exp_na[:, :], ACT.Ln, bias=1.0
                                         ).then_inc(s["ln_u"].sem, 1)
                    act.wait_ge(*done(s["decay_ps"], b))
                    nc.scalar.activation(decay[:, :, :, :].rearrange("p i t h -> p (i t h)"),
                                         seg_ps[:, 0:3 * TPB * NH], ACT.Exp).then_inc(s["decay"].sem, 1)
                    for t in range(TPB):
                        act.wait_ge(*done(s["mix"], (b - 1) * TPB + t))
                        act.wait_ge(*done(s["seg_ps"], b * TPB + t))
                        nc.scalar.activation(seg[:, t, :, :].rearrange("p h t -> p (h t)"), seg_ps[:, :],
                                             ACT.Exp).then_inc(s["seg"].sem, 1)
                    for step in range(TPB + 2):
                        if step < TPB:
                            act.wait_ge(*done(s["skip"], b * TPB + (step - 2)))
                            act.wait_ge(*done(s["tok_ready"], b * USES + use_of("pre", step)))
                            nc.scalar.activation(tok[:, step % 2, :], tok_ps[:, 0:DI + NS], ACT.Copy
                                                 ).then_inc(s["tok_read"].sem, 1)
                        if beside:
                            beside(step)
                        if step >= 2:
                            t = step - 2
                            act.wait_ge(*done(s["tok_ready"], b * USES + use_of("post", t)))
                            nc.scalar.activation(yT[:, t % 2, :], tok_ps[:, 0:DI], ACT.Copy
                                                 ).then_inc(s["tok_read"].sem, 1)
                            act.wait_ge(*done(s["sum_sq"], b * TPB + (t - 1)))
                            nc.scalar.activation(square[:, :], y[:, t % 2, :], ACT.Square,
                                                 accum_out=sum_sq[:, t % 2:t % 2 + 1]
                                                 ).then_inc(s["sum_sq"].sem, 1)

                schedule(front, back)(act)

            @block.vector
            def _(dve):
                def front(b, q, f):
                    if f is not None and f != "head":
                        return
                    for t in range(TPB):
                        last = nc.vector.bn_stats(stats[:, t, :], x_of(b, t))
                    last.then_inc(s["stats"].sem, 1)
                    dve.wait_ge(*done(s["stats"], b))
                    dve.sem_inc(s["dve_held"].sem, 1)
                    for t in range(TPB):
                        last = nc.vector.bn_aggr(moments[:, t, :], stats[:, t, :])
                    last.then_inc(s["moments"].sem, 1)
                    dve.wait_ge(*done(s["xnT_ps"], b - 1))
                    dve.wait_ge(*done(s["rstd"], b))
                    for t in range(TPB):
                        last = nc.vector.tensor_scalar(xn[:, t, :], x_of(b, t), moments[:, t, 0:1],
                                                       rstd[:, t:t + 1], ALU.subtract, ALU.mult)
                    last.then_inc(s["xn"].sem, 1)
                    dve.wait_ge(*done(s["xT_hi"], b))
                    nc.vector.tensor_tensor(xT_lo[:, pad:], front_ps[:, :], xT_hi[:, pad:].bitcast(F32),
                                            ALU.subtract).then_inc(s["xT_lo"].sem, 1)
                    dve.wait_ge(*done(s["dt_ps"], b))
                    nc.vector.tensor_tensor(
                        dt_raw[:, q, :].rearrange("p (t h) -> p t h", h=NH),
                        front_ps[:, 0:TPB * NH].rearrange("p (t h) -> p t h", h=NH),
                        m.rows[:, E:E + NH].unsqueeze(1).to_broadcast([P, TPB, NH]), ALU.add
                        ).then_inc(s["dt_raw"].sem, 1)

                def time_steps(b, q):
                    dve.wait_ge(*done(s["dt_raw"], b))
                    nc.vector.scalar_tensor_tensor(neg_abs[:, :], dt_raw[:, q, :], -1.0, dt_raw[:, q, :],
                                                   ALU.mult, ALU.min).then_inc(s["neg_abs"].sem, 1)
                    dve.wait_ge(*done(s["exp_na"], b))
                    nc.vector.tensor_scalar(u[:, :], exp_na[:, :], 1.0, None, ALU.add
                                            ).then_inc(s["u"].sem, 1)
                    dve.wait_ge(*done(s["u"], b))
                    nc.vector.scalar_tensor_tensor(u_err[:, :], u[:, :], 1.0, exp_na[:, :],
                                                   ALU.subtract, ALU.subtract)
                    nc.vector.reciprocal(u_inv[:, :], u[:, :]).then_inc(s["u_inv"].sem, 1)
                    dve.wait_ge(*done(s["u_inv"], b))
                    nc.vector.tensor_tensor(u_err[:, :], u_err[:, :], u_inv[:, :], ALU.mult
                                            ).then_inc(s["u_fix"].sem, 1)
                    dve.wait_ge(*done(s["u_fix"], b))
                    dve.wait_ge(*done(s["ln_u"], b))
                    nc.vector.tensor_tensor(ln_u[:, :], ln_u[:, :], u_err[:, :], ALU.subtract
                                            ).then_inc(s["ln1p"].sem, 1)
                    dve.wait_ge(*done(s["ln1p"], b))
                    nc.vector.scalar_tensor_tensor(dt[:, :, :].rearrange("p t h -> p (t h)"),
                                                   dt_raw[:, q, :], 0.0, ln_u[:, :], ALU.max, ALU.add
                                                   ).then_inc(s["dt"].sem, 1)
                    dve.wait_ge(*done(s["dt"], b))
                    nc.vector.tensor_tensor(dA[:, :, :], dt[:, :, :],
                                            m.a_neg[:, :].unsqueeze(1).to_broadcast([P, TPB, NH]), ALU.mult
                                            ).then_inc(s["dA"].sem, 1)

                def pre(b, q, t):
                    n = b * TPB + t
                    dve.wait_ge(*done(s["cb_ready"], b * USES + use_of("pre", t)))
                    nc.vector.tensor_tensor(cb_mask[:, t % 2, :], cb_ps[:, 0:P], m.upto[:, :], ALU.mult
                                            ).then_inc(s["cb_read"].sem, 1)
                    dve.wait_ge(*done(s["cb_read"], b * USES + use_of("pre", t)))
                    dve.wait_ge(*done(s["seg"], n))
                    nc.vector.tensor_tensor(mix[:, t % 2, :, :], seg[:, t, :, :],
                                            cb_mask[:, t % 2, :].unsqueeze(1).to_broadcast([P, NH, P]),
                                            ALU.mult).then_inc(s["mix"].sem, 1)

                def main(b, q, t):
                    n = b * TPB + t
                    if t < TPB - 1:
                        i = b * (TPB - 1) + t
                        dve.wait_ge(*done(s["state_ready"], i))
                        if t == 0:
                            nc.vector.tensor_copy(state[:, t % 2, :], state_ps[:, 0:DI]
                                                  ).then_inc(s["state"].sem, 1)
                        else:
                            dve.wait_ge(*done(s["state_dec"], b * (TPB - 2) + (t - 1)))
                            nc.vector.tensor_tensor(state[:, t % 2, :], state_dec[:, :], state_ps[:, 0:DI],
                                                    ALU.add).then_inc(s["state"].sem, 1)
                    dve.wait_ge(*done(s["y_ready"], n))
                    if t:
                        nc.vector.tensor_tensor(by_head(y_in[:, :]), by_head(y_ps[:, DI:]),
                                                heads(decay[:, 0, t, :]), ALU.mult)
                    dve.wait_ge(*done(s["skip"], n))
                    nc.vector.tensor_tensor(y[:, t % 2, :], skip[:, t % 2, :], y_ps[:, 0:DI], ALU.add
                                            ).then_inc(s["y_read"].sem, 1)
                    dve.wait_ge(*done(s["y_read"], n))
                    if t:
                        nc.vector.tensor_tensor(y[:, t % 2, :], y[:, t % 2, :], y_in[:, :], ALU.add
                                                ).then_inc(s["y_sum"].sem, 1)
                        dve.wait_ge(*done(s["y_sum"], b * (TPB - 1) + (t - 1)))
                    nc.vector.tensor_tensor(y[:, t % 2, :], y[:, t % 2, :], gate[:, q, t, :], ALU.mult
                                            ).then_inc(s["yg"].sem, 1)

                def post(b, q, t):
                    n = b * TPB + t
                    dve.wait_ge(*done(s["inv_rms"], n))
                    dve.wait_ge(*done(s["cb_ready"], b * USES + use_of("post", t)))
                    nc.vector.scalar_tensor_tensor(x_of(b, t), cb_ps[:, 0:D], inv_rms[:, t % 2:t % 2 + 1],
                                                   x_of(b, t), ALU.mult, ALU.add
                                                   ).then_inc(s["cb_read"].sem, 1)

                def back(b, q, beside):
                    if beside:
                        beside("head")
                    time_steps(b, q)
                    for step in range(TPB + 2):
                        if step < TPB:
                            pre(b, q, step)
                        if 1 <= step <= TPB:
                            main(b, q, step - 1)
                        if step >= 2:
                            post(b, q, step - 2)

                schedule(front, back)(dve)

            @block.gpsimd
            def _(pool):
                s.give_credits(pool)
                nc.gpsimd.memset(xT_hi[:, 0:pad].bitcast(F32), 0.0)
                nc.gpsimd.memset(xT_lo[:, 0:pad].bitcast(F32), 0.0).then_inc(s["padded"].sem, 1)
                pool.wait_ge(s["padded"].sem, 1)

                def front(b, q, f):
                    if f is not None and f != "head":
                        return
                    pool.wait_ge(*done(s["moments"], b))
                    pool.sem_inc(s["pool_held"].sem, 1)
                    nc.gpsimd.tensor_scalar(var_eps[:, :], moments[:, :, 1], 1.0, EPS, ALU.mult, ALU.add
                                            ).then_inc(s["var_eps"].sem, 1)
                    pool.wait_ge(*done(s["var_eps"], b))
                    nc.gpsimd.tensor_tensor(rstd[:, :], var_eps[:, :], m.minus_half[:, 0:TPB], ALU.pow
                                            ).then_inc(s["rstd"].sem, 1)

                def segments(b, q):
                    pool.wait_ge(*done(s["dA"], b))
                    for t in range(TPB):
                        pool.wait_ge(*done(s["seg_ps"], b * TPB + (t - 2)))
                        nc.gpsimd.tensor_tensor(seg_rhs[:, t % 2, :, :],
                                                dA[:, t, :].unsqueeze(2).to_broadcast([P, NH, P]),
                                                m.upto[:, :].unsqueeze(1).to_broadcast([P, NH, P]), ALU.mult
                                                ).then_inc(s["seg_rhs"].sem, 1)
                    pool.wait_ge(*done(s["decay"], b))
                    nc.gpsimd.tensor_tensor(dt_after[:, :, :], dt[:, :, :], decay[:, 1, :, :], ALU.mult
                                            ).then_inc(s["dt_after"].sem, 1)
                    pool.wait_ge(*done(s["dt_after"], b))

                def pre(b, q, t):
                    n = b * TPB + t
                    x_tok = by_head(tok[:, t % 2, 0:DI])
                    pool.wait_ge(*done(s["tok_read"], b * USES + use_of("pre", t)))
                    if t < TPB - 1:
                        nc.gpsimd.tensor_tensor(by_head(dx_after[:, t % 2, :]), x_tok,
                                                heads(dt_after[:, t, :]), ALU.mult
                                                ).then_inc(s["dx_after"].sem, 1)
                    nc.gpsimd.tensor_tensor(by_head(dx[:, t % 2, :]), x_tok, heads(dt[:, t, :]), ALU.mult
                                            ).then_inc(s["dx"].sem, 1)
                    pool.wait_ge(*done(s["y_read"], n - 2))
                    nc.gpsimd.tensor_tensor(by_head(skip[:, t % 2, :]), x_tok,
                                            heads(m.rows[:, E + 2 * NH:E + 3 * NH]), ALU.mult
                                            ).then_inc(s["skip"].sem, 1)

                def main(b, q, t):
                    if 1 <= t < TPB - 1:
                        pool.wait_ge(*done(s["state"], b * (TPB - 1) + (t - 1)))
                        nc.gpsimd.tensor_tensor(by_head(state_dec[:, :]), by_head(state[:, (t - 1) % 2, :]),
                                                heads(decay[:, 2, t, :]), ALU.mult
                                                ).then_inc(s["state_dec"].sem, 1)

                def post(b, q, t):
                    n = b * TPB + t
                    pool.wait_ge(*done(s["sum_sq"], n))
                    pool.sem_inc(s["pool_held"].sem, 1)
                    i = slice(t % 2, t % 2 + 1)
                    nc.gpsimd.tensor_scalar(mean_sq[:, i], sum_sq[:, i], 1.0 / DI, EPS, ALU.mult, ALU.add
                                            ).then_inc(s["mean_sq"].sem, 1)
                    pool.wait_ge(*done(s["mean_sq"], n))
                    nc.gpsimd.tensor_tensor(inv_rms[:, i], mean_sq[:, i], m.minus_half[:, 0:1], ALU.pow
                                            ).then_inc(s["inv_rms"].sem, 1)

                def back(b, q, beside):
                    if beside:
                        beside("head")
                    segments(b, q)
                    for step in range(TPB + 2):
                        if step < TPB:
                            pre(b, q, step)
                        if 1 <= step <= TPB:
                            main(b, q, step - 1)
                        if step >= 2:
                            post(b, q, step - 2)

                schedule(front, back)(pool)


def program(nc, arrays, out):
    with ExitStack() as ctx:
        m = Tensors()

        def sb(name, shape, dt=F32):
            return ctx.enter_context(nc.sbuf_tensor(name, shape, dt))

        m.x = sb("x_res", [P, TOKENS // P * D])
        m.xn_hi, m.xn_lo = sb("xn_hi", [P, TOKENS], F32R), sb("xn_lo", [P, TOKENS], F32R)
        m.cwT = sb("cwT", [P, TOKENS])
        m.w1_hi, m.w1_lo = sb("w1_hi", [P, BLOCKS * P], F32R), sb("w1_lo", [P, BLOCKS * P], F32R)
        m.w2_hi, m.w2_lo = sb("w2_hi", [P, BLOCKS * P], F32R), sb("w2_lo", [P, BLOCKS * P], F32R)
        m.wz_hi, m.wz_lo = sb("wz_hi", [P, ZW + NH], F32R), sb("wz_lo", [P, ZW + NH], F32R)
        m.wc_hi = sb("wc_hi", [P, CB * TAPS * P], F32R)
        m.wc_lo = sb("wc_lo", [P, CB * TAPS * P], F32R)
        m.wout = sb("wout", [P, DI // P, D])
        m.router_w = sb("router_w", [P, E])
        m.cols = sb("cols", [P, N_COLS])
        m.rows = sb("rows", [P, N_ROWS])
        m.a_neg = sb("a_neg", [P, NH])
        m.b2q = sb("b2q", [P, D])
        m.half_sb2 = sb("half_sb2", [P, 1])
        m.ident, m.upto, m.after = sb("ident", [P, P]), sb("upto", [P, P]), sb("after", [P, P])
        m.ones, m.minus_half = sb("ones", [P, P]), sb("minus_half", [P, TPB])
        prepare_phase(nc, m, arrays)
        router_phase(nc, m, "router1")
        ffn_phase(nc, m, "ffn1", out)
        ssm_phase(nc, m)
        router_phase(nc, m, "router2")
        ffn_phase(nc, m, "ffn2", out)


_NAMES = {"L0_attn_u": "u", "L0_attn_W_in": "W_in", "L0_attn_conv_w": "conv_w", "L0_attn_conv_b": "conv_b",
          "L0_attn_dt_bias": "dt_bias", "L0_attn_A_log": "A_log", "L0_attn_D_param": "D_param",
          "L0_attn_norm_w": "norm_w", "L0_attn_W_out": "W_out", "L0_ffn_router_w": "router_w",
          "L0_ffn_router_b": "router_b", "L0_ffn_w1": "w1", "L0_ffn_b1": "b1", "L0_ffn_w2": "w2",
          "L0_ffn_b2": "b2", "L0_ffn_sw1": "sw1", "L0_ffn_sb1": "sb1", "L0_ffn_sw2": "sw2",
          "L0_ffn_sb2": "sb2"}


def kernel(**inputs):
    import numpy as _np
    import concourse.bacc as _bacc
    from concourse import mybir as _mybir
    from concourse.bass_utils import run_bass_kernel_spmd as _run

    nc = _bacc.Bacc("TRN2", target_bir_lowering=False, num_devices=1)
    arrays, aps = {}, {}
    for name, short in _NAMES.items():
        arr = _np.ascontiguousarray(inputs[name])
        arrays[f"in_{short}"] = arr
        aps[short] = nc.dram_tensor(f"in_{short}", arr.shape, _mybir.dt.from_np(arr.dtype),
                                    kind="ExternalInput").ap()
    out = nc.dram_tensor("out_x", (BATCHES, SEQ, D), _mybir.dt.float32, kind="ExternalOutput").ap()
    program(nc, aps, out)
    r = _run(nc, [arrays], core_ids=[0])
    return r.results[0]["out_x"]
```

```python
import numpy as np
import concourse.bass as bass
from concourse import mybir
from contextlib import ExitStack

F32 = mybir.dt.float32
F32R = mybir.dt.float32r
ALU = mybir.AluOpType
ACT = mybir.ActivationFunctionType
AX = mybir.AxisListType

P = 128
D = 128
BATCHES, SEQ = 8, 512
TOKENS = BATCHES * SEQ
TILES = TOKENS // P
TPB = SEQ // P
E, HE = 64, 32
ES, HS = 2, 256
TOPK = 8
EPS = 1e-5
ROUTED = E * HE // P
SHARED = ES * HS // P
BLOCKS = ROUTED + SHARED
EPB = P // HE
RING = 4
LAG = 3

DI = 256
NH, HD = 4, 64
NS = 128
ZW = DI
CB = (DI + 2 * NS) // P
TAPS = 4

ORDER = []
for _q in range(SHARED):
    ORDER += [("routed", _q * (ROUTED // SHARED) + _r) for _r in range(ROUTED // SHARED)]
    ORDER.append(("shared", ROUTED + _q))


class Signal:

    def __init__(self, sem, credit):
        self.sem, self.credit = sem, credit

    def at(self, n):
        return n + (1 + self.credit)


def done(signal, n):
    return signal.sem, signal.at(n)


class Signals:

    def __init__(self, nc, ctx, phase, names, credits=()):
        self.all = {}
        for name in names:
            self.all[name] = Signal(ctx.enter_context(nc.semaphore(f"{phase}_{name}")), 0)
        for name, credit in dict(credits).items():
            self.all[name] = Signal(ctx.enter_context(nc.semaphore(f"{phase}_{name}")), credit)

    def __getitem__(self, name):
        return self.all[name]

    def give_credits(self, eng):
        for s in self.all.values():
            if s.credit:
                eng.sem_inc(s.sem, s.credit)


class Tensors:
    pass


N_COLS = BLOCKS + CB + DI // P
N_ROWS = E + 3 * NH


def prepare_phase(nc, m, a):
    with ExitStack() as ctx:
        def sb(name, shape, dt=F32):
            return ctx.enter_context(nc.sbuf_tensor(f"prep_{name}", shape, dt))

        w1_raw = sb("w1_raw", [P, BLOCKS * P])
        w2_raw = sb("w2_raw", [P, BLOCKS * P])
        col_rows = sb("col_rows", [N_COLS, P])
        row_vals = sb("row_vals", [1, N_ROWS])
        sb2_rows = sb("sb2_rows", [ES, D])
        win = sb("win", [P, 2 + CB, D])
        win_dt = sb("win_dt", [NH, D])
        conv_w = sb("conv_w", [P, CB, TAPS])
        win_tap = sb("win_tap", [P, CB, TAPS, D])
        wout_raw = sb("wout_raw", [P, DI])
        sb2_sum = sb("sb2_sum", [P, 1])
        ps = ctx.enter_context(nc.psum_tensor("prep_ps", [P, 8, 512], F32))
        s = Signals(nc, ctx, "prep", [
            "x_in", "small_in", "win_in", "w1_in", "w2_in", "zeroed", "consts", "b2q_zeroed", "b2q_in",
            "cols_ps", "cols", "rows_ps", "rows", "exp_a", "sb2_ps", "sb2", "z_ps", "z_hi", "taps",
            "taps_ps", "taps_hi", "wout_ps", "w1_hi", "w2_hi"])

        with nc.Block() as block:
            @block.sync
            def _(sp):
                sp.dma_start(win[:, :, :], a["W_in"][0:(2 + CB) * P, :].rearrange("(b p) d -> p b d", p=P)
                             ).then_inc(s["win_in"].sem, 16)
                sp.dma_start(win_dt[:, :], a["W_in"][(2 + CB) * P:, :]).then_inc(s["win_in"].sem, 16)
                sp.dma_start(m.x[:, :].rearrange("p (t d) -> p t d", d=D),
                             a["u"].rearrange("b (t p) d -> p (b t) d", p=P)).then_inc(s["x_in"].sem, 16)
                sp.dma_start(w2_raw[:, 0:ROUTED * P].rearrange("p (b d) -> p b d", d=D),
                             a["w2"].rearrange("e h d -> (e h) d").rearrange("(b p) d -> p b d", p=P)
                             ).then_inc(s["w2_in"].sem, 16)
                sp.dma_start(w2_raw[:, ROUTED * P:].rearrange("p (b d) -> p b d", d=D),
                             a["sw2"].rearrange("e h d -> (e h) d").rearrange("(b p) d -> p b d", p=P)
                             ).then_inc(s["w2_in"].sem, 16)
                sp.wait_ge(s["x_in"].sem, 16)
                sp.wait_ge(s["b2q_in"].sem, 64)

            @block.scalar
            def _(act):
                def rows_in(lo, hi, src):
                    act.dma_start(col_rows[lo:hi, :], src).then_inc(s["small_in"].sem, 16)

                rows_in(0, ROUTED, a["b1"].rearrange("(b e) h -> b (e h)", e=EPB))
                rows_in(ROUTED, BLOCKS, a["sb1"].rearrange("e (b h) -> (e b) h", h=P))
                rows_in(BLOCKS, BLOCKS + CB, a["conv_b"].rearrange("(b p) -> b p", p=P))
                rows_in(BLOCKS + CB, N_COLS, a["norm_w"].rearrange("(b p) -> b p", p=P))

                def vals_in(lo, hi, src):
                    act.dma_start(row_vals[0:1, lo:hi], src.rearrange("(a n) -> a n", a=1)
                                  ).then_inc(s["small_in"].sem, 16)

                vals_in(0, E, a["router_b"])
                vals_in(E, E + NH, a["dt_bias"])
                vals_in(E + NH, E + 2 * NH, a["A_log"])
                vals_in(E + 2 * NH, N_ROWS, a["D_param"])
                act.dma_start(sb2_rows[:, :], a["sb2"]).then_inc(s["small_in"].sem, 16)
                act.dma_start(conv_w[:, :, :], a["conv_w"].rearrange("(b p) o k -> p b (o k)", p=P)
                              ).then_inc(s["small_in"].sem, 16)
                act.dma_start(wout_raw[:, :], a["W_out"]).then_inc(s["small_in"].sem, 16)
                act.dma_start(m.router_w[:, :], a["router_w"]).then_inc(s["small_in"].sem, 16)
                act.dma_start(w1_raw[:, 0:ROUTED * P].rearrange("p (e h) -> p e h", h=HE),
                              a["w1"].rearrange("e d h -> d e h")).then_inc(s["w1_in"].sem, 16)
                act.dma_start(w1_raw[:, ROUTED * P:].rearrange("p (e h) -> p e h", h=HS),
                              a["sw1"].rearrange("e d h -> d e h")).then_inc(s["w1_in"].sem, 16)
                act.wait_ge(s["cols_ps"].sem, 1)
                nc.scalar.activation(m.cols[:, :], ps[:, 0, 0:N_COLS], ACT.Copy).then_inc(s["cols"].sem, 1)
                act.wait_ge(s["rows_ps"].sem, 1)
                nc.scalar.activation(m.rows[:, :], ps[:, 1, 0:N_ROWS], ACT.Copy).then_inc(s["rows"].sem, 1)
                act.wait_ge(s["rows"].sem, 1)
                nc.scalar.activation(m.a_neg[:, :], m.rows[:, E + NH:E + 2 * NH], ACT.Exp
                                     ).then_inc(s["exp_a"].sem, 1)
                act.wait_ge(s["z_ps"].sem, 1)
                nc.scalar.activation(m.wz_hi[:, :], ps[:, 2, 0:ZW + NH], ACT.Copy).then_inc(s["z_hi"].sem, 1)
                act.wait_ge(s["taps_ps"].sem, 1)
                nc.scalar.activation(m.wc_hi[:, :], ps[:, 3:3 + CB, :], ACT.Copy
                                     ).then_inc(s["taps_hi"].sem, 1)
                act.wait_ge(s["w2_in"].sem, 32)
                nc.scalar.activation(m.w2_hi[:, :], w2_raw[:, :], ACT.Copy).then_inc(s["w2_hi"].sem, 1)
                act.wait_ge(s["w1_in"].sem, 32)
                nc.scalar.activation(m.w1_hi[:, :], w1_raw[:, :], ACT.Copy).then_inc(s["w1_hi"].sem, 1)

            @block.gpsimd
            def _(pool):
                nc.gpsimd.memset(m.b2q[:, :], 0.0).then_inc(s["b2q_zeroed"].sem, 1)
                nc.gpsimd.memset(m.minus_half[:, :], -0.5)
                nc.gpsimd.memset(m.ones[:, :], 1.0).then_inc(s["zeroed"].sem, 1)
                pool.wait_ge(s["zeroed"].sem, 1)
                nc.gpsimd.affine_select(out=m.ident[:, :], in_=m.ones[:, :], compare_op=ALU.is_equal,
                                        fill=0.0, base=0, pattern=[[-1, P]], channel_multiplier=1
                                        ).then_inc(s["consts"].sem, 1)
                nc.gpsimd.affine_select(out=m.upto[:, :], in_=m.ones[:, :], compare_op=ALU.is_ge,
                                        fill=0.0, base=0, pattern=[[1, P]], channel_multiplier=-1
                                        ).then_inc(s["consts"].sem, 1)
                nc.gpsimd.affine_select(out=m.after[:, :], in_=m.ones[:, :], compare_op=ALU.is_gt,
                                        fill=0.0, base=0, pattern=[[-1, P]], channel_multiplier=1
                                        ).then_inc(s["consts"].sem, 1)
                pool.wait_ge(s["b2q_zeroed"].sem, 1)
                b2_v = a["b2"].rearrange("(j q) d -> q j d", q=4)
                for q in range(4):
                    pool.dma_start(m.b2q[32 * q:32 * q + E // 4, :], b2_v[q, :, :]
                                   ).then_inc(s["b2q_in"].sem, 16)

            @block.tensor
            def _(pe):
                pe.wait_ge(s["consts"].sem, 3)
                pe.wait_ge(s["small_in"].sem, 16 * 12)
                nc.tensor.transpose(ps[:, 0, 0:N_COLS], col_rows[:, :], m.ident[0:N_COLS, 0:N_COLS]
                                    ).then_inc(s["cols_ps"].sem, 1)
                nc.tensor.matmul(ps[:, 1, 0:N_ROWS], m.ones[0:1, :], row_vals[:, :], start=True, stop=True
                                 ).then_inc(s["rows_ps"].sem, 1)
                pe.wait_ge(s["win_in"].sem, 32)
                for b in range(ZW // P):
                    nc.tensor.transpose(ps[:, 2, b * P:(b + 1) * P], win[:, b, :], m.ident[:, :])
                nc.tensor.transpose(ps[:, 2, ZW:ZW + NH], win_dt[:, :], m.ident[0:NH, 0:NH]
                                    ).then_inc(s["z_ps"].sem, 1)
                pe.wait_ge(s["taps"].sem, 1)
                for b in range(CB):
                    for k in range(TAPS):
                        last = nc.tensor.transpose(ps[:, 3 + b, k * P:(k + 1) * P], win_tap[:, b, k, :],
                                                   m.ident[:, :])
                last.then_inc(s["taps_ps"].sem, 1)
                for b in range(DI // P):
                    last = nc.tensor.transpose(ps[:, 7, b * P:(b + 1) * P], wout_raw[:, b * P:(b + 1) * P],
                                               m.ident[:, :])
                last.then_inc(s["wout_ps"].sem, 1)
                pe.wait_ge(s["cols"].sem, 1)
                nc.tensor.matmul(ps[:, 0, 0:1], sb2_rows[:, :], m.ones[0:ES, 0:1], start=True, stop=True
                                 ).then_inc(s["sb2_ps"].sem, 1)

            @block.vector
            def _(dve):
                dve.wait_ge(s["small_in"].sem, 16 * 12)
                dve.wait_ge(s["win_in"].sem, 32)
                for b in range(CB):
                    for k in range(TAPS):
                        last = nc.vector.tensor_scalar(win_tap[:, b, k, :], win[:, 2 + b, :],
                                                       conv_w[:, b, k:k + 1], None, ALU.mult)
                last.then_inc(s["taps"].sem, 1)
                dve.wait_ge(s["exp_a"].sem, 1)
                nc.vector.tensor_scalar(m.a_neg[:, :], m.a_neg[:, :], -1.0, None, ALU.mult)
                dve.wait_ge(s["z_hi"].sem, 1)
                nc.vector.tensor_tensor(m.wz_lo[:, :], ps[:, 2, 0:ZW + NH], m.wz_hi[:, :].bitcast(F32),
                                        ALU.subtract)
                dve.wait_ge(s["taps_hi"].sem, 1)
                nc.vector.tensor_tensor(m.wc_lo[:, :], ps[:, 3:3 + CB, :], m.wc_hi[:, :].bitcast(F32),
                                        ALU.subtract)
                dve.wait_ge(s["wout_ps"].sem, 1)
                dve.wait_ge(s["cols"].sem, 1)
                for b in range(DI // P):
                    c = BLOCKS + CB + b
                    nc.vector.tensor_scalar(m.wout[:, b, :], ps[:, 7, b * P:(b + 1) * P],
                                            m.cols[:, c:c + 1], None, ALU.mult)
                dve.wait_ge(s["sb2_ps"].sem, 1)
                nc.vector.tensor_scalar(m.half_sb2[:, :], ps[:, 0, 0:1], 0.5, None, ALU.mult)
                dve.wait_ge(s["w2_hi"].sem, 1)
                nc.vector.tensor_tensor(m.w2_lo[:, :], w2_raw[:, :], m.w2_hi[:, :].bitcast(F32), ALU.subtract)
                dve.wait_ge(s["w1_hi"].sem, 1)
                nc.vector.tensor_tensor(m.w1_lo[:, :], w1_raw[:, :], m.w1_hi[:, :].bitcast(F32), ALU.subtract)


SLOTS = 2 * BLOCKS
TAIL = LAG + 2
FILLS = 2 + CB
FILL_AT = [6, 7, 9, 12, 15, 18]
TILE_SLOTS = 4
AT = dict(stats=0, moments=1, xn=2, xnT=4, xT_lo=5, dt=6, neg_abs=7,
          r_stats=2, r_moments=3, r_xn0=5, r_xn1=6, r_xnT0=7, r_xnT1=8, logits=10, peak=11, exp=12,
          top=13, rest=14, cwq0=16, cwq1=15, xn_hi1=17, cwT1=19, xn_hi0=22, cwT0=26,
          softplus=13, time=14, sums=15, seg_rhs=[15, 15, 16, 16], seg=[16, 17, 18, 18], seg_exp=18,
          pre=20, mix=21, main=22, y=23, state_dec=21, yT=25, out=27,
          ffn_y0=BLOCKS + LAG, ffn_y1=2 * BLOCKS + LAG)
USES_A = [f"fill{f}" for f in range(FILLS)] + ["state0", "state1", "out0", "state2", "out1", "out2", "out3"]
USES_C = ["seg0", "seg2", "tok0", "tok1", "yT0", "tok2", "yT1", "tok3", "yT2", "yT3"]
USES_D = ["seg1", "seg3", "y0", "y1", "y2", "y3"]
USES_B = [("xnT", "ssm"), ("dt", "ssm"), ("r_xnT0", "router0"), ("r_xnT1", "router1"), ("logits", "router"),
          ("sums", "ssm"), ("cwT1", "router1"), ("ffn_yT0", "ffn0"), ("cwT0", "router0"), ("ffn_yT1", "ffn1")]


def parts(i):
    p = {"ssm": 0 <= i < BATCHES, "router0": i + 2 < BATCHES, "router1": i >= 1,
         "ffn0": 0 <= i + 1 < BATCHES, "ffn1": i >= 1}
    p["router"] = p["router0"] or p["router1"]
    return p


def counts(i):
    p = parts(i)
    ffns = p["ffn0"] + p["ffn1"]
    return {"blocks": ffns * BLOCKS, "gates": ffns * ROUTED, "runs": ffns,
            "a": p["ssm"] * len(USES_A), "b": sum(p[part] for _, part in USES_B),
            "c": p["ssm"] * len(USES_C), "d": p["ssm"] * len(USES_D)}


class Iteration:

    def __init__(self, eng, like, i=None):
        self.i = like if i is None else i
        self.like, self.has = like, parts(like)
        self.sides = [side for side in range(2) if self.has[f"router{side}"]]
        self.uses_b = [name for name, part in USES_B if self.has[part]]

        def before(kind):
            size, count = counts(like)[kind], sum(counts(k)[kind] for k in range(-2, like))
            return count if i is None else eng.snap(i * size + (count - like * size))

        self.blocks, self.gates, self.runs = before("blocks"), before("gates"), before("runs")
        self.before_a, self.before_b = before("a"), before("b")
        self.before_c, self.before_d = before("c"), before("d")

    def block(self, n):
        if 0 <= n < 2 * BLOCKS and self.has[f"ffn{n // BLOCKS}"]:
            side = n // BLOCKS
            return n % BLOCKS, self.blocks + (n if self.has["ffn0"] else n - BLOCKS), side
        return None

    def gate(self, n):
        k, _, side = self.block(n)
        before = ROUTED if side and self.has["ffn0"] else 0
        return self.gates + (before + sum(kind == "routed" for kind, _ in ORDER[:k + 1]) - 1)

    def run(self, side):
        return self.runs + (1 if side and self.has["ffn0"] else 0)

    def last_block(self, side):
        return self.blocks + (BLOCKS * (1 + (side and self.has["ffn0"])) - 1)

    def ffn_batch(self, side):
        return self.i - 1 if side else self.i + 1

    def router_batch(self, side):
        return self.i - 1 if side else self.i + 2

    def ffn1_before(self):
        return self.runs - (2 if self.like > 1 else 1)

    def ssm_tile(self, t):
        return self.i * TPB + t

    def a(self, name):
        return self.before_a + USES_A.index(name)

    def b(self, name):
        return self.before_b + self.uses_b.index(name)

    def c(self, name):
        return self.before_c + USES_C.index(name)

    def d(self, name):
        return self.before_d + USES_D.index(name)


def main_phase(nc, m, out):
    with ExitStack() as ctx:
        def sb(name, shape, dt=F32):
            return ctx.enter_context(nc.sbuf_tensor(name, shape, dt))

        def bank(name):
            return ctx.enter_context(nc.psum_tensor(name, [P, 512], F32))

        xn_hi, xn_lo = sb("xn_hi", [P, 2, SEQ], F32R), sb("xn_lo", [P, 2, SEQ], F32R)
        weights = sb("weights", [P, 2, SEQ])
        hidden = sb("hidden", [P, RING, SEQ])
        hid_hi, hid_lo = sb("hid_hi", [P, RING, SEQ], F32R), sb("hid_lo", [P, RING, SEQ], F32R)
        ffn_y = sb("ffn_y", [P, SEQ])
        r_stats = sb("r_stats", [P, 2 * TPB, 6])
        r_moments = sb("r_moments", [P, 2 * TPB, 2])
        r_var = sb("r_var", [P, 2 * TPB])
        r_rstd = sb("r_rstd", [P, 2 * TPB])
        r_xn = sb("r_xn", [P, 2, TPB, D])
        r_xT = sb("r_xT", [P, 2, SEQ])
        logits = sb("logits_sb", [P, 2 * TPB, E])
        peak = sb("peak", [P, 2 * TPB])
        probs = sb("probs", [P, 2 * TPB, E])
        top = sb("top", [P, 2 * TPB, TOPK])
        rest = sb("rest", [P, 2 * TPB, E])
        top_sum = sb("top_sum", [P, 2 * TPB])
        top_inv = sb("top_inv", [P, 2 * TPB])
        cwq = sb("cwq", [P, 2 * TPB, 4, 32])
        pad = TAPS
        stats = sb("stats", [P, TPB, 6])
        moments = sb("moments", [P, TPB, 2])
        var_eps = sb("var_eps", [P, TPB])
        rstd = sb("rstd", [P, TPB])
        xn = sb("xn", [P, TPB, D])
        xT_hi, xT_lo = sb("xT_hi", [P, pad + SEQ], F32R), sb("xT_lo", [P, pad + SEQ], F32R)
        gate = sb("gate", [P, TPB, DI])
        chan = sb("chan", [P, CB, SEQ])
        dt_raw = sb("dt_raw", [P, TPB * NH])
        neg_abs, exp_na, u = sb("neg_abs", [P, TPB * NH]), sb("exp_na", [P, TPB * NH]), sb("u", [P, TPB * NH])
        u_err, u_inv, ln_u = sb("u_err", [P, TPB * NH]), sb("u_inv", [P, TPB * NH]), sb("ln_u", [P, TPB * NH])
        dt, dA = sb("dt", [P, TPB, NH]), sb("dA", [P, TPB, NH])
        decay = sb("decay", [P, 3, TPB, NH])
        dt_after = sb("dt_after", [P, TPB, NH])
        seg_rhs = sb("seg_rhs", [P, TPB, NH, P])
        seg = sb("seg", [P, TPB, NH, P])
        cb_mask = sb("cb_mask", [P, 2, P])
        mix = sb("mix", [P, 2, NH, P])
        tok = sb("tok", [P, 2, DI + NS + P])
        dx, dx_after = sb("dx", [P, 2, DI]), sb("dx_after", [P, 2, DI])
        skip, y_in, y = sb("skip", [P, 2, DI]), sb("y_in", [P, DI]), sb("y", [P, 2, DI])
        square = sb("square", [P, DI])
        sum_sq, mean_sq, inv_rms = sb("sum_sq", [P, TPB]), sb("mean_sq", [P, TPB]), sb("inv_rms", [P, TPB])
        yT = sb("yT", [P, 2, DI])
        state, state_dec = sb("state", [P, 2, DI]), sb("state_dec", [P, DI])

        up_ps = [bank("up0_ps"), bank("up1_ps")]
        acc_ps, cw_ps = bank("acc_ps"), bank("cw_ps")
        a_ps, b_ps, c_ps, d_ps = bank("a_ps"), bank("b_ps"), bank("c_ps"), bank("d_ps")

        s = Signals(nc, ctx, "main", [
            "dve_held", "pool_held",
            "zeroed", "up_ready", "hi_ready", "shuffled", "stored",
            "a_ready", "b_ready", "c_ready", "d_ready",
            "r_stats", "r_moments", "r_var", "r_rstd", "r_xn0", "r_xn1", "xn_hi0", "xn_hi1",
            "xn_lo0", "xn_lo1", "weights0", "weights1",
            "logits", "peak", "shifted", "probs", "top", "rest", "top_sum", "top_inv", "top_probs",
            "cwq0", "cwq1",
            "stats", "moments", "var_eps", "rstd", "xn", "xT_hi",
            "neg_abs", "exp_na", "ln_u", "u", "u_inv", "u_fix", "ln1p", "dt", "dA", "dt_after",
            "seg_rhs", "dx", "dx_after", "skip", "cb_mask", "mix", "state", "y_sum", "yg", "state_dec",
            "mean_sq", "inv_rms", "x_updated"],
            {"silu_done": 2, "gated": 1, "lo_ready": RING, "down_done": RING, "ffn_y": 1,
             "a_read": 1, "b_read": 1, "c_read": 1, "d_read": 1, "sum_sq": 1})

        out_v = out.rearrange("b (t p) d -> b p t d", p=P)

        def heads(ap):
            return ap.unsqueeze(2).to_broadcast([P, NH, HD])

        def by_head(ap):
            return ap.rearrange("p (h d) -> p h d", h=NH)

        def x_of(b, t):
            return m.x[:, bass.ds(b * SEQ + t * D, D)]

        def x_batch(b):
            return m.x[:, bass.ds(b * SEQ, SEQ)]

        def tiles_of(it):
            return slice(it.sides[0] * TPB, (it.sides[-1] + 1) * TPB)

        def tile_at(n, at):
            t, odd = divmod(n - at, TILE_SLOTS)
            return t if not odd and 0 <= t < TPB else None

        def iterations(eng, step):
            def run(it, prev):
                for n in range(SLOTS):
                    if prev and n < TAIL:
                        step(prev, SLOTS + n)
                    step(it, n)

            first, last = 2, BATCHES - 3
            prev = None
            for i in range(-2, first):
                it = Iteration(eng, i)
                run(it, prev)
                prev = it
            with eng.Fori(first, last + 1) as i:
                run(Iteration(eng, first, i), Iteration(eng, first, i - 1))
            prev = Iteration(eng, last)
            for i in range(last + 1, BATCHES + 1):
                it = Iteration(eng, i)
                run(it, prev)
                prev = it
            for n in range(TAIL):
                step(prev, SLOTS + n)

        with nc.Block() as block:
            @block.sync
            def _(sp):
                def step(it, n):
                    if n == AT["ffn_y1"] + 1 and it.has["ffn1"]:
                        sp.wait_ge(*done(s["x_updated"], it.run(1)))
                        sp.dma_start(out_v[it.ffn_batch(1)], x_batch(it.ffn_batch(1)).rearrange(
                            "p (t d) -> p t d", d=D)).then_inc(s["stored"].sem, 16)

                iterations(sp, step)
                sp.wait_ge(s["stored"].sem, 16 * BATCHES)

            @block.tensor
            def _(pe):
                def up(it, n):
                    k, i, side = it.block(n)
                    j = ORDER[k][1]
                    wh, wl = m.w1_hi[:, j * P:(j + 1) * P], m.w1_lo[:, j * P:(j + 1) * P]
                    if k == 0:
                        pe.wait_ge(*done(s[f"xn_lo{side}"], it.ffn_batch(side)))
                    pe.wait_ge(*done(s["silu_done"], i - 2))
                    o = up_ps[n % 2][:, :]
                    nc.tensor.matmul(o, wh, xn_hi[:, side, :], start=True, stop=False)
                    nc.tensor.matmul(o, wh, xn_lo[:, side, :], start=False, stop=False)
                    nc.tensor.matmul(o, wl, xn_hi[:, side, :], start=False, stop=True
                                     ).then_inc(s["up_ready"].sem, 1)

                def down(it, n):
                    k, i, side = it.block(n)
                    j = ORDER[k][1]
                    wh, wl = m.w2_hi[:, j * P:(j + 1) * P], m.w2_lo[:, j * P:(j + 1) * P]
                    if k == 0:
                        pe.wait_ge(*done(s[f"weights{side}"], it.ffn_batch(side)))
                        pe.wait_ge(*done(s["ffn_y"], it.run(side) - 1))
                        nc.tensor.matmul(acc_ps[:, :], m.b2q[:, :], weights[:, side, :],
                                         start=True, stop=False)
                    pe.wait_ge(*done(s["lo_ready"], i))
                    nc.tensor.matmul(acc_ps[:, :], wh, hid_hi[:, n % RING, :], start=False, stop=False)
                    nc.tensor.matmul(acc_ps[:, :], wh, hid_lo[:, n % RING, :], start=False, stop=False)
                    nc.tensor.matmul(acc_ps[:, :], wl, hid_hi[:, n % RING, :], start=False,
                                     stop=k == BLOCKS - 1).then_inc(s["down_done"].sem, 1)

                def bank_b(it, name):
                    pe.wait_ge(*done(s["b_read"], it.b(name) - 1))

                def transposed(o, tiles, sem):
                    for t, tile in enumerate(tiles):
                        last = nc.tensor.transpose(o[:, t * P:(t + 1) * P], tile, m.ident[:, :])
                    last.then_inc(sem, 1)

                def router(it, n):
                    for side in it.sides:
                        if n == AT[f"r_xnT{side}"]:
                            bank_b(it, f"r_xnT{side}")
                            pe.wait_ge(*done(s[f"r_xn{side}"], it.router_batch(side)))
                            transposed(b_ps, [r_xn[:, side, t, :] for t in range(TPB)], s["b_ready"].sem)
                        if n == AT[f"cwT{side}"]:
                            bank_b(it, f"cwT{side}")
                            pe.wait_ge(*done(s[f"cwq{side}"], it.router_batch(side)))
                            transposed(b_ps, [cwq[:, side * TPB + t, :, :].rearrange("p q j -> p (q j)")
                                              for t in range(TPB)], s["b_ready"].sem)
                    if it.sides and n == AT["logits"]:
                        bank_b(it, "logits")
                        for side in it.sides:
                            for t in range(TPB):
                                o = (side * TPB + t) * E
                                last = nc.tensor.matmul(b_ps[:, o:o + E], r_xT[:, side, t * P:(t + 1) * P],
                                                        m.router_w[:, :], start=True, stop=True)
                        last.then_inc(s["b_ready"].sem, 1)

                def fill(it, f):
                    pe.wait_ge(*done(s["a_read"], it.a(f"fill{f}") - 1))
                    if f < 2:
                        for i in range(2):
                            c = slice(pad + (2 * f + i) * P, pad + (2 * f + i + 1) * P)
                            o = a_ps[:, i * ZW:(i + 1) * ZW]
                            nc.tensor.matmul(o, xT_hi[:, c], m.wz_hi[:, 0:ZW], start=True, stop=False)
                            nc.tensor.matmul(o, xT_lo[:, c], m.wz_hi[:, 0:ZW], start=False, stop=False)
                            last = nc.tensor.matmul(o, xT_hi[:, c], m.wz_lo[:, 0:ZW], start=False, stop=True)
                    else:
                        for k in range(TAPS):
                            w = slice(((f - 2) * TAPS + k) * P, ((f - 2) * TAPS + k + 1) * P)
                            c = slice(pad - (TAPS - 1) + k, pad - (TAPS - 1) + k + SEQ)
                            nc.tensor.matmul(a_ps[:, :], m.wc_hi[:, w], xT_hi[:, c], start=k == 0, stop=False)
                            nc.tensor.matmul(a_ps[:, :], m.wc_hi[:, w], xT_lo[:, c], start=False, stop=False)
                            last = nc.tensor.matmul(a_ps[:, :], m.wc_lo[:, w], xT_hi[:, c], start=False,
                                                    stop=k == TAPS - 1)
                    last.then_inc(s["a_ready"].sem, 1)

                def ssm(it, n):
                    b = it.i
                    if n == AT["xnT"]:
                        bank_b(it, "xnT")
                        pe.wait_ge(*done(s["xn"], b))
                        transposed(b_ps, [xn[:, t, :] for t in range(TPB)], s["b_ready"].sem)
                    if n == AT["dt"]:
                        bank_b(it, "dt")
                        for t in range(TPB):
                            c = slice(pad + t * P, pad + (t + 1) * P)
                            o = b_ps[:, t * NH:(t + 1) * NH]
                            nc.tensor.matmul(o, xT_hi[:, c], m.wz_hi[:, ZW:], start=True, stop=False)
                            nc.tensor.matmul(o, xT_lo[:, c], m.wz_hi[:, ZW:], start=False, stop=False)
                            last = nc.tensor.matmul(o, xT_hi[:, c], m.wz_lo[:, ZW:], start=False, stop=True)
                        last.then_inc(s["b_ready"].sem, 1)
                    for f in range(FILLS):
                        if n == FILL_AT[f]:
                            fill(it, f)
                    if n == AT["sums"]:
                        bank_b(it, "sums")
                        pe.wait_ge(*done(s["dA"], b))
                        dA16 = dA[:, :, :].rearrange("p t h -> p (t h)")
                        for i, w in enumerate((m.upto, m.after, m.ones)):
                            last = nc.tensor.matmul(b_ps[:, i * TPB * NH:(i + 1) * TPB * NH], w[:, :], dA16,
                                                    start=True, stop=True)
                        last.then_inc(s["b_ready"].sem, 1)
                    for t in range(TPB):
                        if n == AT["seg"][t]:
                            if t % 2:
                                o, ready = d_ps, s["d_ready"]
                                pe.wait_ge(*done(s["d_read"], it.d(f"seg{t}") - 1))
                            else:
                                o, ready = c_ps, s["c_ready"]
                                pe.wait_ge(*done(s["c_read"], it.c(f"seg{t}") - 1))
                            pe.wait_ge(*done(s["seg_rhs"], it.ssm_tile(t)))
                            nc.tensor.matmul(o[:, :], m.after[:, :],
                                             seg_rhs[:, t, :, :].rearrange("p h t -> p (h t)"),
                                             start=True, stop=True).then_inc(ready.sem, 1)
                    t = tile_at(n, AT["pre"])
                    if t is not None:
                        c = slice(t * P, (t + 1) * P)
                        pe.wait_ge(*done(s["c_read"], it.c(f"tok{t}") - 1))
                        pe.wait_ge(*done(s["a_read"], it.a(f"fill{FILLS - 1}")))
                        for i in range(3):
                            nc.tensor.transpose(c_ps[:, i * P:(i + 1) * P], chan[:, i, c], m.ident[:, :])
                        nc.tensor.matmul(c_ps[:, 3 * P:], chan[:, 2, c], chan[:, 3, c], start=True, stop=True
                                         ).then_inc(s["c_ready"].sem, 1)
                    t = tile_at(n, AT["main"])
                    if t is not None:
                        main(it, t)
                    t = tile_at(n, AT["yT"])
                    if t is not None:
                        pe.wait_ge(*done(s["c_read"], it.c(f"yT{t}") - 1))
                        pe.wait_ge(*done(s["yg"], it.ssm_tile(t)))
                        transposed(c_ps, [y[:, t % 2, i * P:(i + 1) * P] for i in range(DI // P)],
                                   s["c_ready"].sem)
                    t = tile_at(n, AT["out"])
                    if t is not None:
                        pe.wait_ge(*done(s["a_read"], it.a(f"out{t}") - 1))
                        pe.wait_ge(*done(s["c_read"], it.c(f"yT{t}")))
                        for i in range(DI // P):
                            last = nc.tensor.matmul(a_ps[:, 0:D], yT[:, t % 2, i * P:(i + 1) * P],
                                                    m.wout[:, i, :], start=i == 0, stop=i == DI // P - 1)
                        last.then_inc(s["a_ready"].sem, 1)

                def main(it, t):
                    c = slice(t * P, (t + 1) * P)
                    if t < TPB - 1:
                        pe.wait_ge(*done(s["a_read"], it.a(f"state{t}") - 1))
                        pe.wait_ge(*done(s["dx_after"], it.i * (TPB - 1) + t))
                        nc.tensor.matmul(a_ps[:, 0:DI], tok[:, t % 2, DI:DI + NS], dx_after[:, t % 2, :],
                                         start=True, stop=True).then_inc(s["a_ready"].sem, 1)
                    pe.wait_ge(*done(s["d_read"], it.d(f"y{t}") - 1))
                    if t:
                        pe.wait_ge(*done(s["state"], it.i * (TPB - 1) + (t - 1)))
                        nc.tensor.matmul(d_ps[:, DI:], chan[:, 3, c], state[:, (t - 1) % 2, :],
                                         start=True, stop=True)
                    pe.wait_ge(*done(s["dx"], it.ssm_tile(t)))
                    pe.wait_ge(*done(s["mix"], it.ssm_tile(t)))
                    for h in range(NH):
                        last = nc.tensor.matmul(d_ps[:, h * HD:(h + 1) * HD], mix[:, t % 2, h, :],
                                                dx[:, t % 2, h * HD:(h + 1) * HD], start=True, stop=True)
                    last.then_inc(s["d_ready"].sem, 1)

                def step(it, n):
                    if it.block(n):
                        up(it, n)
                    if it.has["ssm"]:
                        ssm(it, n)
                    router(it, n)
                    for side in range(2):
                        if n == AT[f"ffn_y{side}"] + 1 and it.has[f"ffn{side}"]:
                            bank_b(it, f"ffn_yT{side}")
                            pe.wait_ge(*done(s["ffn_y"], it.run(side)))
                            transposed(b_ps, [ffn_y[:, t * P:(t + 1) * P] for t in range(TPB)],
                                       s["b_ready"].sem)
                    if it.block(n - LAG):
                        down(it, n - LAG)

                iterations(pe, step)

            @block.scalar
            def _(act):
                def exps(it):
                    nc.scalar.preload_act_table_set("natural_log_exp_and_others")
                    if it.sides:
                        r = tiles_of(it)
                        act.wait_ge(*done(s["shifted"], it.i + 2))
                        nc.scalar.activation(probs[:, r, :], logits[:, r, :], ACT.Exp
                                             ).then_inc(s["probs"].sem, 1)
                    if it.has["ssm"]:
                        act.wait_ge(*done(s["neg_abs"], it.i))
                        nc.scalar.activation(exp_na[:, :], neg_abs[:, :], ACT.Exp).then_inc(s["exp_na"].sem, 1)
                        act.wait_ge(*done(s["exp_na"], it.i))
                        nc.scalar.activation(ln_u[:, :], exp_na[:, :], ACT.Ln, bias=1.0
                                             ).then_inc(s["ln_u"].sem, 1)
                    if it.has["ffn0"] or it.has["ssm"]:
                        nc.scalar.preload_act_table(ACT.Silu)

                def decays(it):
                    nc.scalar.preload_act_table(ACT.Exp)
                    act.wait_ge(*done(s["b_ready"], it.b("sums")))
                    nc.scalar.activation(decay[:, :, :, :].rearrange("p i t h -> p (i t h)"),
                                         b_ps[:, 0:3 * TPB * NH], ACT.Exp).then_inc(s["b_read"].sem, 1)
                    for t in range(TPB):
                        bank, ready, read, use = ((d_ps, s["d_ready"], s["d_read"], it.d) if t % 2 else
                                                  (c_ps, s["c_ready"], s["c_read"], it.c))
                        act.wait_ge(*done(ready, use(f"seg{t}")))
                        nc.scalar.activation(seg[:, t, :, :].rearrange("p h t -> p (h t)"), bank[:, :],
                                             ACT.Exp).then_inc(read.sem, 1)
                    nc.scalar.preload_act_table(ACT.Silu)

                def router(it, n):
                    for side in it.sides:
                        batch = it.router_batch(side)
                        if n == AT[f"r_xnT{side}"]:
                            act.wait_ge(*done(s["b_ready"], it.b(f"r_xnT{side}")))
                            nc.scalar.activation(r_xT[:, side, :], b_ps[:, :], ACT.Copy
                                                 ).then_inc(s["b_read"].sem, 1)
                        if n == AT[f"xn_hi{side}"]:
                            act.wait_ge(*done(s["b_read"], it.b(f"r_xnT{side}")))
                            nc.scalar.activation(xn_hi[:, side, :], r_xT[:, side, :], ACT.Copy
                                                 ).then_inc(s[f"xn_hi{side}"].sem, 1)
                        if n == AT[f"cwT{side}"]:
                            act.wait_ge(*done(s["b_ready"], it.b(f"cwT{side}")))
                            nc.scalar.activation(weights[:, side, :], b_ps[:, :], ACT.Copy
                                                 ).then_inc(s[f"weights{side}"].sem, 1)
                            act.wait_ge(*done(s[f"weights{side}"], batch))
                            act.sem_inc(s["b_read"].sem, 1)

                def ssm(it, n):
                    if n == AT["xnT"]:
                        act.wait_ge(*done(s["b_ready"], it.b("xnT")))
                        nc.scalar.activation(xT_hi[:, pad:], b_ps[:, :], ACT.Copy).then_inc(s["xT_hi"].sem, 1)
                    for f in range(FILLS):
                        if n == FILL_AT[f]:
                            act.wait_ge(*done(s["a_ready"], it.a(f"fill{f}")))
                            if f < 2:
                                nc.scalar.activation(gate[:, 2 * f:2 * f + 2, :].rearrange("p t c -> p (t c)"),
                                                     a_ps[:, :], ACT.Silu).then_inc(s["a_read"].sem, 1)
                            else:
                                c = BLOCKS + f - 2
                                nc.scalar.activation(chan[:, f - 2, :], a_ps[:, :], ACT.Silu,
                                                     bias=m.cols[:, c:c + 1]).then_inc(s["a_read"].sem, 1)
                    t = tile_at(n, AT["pre"])
                    if t is not None:
                        if t >= 2:
                            act.wait_ge(*done(s["skip"], it.ssm_tile(t - 2)))
                        act.wait_ge(*done(s["c_ready"], it.c(f"tok{t}")))
                        nc.scalar.activation(tok[:, t % 2, :], c_ps[:, :], ACT.Copy).then_inc(s["c_read"].sem, 1)
                    t = tile_at(n, AT["yT"])
                    if t is not None:
                        act.wait_ge(*done(s["sum_sq"], it.ssm_tile(t - 1)))
                        act.wait_ge(*done(s["c_ready"], it.c(f"yT{t}")))
                        nc.scalar.activation(yT[:, t % 2, :], c_ps[:, 0:DI], ACT.Copy
                                             ).then_inc(s["c_read"].sem, 1)
                        nc.scalar.activation(square[:, :], y[:, t % 2, :], ACT.Square,
                                             accum_out=sum_sq[:, t:t + 1]).then_inc(s["sum_sq"].sem, 1)

                def step(it, n):
                    for side in range(2):
                        if n == AT[f"ffn_y{side}"] and it.has[f"ffn{side}"]:
                            act.wait_ge(*done(s["down_done"], it.last_block(side)))
                            nc.scalar.activation(ffn_y[:, :], acc_ps[:, :], ACT.Identity,
                                                 bias=m.half_sb2[:, 0:1], scale=0.5).then_inc(s["ffn_y"].sem, 1)
                    if it.block(n):
                        k, i, _ = it.block(n)
                        j = ORDER[k][1]
                        act.wait_ge(*done(s["lo_ready"], i - RING))
                        act.wait_ge(*done(s["up_ready"], i))
                        nc.scalar.activation(hidden[:, n % RING, :], up_ps[n % 2][:, :], ACT.Silu,
                                             bias=m.cols[:, j:j + 1]).then_inc(s["silu_done"].sem, 1)
                    if it.block(n - 1):
                        k, i, _ = it.block(n - 1)
                        if ORDER[k][0] == "routed":
                            act.wait_ge(*done(s["gated"], it.gate(n - 1)))
                        else:
                            act.wait_ge(*done(s["silu_done"], i))
                        act.wait_ge(*done(s["down_done"], i - RING))
                        nc.scalar.activation(hid_hi[:, (n - 1) % RING, :], hidden[:, (n - 1) % RING, :],
                                             ACT.Copy).then_inc(s["hi_ready"].sem, 1)
                    if n == AT["exp"]:
                        exps(it)
                    if n == AT["seg_exp"] and it.has["ssm"]:
                        decays(it)
                    if it.has["ssm"]:
                        ssm(it, n)
                    router(it, n)

                iterations(act, step)

            @block.vector
            def _(dve):
                def aggregate(stats, moments, tiles, stats_done, moments_done, n):
                    dve.wait_ge(*done(stats_done, n))
                    dve.sem_inc(s["dve_held"].sem, 1)
                    for t in tiles:
                        last = nc.vector.bn_aggr(moments[:, t, :], stats[:, t, :])
                    last.then_inc(moments_done.sem, 1)

                def normed(out_of, x, moments, rstd, tiles, sem):
                    for t, tile in enumerate(tiles):
                        last = nc.vector.tensor_scalar(out_of(t), x(t), moments[:, tile, 0:1],
                                                       rstd[:, tile:tile + 1], ALU.subtract, ALU.mult)
                    last.then_inc(sem, 1)

                def router(it, n):
                    r = tiles_of(it)
                    run = it.i + 2
                    if n == AT["r_stats"]:
                        if it.has["router1"]:
                            dve.wait_ge(*done(s["a_read"], it.i * len(USES_A) - 1))
                        for side in it.sides:
                            for t in range(TPB):
                                last = nc.vector.bn_stats(r_stats[:, side * TPB + t, :],
                                                          x_of(it.router_batch(side), t))
                        last.then_inc(s["r_stats"].sem, 1)
                    if n == AT["r_moments"]:
                        aggregate(r_stats, r_moments, range(r.start, r.stop), s["r_stats"], s["r_moments"], run)
                    for side in it.sides:
                        if n == AT[f"r_xn{side}"]:
                            batch = it.router_batch(side)
                            dve.wait_ge(*done(s["r_rstd"], run))
                            normed(lambda t: r_xn[:, side, t, :], lambda t: x_of(batch, t), r_moments, r_rstd,
                                   range(side * TPB, (side + 1) * TPB), s[f"r_xn{side}"].sem)
                    width = r.stop - r.start
                    if n == AT["logits"]:
                        dve.wait_ge(*done(s["b_ready"], it.b("logits")))
                        nc.vector.tensor_tensor(
                            logits[:, r, :],
                            b_ps[:, r.start * E:r.stop * E].rearrange("p (t e) -> p t e", e=E),
                            m.rows[:, 0:E].unsqueeze(1).to_broadcast([P, width, E]), ALU.add
                            ).then_inc(s["b_read"].sem, 1)
                    if n == AT["peak"]:
                        dve.wait_ge(*done(s["b_read"], it.b("logits")))
                        nc.vector.tensor_reduce(peak[:, r], logits[:, r, :], AX.X, ALU.max
                                                ).then_inc(s["peak"].sem, 1)
                    if n == AT["top"]:
                        dve.wait_ge(*done(s["probs"], run))
                        dve.sem_inc(s["dve_held"].sem, 1)
                        for t in range(r.start, r.stop):
                            last = nc.vector.max(top[:, t, :], probs[:, t, :])
                        last.then_inc(s["top"].sem, 1)
                    if n == AT["rest"]:
                        dve.wait_ge(*done(s["top"], run))
                        dve.sem_inc(s["dve_held"].sem, 1)
                        for t in range(r.start, r.stop):
                            last = nc.vector.match_replace(rest[:, t, :], top[:, t, :], probs[:, t, :], 0.0)
                        last.then_inc(s["rest"].sem, 1)
                        nc.vector.tensor_reduce(top_sum[:, r], top[:, r, :], AX.X, ALU.add
                                                ).then_inc(s["top_sum"].sem, 1)
                        dve.wait_ge(*done(s["top_sum"], run))
                        nc.vector.reciprocal(top_inv[:, r], top_sum[:, r]).then_inc(s["top_inv"].sem, 1)

                def softplus(b):
                    dve.wait_ge(*done(s["exp_na"], b))
                    nc.vector.tensor_scalar(u[:, :], exp_na[:, :], 1.0, None, ALU.add
                                            ).then_inc(s["u"].sem, 1)
                    dve.wait_ge(*done(s["u"], b))
                    nc.vector.scalar_tensor_tensor(u_err[:, :], u[:, :], 1.0, exp_na[:, :],
                                                   ALU.subtract, ALU.subtract)
                    nc.vector.reciprocal(u_inv[:, :], u[:, :]).then_inc(s["u_inv"].sem, 1)
                    dve.wait_ge(*done(s["u_inv"], b))
                    nc.vector.tensor_tensor(u_err[:, :], u_err[:, :], u_inv[:, :], ALU.mult
                                            ).then_inc(s["u_fix"].sem, 1)

                def time_steps(b):
                    dve.wait_ge(*done(s["u_fix"], b))
                    dve.wait_ge(*done(s["ln_u"], b))
                    nc.vector.tensor_tensor(ln_u[:, :], ln_u[:, :], u_err[:, :], ALU.subtract
                                            ).then_inc(s["ln1p"].sem, 1)
                    dve.wait_ge(*done(s["ln1p"], b))
                    nc.vector.scalar_tensor_tensor(dt[:, :, :].rearrange("p t h -> p (t h)"),
                                                   dt_raw[:, :], 0.0, ln_u[:, :], ALU.max, ALU.add
                                                   ).then_inc(s["dt"].sem, 1)
                    dve.wait_ge(*done(s["dt"], b))
                    nc.vector.tensor_tensor(dA[:, :, :], dt[:, :, :],
                                            m.a_neg[:, :].unsqueeze(1).to_broadcast([P, TPB, NH]), ALU.mult
                                            ).then_inc(s["dA"].sem, 1)

                def ssm(it, n):
                    b = it.i
                    if n == AT["stats"]:
                        dve.wait_ge(*done(s["x_updated"], it.ffn1_before()))
                        for t in range(TPB):
                            last = nc.vector.bn_stats(stats[:, t, :], x_of(b, t))
                        last.then_inc(s["stats"].sem, 1)
                    if n == AT["moments"]:
                        aggregate(stats, moments, range(TPB), s["stats"], s["moments"], b)
                    if n == AT["xn"]:
                        dve.wait_ge(*done(s["rstd"], b))
                        normed(lambda t: xn[:, t, :], lambda t: x_of(b, t), moments, rstd, range(TPB),
                               s["xn"].sem)
                    if n == AT["xT_lo"]:
                        dve.wait_ge(*done(s["xT_hi"], b))
                        nc.vector.tensor_tensor(xT_lo[:, pad:], b_ps[:, :], xT_hi[:, pad:].bitcast(F32),
                                                ALU.subtract).then_inc(s["b_read"].sem, 1)
                    if n == AT["dt"]:
                        dve.wait_ge(*done(s["b_ready"], it.b("dt")))
                        nc.vector.tensor_tensor(
                            dt_raw[:, :].rearrange("p (t h) -> p t h", h=NH),
                            b_ps[:, 0:TPB * NH].rearrange("p (t h) -> p t h", h=NH),
                            m.rows[:, E:E + NH].unsqueeze(1).to_broadcast([P, TPB, NH]), ALU.add
                            ).then_inc(s["b_read"].sem, 1)
                    if n == AT["neg_abs"]:
                        dve.wait_ge(*done(s["b_read"], it.b("dt")))
                        nc.vector.scalar_tensor_tensor(neg_abs[:, :], dt_raw[:, :], -1.0, dt_raw[:, :],
                                                       ALU.mult, ALU.min).then_inc(s["neg_abs"].sem, 1)
                    if n == AT["softplus"]:
                        softplus(b)
                    if n == AT["time"]:
                        time_steps(b)
                    t = tile_at(n, AT["mix"])
                    if t is not None:
                        i = it.ssm_tile(t)
                        dve.wait_ge(*done(s["c_read"], it.c(f"tok{t}")))
                        nc.vector.tensor_tensor(cb_mask[:, t % 2, :], tok[:, t % 2, DI + NS:], m.upto[:, :],
                                                ALU.mult).then_inc(s["cb_mask"].sem, 1)
                        dve.wait_ge(*done(s["cb_mask"], i))
                        nc.vector.tensor_tensor(mix[:, t % 2, :, :], seg[:, t, :, :],
                                                cb_mask[:, t % 2, :].unsqueeze(1).to_broadcast([P, NH, P]),
                                                ALU.mult).then_inc(s["mix"].sem, 1)
                    t = tile_at(n, AT["main"])
                    if t is not None and t < TPB - 1:
                        dve.wait_ge(*done(s["a_ready"], it.a(f"state{t}")))
                        if t == 0:
                            nc.vector.tensor_copy(state[:, t % 2, :], a_ps[:, 0:DI]
                                                  ).then_inc(s["state"].sem, 1)
                        else:
                            dve.wait_ge(*done(s["state_dec"], b * (TPB - 2) + (t - 1)))
                            nc.vector.tensor_tensor(state[:, t % 2, :], state_dec[:, :], a_ps[:, 0:DI],
                                                    ALU.add).then_inc(s["state"].sem, 1)
                        dve.wait_ge(*done(s["state"], b * (TPB - 1) + t))
                        dve.sem_inc(s["a_read"].sem, 1)
                    t = tile_at(n, AT["y"])
                    if t is not None:
                        y_of(it, t)
                    t = tile_at(n, AT["out"])
                    if t is not None:
                        dve.wait_ge(*done(s["inv_rms"], it.ssm_tile(t)))
                        dve.wait_ge(*done(s["a_ready"], it.a(f"out{t}")))
                        nc.vector.scalar_tensor_tensor(x_of(b, t), a_ps[:, 0:D], inv_rms[:, t:t + 1],
                                                       x_of(b, t), ALU.mult, ALU.add
                                                       ).then_inc(s["a_read"].sem, 1)

                def y_of(it, t):
                    b = it.i
                    dve.wait_ge(*done(s["d_ready"], it.d(f"y{t}")))
                    if t:
                        nc.vector.tensor_tensor(by_head(y_in[:, :]), by_head(d_ps[:, DI:]),
                                                heads(decay[:, 0, t, :]), ALU.mult)
                    dve.wait_ge(*done(s["skip"], it.ssm_tile(t)))
                    nc.vector.tensor_tensor(y[:, t % 2, :], skip[:, t % 2, :], d_ps[:, 0:DI], ALU.add
                                            ).then_inc(s["d_read"].sem, 1)
                    dve.wait_ge(*done(s["d_read"], it.d(f"y{t}")))
                    if t:
                        nc.vector.tensor_tensor(y[:, t % 2, :], y[:, t % 2, :], y_in[:, :], ALU.add
                                                ).then_inc(s["y_sum"].sem, 1)
                        dve.wait_ge(*done(s["y_sum"], b * (TPB - 1) + (t - 1)))
                    nc.vector.tensor_tensor(y[:, t % 2, :], y[:, t % 2, :], gate[:, t, :], ALU.mult
                                            ).then_inc(s["yg"].sem, 1)

                def step(it, n):
                    routed = it.block(n) and ORDER[it.block(n)[0]][0] == "routed"
                    if routed:
                        k, i, side = it.block(n)
                        if k == 0:
                            dve.wait_ge(*done(s[f"weights{side}"], it.ffn_batch(side)))
                        dve.wait_ge(*done(s["gated"], it.gate(n) - 1))
                        dve.sem_inc(s["dve_held"].sem, 1)
                        nc.vector.stream_shuffle(cw_ps[:, :], weights[:, side, :], [ORDER[k][1]] * 32
                                                 ).then_inc(s["shuffled"].sem, 1)
                    if it.has["ssm"]:
                        ssm(it, n)
                    if it.sides:
                        router(it, n)
                    for side in range(2):
                        if n == AT[f"ffn_y{side}"] + 1 and it.has[f"ffn{side}"]:
                            dve.wait_ge(*done(s["b_ready"], it.b(f"ffn_yT{side}")))
                            nc.vector.tensor_tensor(x_batch(it.ffn_batch(side)), b_ps[:, :],
                                                    x_batch(it.ffn_batch(side)), ALU.add
                                                    ).then_inc(s["x_updated"].sem, 1)
                            dve.wait_ge(*done(s["x_updated"], it.run(side)))
                            dve.sem_inc(s["b_read"].sem, 1)
                    if routed:
                        dve.wait_ge(*done(s["shuffled"], it.gate(n)))
                        dve.wait_ge(*done(s["silu_done"], i))
                        nc.vector.tensor_tensor(hidden[:, n % RING, :], hidden[:, n % RING, :], cw_ps[:, :],
                                                ALU.mult).then_inc(s["gated"].sem, 1)

                iterations(dve, step)

            @block.gpsimd
            def _(pool):
                s.give_credits(pool)
                nc.gpsimd.memset(xT_hi[:, 0:pad].bitcast(F32), 0.0)
                nc.gpsimd.memset(xT_lo[:, 0:pad].bitcast(F32), 0.0)
                nc.gpsimd.memset(cwq[:, :, :, :], 0.0).then_inc(s["zeroed"].sem, 1)
                pool.wait_ge(s["zeroed"].sem, 1)

                def inverse_root(var, moments, out, tiles, moments_done, var_done, out_done, n):
                    pool.wait_ge(*done(moments_done, n))
                    pool.sem_inc(s["pool_held"].sem, 1)
                    nc.gpsimd.tensor_scalar(var[:, tiles], moments[:, tiles, 1], 1.0, EPS, ALU.mult, ALU.add
                                            ).then_inc(var_done.sem, 1)
                    pool.wait_ge(*done(var_done, n))
                    nc.gpsimd.tensor_tensor(out[:, tiles], var[:, tiles], m.minus_half[:, tiles], ALU.pow
                                            ).then_inc(out_done.sem, 1)

                def router(it, n):
                    r, run = tiles_of(it), it.i + 2
                    if n == AT["r_moments"]:
                        inverse_root(r_var, r_moments, r_rstd, r, s["r_moments"], s["r_var"], s["r_rstd"], run)
                    if n == AT["peak"]:
                        pool.wait_ge(*done(s["peak"], run))
                        nc.gpsimd.tensor_tensor(logits[:, r, :], logits[:, r, :],
                                                peak[:, r].unsqueeze(2).to_broadcast([P, r.stop - r.start, E]),
                                                ALU.subtract).then_inc(s["shifted"].sem, 1)
                    if n == AT["rest"]:
                        pool.wait_ge(*done(s["rest"], run))
                        nc.gpsimd.tensor_tensor(probs[:, r, :], probs[:, r, :], rest[:, r, :], ALU.subtract
                                                ).then_inc(s["top_probs"].sem, 1)
                    for side in it.sides:
                        if n == AT[f"cwq{side}"]:
                            pool.wait_ge(*done(s["top_inv"], run))
                            pool.wait_ge(*done(s["top_probs"], run))
                            for t in range(side * TPB, (side + 1) * TPB):
                                last = nc.gpsimd.tensor_tensor(
                                    cwq[:, t, :, 0:E // 4], probs[:, t, :].rearrange("p (j q) -> p q j", q=4),
                                    top_inv[:, t:t + 1].unsqueeze(2).to_broadcast([P, 4, E // 4]), ALU.mult)
                            last.then_inc(s[f"cwq{side}"].sem, 1)
                        if n == AT[f"xn_hi{side}"]:
                            pool.wait_ge(*done(s[f"xn_hi{side}"], it.router_batch(side)))
                            nc.gpsimd.tensor_tensor(xn_lo[:, side, :], r_xT[:, side, :],
                                                    xn_hi[:, side, :].bitcast(F32), ALU.subtract
                                                    ).then_inc(s[f"xn_lo{side}"].sem, 1)

                def ssm(it, n):
                    b = it.i
                    if n == AT["moments"]:
                        inverse_root(var_eps, moments, rstd, slice(0, TPB), s["moments"], s["var_eps"],
                                     s["rstd"], b)
                    for t in range(TPB):
                        if n == AT["seg_rhs"][t]:
                            pool.wait_ge(*done(s["dA"], b))
                            nc.gpsimd.tensor_tensor(seg_rhs[:, t, :, :],
                                                    dA[:, t, :].unsqueeze(2).to_broadcast([P, NH, P]),
                                                    m.upto[:, :].unsqueeze(1).to_broadcast([P, NH, P]),
                                                    ALU.mult).then_inc(s["seg_rhs"].sem, 1)
                    if n == AT["seg_exp"] + 1:
                        pool.wait_ge(*done(s["b_read"], it.b("sums")))
                        nc.gpsimd.tensor_tensor(dt_after[:, :, :], dt[:, :, :], decay[:, 1, :, :], ALU.mult
                                                ).then_inc(s["dt_after"].sem, 1)
                    t = tile_at(n, AT["pre"])
                    if t is not None:
                        x_tok = by_head(tok[:, t % 2, 0:DI])
                        pool.wait_ge(*done(s["dt_after"], b))
                        pool.wait_ge(*done(s["c_read"], it.c(f"tok{t}")))
                        if t < TPB - 1:
                            nc.gpsimd.tensor_tensor(by_head(dx_after[:, t % 2, :]), x_tok,
                                                    heads(dt_after[:, t, :]), ALU.mult
                                                    ).then_inc(s["dx_after"].sem, 1)
                        nc.gpsimd.tensor_tensor(by_head(dx[:, t % 2, :]), x_tok, heads(dt[:, t, :]), ALU.mult
                                                ).then_inc(s["dx"].sem, 1)
                        nc.gpsimd.tensor_tensor(by_head(skip[:, t % 2, :]), x_tok,
                                                heads(m.rows[:, E + 2 * NH:E + 3 * NH]), ALU.mult
                                                ).then_inc(s["skip"].sem, 1)
                    t = tile_at(n, AT["state_dec"])
                    if t is not None and 1 <= t < TPB - 1:
                        pool.wait_ge(*done(s["state"], b * (TPB - 1) + (t - 1)))
                        nc.gpsimd.tensor_tensor(by_head(state_dec[:, :]), by_head(state[:, (t - 1) % 2, :]),
                                                heads(decay[:, 2, t, :]), ALU.mult
                                                ).then_inc(s["state_dec"].sem, 1)
                    t = tile_at(n, AT["yT"])
                    if t is not None:
                        i = slice(t, t + 1)
                        pool.wait_ge(*done(s["sum_sq"], it.ssm_tile(t)))
                        pool.sem_inc(s["pool_held"].sem, 1)
                        nc.gpsimd.tensor_scalar(mean_sq[:, i], sum_sq[:, i], 1.0 / DI, EPS, ALU.mult, ALU.add
                                                ).then_inc(s["mean_sq"].sem, 1)
                        pool.wait_ge(*done(s["mean_sq"], it.ssm_tile(t)))
                        nc.gpsimd.tensor_tensor(inv_rms[:, i], mean_sq[:, i], m.minus_half[:, 0:1], ALU.pow
                                                ).then_inc(s["inv_rms"].sem, 1)

                def step(it, n):
                    if it.block(n - 1):
                        _, i, _ = it.block(n - 1)
                        pool.wait_ge(*done(s["hi_ready"], i))
                        nc.gpsimd.tensor_tensor(hid_lo[:, (n - 1) % RING, :], hidden[:, (n - 1) % RING, :],
                                                hid_hi[:, (n - 1) % RING, :].bitcast(F32), ALU.subtract
                                                ).then_inc(s["lo_ready"].sem, 1)
                    if it.has["ssm"]:
                        ssm(it, n)
                    if it.sides:
                        router(it, n)

                iterations(pool, step)




def program(nc, arrays, out):
    with ExitStack() as ctx:
        m = Tensors()

        def sb(name, shape, dt=F32):
            return ctx.enter_context(nc.sbuf_tensor(name, shape, dt))

        m.x = sb("x_res", [P, TOKENS // P * D])
        m.w1_hi, m.w1_lo = sb("w1_hi", [P, BLOCKS * P], F32R), sb("w1_lo", [P, BLOCKS * P], F32R)
        m.w2_hi, m.w2_lo = sb("w2_hi", [P, BLOCKS * P], F32R), sb("w2_lo", [P, BLOCKS * P], F32R)
        m.wz_hi, m.wz_lo = sb("wz_hi", [P, ZW + NH], F32R), sb("wz_lo", [P, ZW + NH], F32R)
        m.wc_hi = sb("wc_hi", [P, CB * TAPS * P], F32R)
        m.wc_lo = sb("wc_lo", [P, CB * TAPS * P], F32R)
        m.wout = sb("wout", [P, DI // P, D])
        m.router_w = sb("router_w", [P, E])
        m.cols = sb("cols", [P, N_COLS])
        m.rows = sb("rows", [P, N_ROWS])
        m.a_neg = sb("a_neg", [P, NH])
        m.b2q = sb("b2q", [P, D])
        m.half_sb2 = sb("half_sb2", [P, 1])
        m.ident, m.upto, m.after = sb("ident", [P, P]), sb("upto", [P, P]), sb("after", [P, P])
        m.ones, m.minus_half = sb("ones", [P, P]), sb("minus_half", [P, 2 * TPB])
        prepare_phase(nc, m, arrays)
        main_phase(nc, m, out)


_NAMES = {"L0_attn_u": "u", "L0_attn_W_in": "W_in", "L0_attn_conv_w": "conv_w", "L0_attn_conv_b": "conv_b",
          "L0_attn_dt_bias": "dt_bias", "L0_attn_A_log": "A_log", "L0_attn_D_param": "D_param",
          "L0_attn_norm_w": "norm_w", "L0_attn_W_out": "W_out", "L0_ffn_router_w": "router_w",
          "L0_ffn_router_b": "router_b", "L0_ffn_w1": "w1", "L0_ffn_b1": "b1", "L0_ffn_w2": "w2",
          "L0_ffn_b2": "b2", "L0_ffn_sw1": "sw1", "L0_ffn_sb1": "sb1", "L0_ffn_sw2": "sw2",
          "L0_ffn_sb2": "sb2"}


def kernel(**inputs):
    import numpy as _np
    import concourse.bacc as _bacc
    from concourse import mybir as _mybir
    from concourse.bass_utils import run_bass_kernel_spmd as _run

    nc = _bacc.Bacc("TRN2", target_bir_lowering=False, num_devices=1)
    arrays, aps = {}, {}
    for name, short in _NAMES.items():
        arr = _np.ascontiguousarray(inputs[name])
        arrays[f"in_{short}"] = arr
        aps[short] = nc.dram_tensor(f"in_{short}", arr.shape, _mybir.dt.from_np(arr.dtype),
                                    kind="ExternalInput").ap()
    out = nc.dram_tensor("out_x", (BATCHES, SEQ, D), _mybir.dt.float32, kind="ExternalOutput").ap()
    program(nc, aps, out)
    r = _run(nc, [arrays], core_ids=[0])
    return r.results[0]["out_x"]
```

```python
import numpy as np
import concourse.bass as bass
from concourse import mybir
from contextlib import ExitStack

F32 = mybir.dt.float32
F32R = mybir.dt.float32r
ALU = mybir.AluOpType
ACT = mybir.ActivationFunctionType
AX = mybir.AxisListType

P = 128
D = 128
BATCHES, SEQ = 8, 512
TOKENS = BATCHES * SEQ
TILES = TOKENS // P
TPB = SEQ // P
E, HE = 64, 32
ES, HS = 2, 256
TOPK = 8
EPS = 1e-5
ROUTED = E * HE // P
SHARED = ES * HS // P
BLOCKS = ROUTED + SHARED
EPB = P // HE
RING = 5
HI_LAG = 2
LAG = 5

DI = 256
NH, HD = 4, 64
NS = 128
ZW = DI
CB = (DI + 2 * NS) // P
TAPS = 4

ORDER = [("shared", ROUTED), ("shared", ROUTED + 1)]
for _r in range(ROUTED):
    if _r in (ROUTED // 2, ROUTED * 3 // 4):
        ORDER.append(("shared", ROUTED + _r // (ROUTED // 4)))
    ORDER.append(("routed", _r))


class Signal:

    def __init__(self, sem, credit):
        self.sem, self.credit = sem, credit

    def at(self, n):
        return n + (1 + self.credit)


def done(signal, n):
    return signal.sem, signal.at(n)


class Signals:

    def __init__(self, nc, ctx, phase, names, credits=()):
        self.all = {}
        for name in names:
            self.all[name] = Signal(ctx.enter_context(nc.semaphore(f"{phase}_{name}")), 0)
        for name, credit in dict(credits).items():
            self.all[name] = Signal(ctx.enter_context(nc.semaphore(f"{phase}_{name}")), credit)

    def __getitem__(self, name):
        return self.all[name]

    def give_credits(self, eng):
        for s in self.all.values():
            if s.credit:
                eng.sem_inc(s.sem, s.credit)


class Tensors:
    pass


N_COLS = BLOCKS + CB + DI // P
N_ROWS = E + 3 * NH


def prepare_phase(nc, m, a):
    with ExitStack() as ctx:
        def sb(name, shape, dt=F32):
            return ctx.enter_context(nc.sbuf_tensor(f"prep_{name}", shape, dt))

        w1_raw, w2_raw = m.w1_raw, m.w2_raw
        col_rows = sb("col_rows", [N_COLS, P])
        row_vals = sb("row_vals", [1, N_ROWS])
        sb2_rows = sb("sb2_rows", [ES, D])
        win = sb("win", [P, 2 + CB, D])
        win_dt = sb("win_dt", [NH, D])
        wout_raw = sb("wout_raw", [P, DI])
        ps = ctx.enter_context(nc.psum_tensor("prep_ps", [P, 8, 512], F32))
        s = Signals(nc, ctx, "prep", [
            "x_in", "small_in", "win_in", "zeroed", "consts", "b2q_zeroed", "b2q_in",
            "cols_ps", "cols", "rows_ps", "rows", "exp_a", "sb2_ps", "z_ps", "z_hi",
            "chan_ps", "chan_hi", "wout_ps"])

        with nc.Block() as block:
            @block.sync
            def _(sp):
                sp.dma_start(win[:, :, :], a["W_in"][0:(2 + CB) * P, :].rearrange("(b p) d -> p b d", p=P)
                             ).then_inc(s["win_in"].sem, 16)
                sp.dma_start(win_dt[:, :], a["W_in"][(2 + CB) * P:, :]).then_inc(s["win_in"].sem, 16)
                sp.dma_start(m.x[:, :].rearrange("p (t d) -> p t d", d=D),
                             a["u"].rearrange("b (t p) d -> p (b t) d", p=P)).then_inc(s["x_in"].sem, 16)

                def vals_in(lo, hi, src):
                    sp.dma_start(row_vals[0:1, lo:hi], src.rearrange("(a n) -> a n", a=1)
                                  ).then_inc(s["small_in"].sem, 16)

                vals_in(0, E, a["router_b"])
                vals_in(E, E + NH, a["dt_bias"])
                vals_in(E + NH, E + 2 * NH, a["A_log"])
                vals_in(E + 2 * NH, N_ROWS, a["D_param"])
                sp.dma_start(sb2_rows[:, :], a["sb2"]).then_inc(s["small_in"].sem, 16)
                sp.dma_start(w1_raw[:, 0:ROUTED * P].rearrange("p (e h) -> p e h", h=HE),
                              a["w1"].rearrange("e d h -> d e h")).then_inc(m.w1_in, 16)
                sp.dma_start(w1_raw[:, ROUTED * P:].rearrange("p (e h) -> p e h", h=HS),
                              a["sw1"].rearrange("e d h -> d e h")).then_inc(m.w1_in, 16)
                sp.dma_start(w2_raw[:, 0:ROUTED * P].rearrange("p (b d) -> p b d", d=D),
                             a["w2"].rearrange("e h d -> (e h) d").rearrange("(b p) d -> p b d", p=P)
                             ).then_inc(m.w2_in, 16)
                sp.dma_start(w2_raw[:, ROUTED * P:].rearrange("p (b d) -> p b d", d=D),
                             a["sw2"].rearrange("e h d -> (e h) d").rearrange("(b p) d -> p b d", p=P)
                             ).then_inc(m.w2_in, 16)
                sp.wait_ge(s["x_in"].sem, 16)
                sp.wait_ge(s["b2q_in"].sem, 64)

            @block.scalar
            def _(act):
                act.dma_start(m.conv_w[:, :, :], a["conv_w"].rearrange("(b p) o k -> p b (o k)", p=P)
                              ).then_inc(s["small_in"].sem, 16)
                act.dma_start(m.router_w[:, :], a["router_w"]).then_inc(s["small_in"].sem, 16)

                def rows_in(lo, hi, src):
                    act.dma_start(col_rows[lo:hi, :], src).then_inc(s["small_in"].sem, 16)

                rows_in(0, ROUTED, a["b1"].rearrange("(b e) h -> b (e h)", e=EPB))
                rows_in(ROUTED, BLOCKS, a["sb1"].rearrange("e (b h) -> (e b) h", h=P))
                rows_in(BLOCKS, BLOCKS + CB, a["conv_b"].rearrange("(b p) -> b p", p=P))
                rows_in(BLOCKS + CB, N_COLS, a["norm_w"].rearrange("(b p) -> b p", p=P))

                act.dma_start(wout_raw[:, :], a["W_out"]).then_inc(s["small_in"].sem, 16)
                act.wait_ge(s["z_ps"].sem, 1)
                nc.scalar.activation(m.wz_hi[:, :], ps[:, 2, 0:ZW + NH], ACT.Copy).then_inc(s["z_hi"].sem, 1)
                act.wait_ge(s["chan_ps"].sem, 1)
                nc.scalar.activation(m.wc_hi[:, :], ps[:, 3, :], ACT.Copy
                                     ).then_inc(s["chan_hi"].sem, 1)
                act.wait_ge(s["cols_ps"].sem, 1)
                nc.scalar.activation(m.cols[:, :], ps[:, 0, 0:N_COLS], ACT.Copy).then_inc(s["cols"].sem, 1)
                act.wait_ge(s["rows_ps"].sem, 1)
                nc.scalar.activation(m.rows[:, :], ps[:, 1, 0:N_ROWS], ACT.Copy).then_inc(s["rows"].sem, 1)
                act.wait_ge(s["rows"].sem, 1)
                nc.scalar.activation(m.a_neg[:, :], m.rows[:, E + NH:E + 2 * NH], ACT.Exp
                                     ).then_inc(s["exp_a"].sem, 1)

            @block.gpsimd
            def _(pool):
                nc.gpsimd.memset(m.b2q[:, :], 0.0).then_inc(s["b2q_zeroed"].sem, 1)
                nc.gpsimd.memset(m.minus_half[:, :], -0.5)
                nc.gpsimd.memset(m.ones[:, :], 1.0).then_inc(s["zeroed"].sem, 1)
                pool.wait_ge(s["zeroed"].sem, 1)
                nc.gpsimd.affine_select(out=m.ident[:, :], in_=m.ones[:, :], compare_op=ALU.is_equal,
                                        fill=0.0, base=0, pattern=[[-1, P]], channel_multiplier=1
                                        ).then_inc(s["consts"].sem, 1)
                nc.gpsimd.affine_select(out=m.upto[:, :], in_=m.ones[:, :], compare_op=ALU.is_ge,
                                        fill=0.0, base=0, pattern=[[1, P]], channel_multiplier=-1
                                        ).then_inc(s["consts"].sem, 1)
                nc.gpsimd.affine_select(out=m.after[:, :], in_=m.ones[:, :], compare_op=ALU.is_gt,
                                        fill=0.0, base=0, pattern=[[-1, P]], channel_multiplier=1
                                        ).then_inc(s["consts"].sem, 1)
                pool.wait_ge(s["b2q_zeroed"].sem, 1)
                b2_v = a["b2"].rearrange("(j q) d -> q j d", q=4)
                for q in range(4):
                    pool.dma_start(m.b2q[32 * q:32 * q + E // 4, :], b2_v[q, :, :]
                                   ).then_inc(s["b2q_in"].sem, 16)

            @block.tensor
            def _(pe):
                pe.wait_ge(s["consts"].sem, 3)
                pe.wait_ge(s["win_in"].sem, 32)
                for b in range(ZW // P):
                    nc.tensor.transpose(ps[:, 2, b * P:(b + 1) * P], win[:, b, :], m.ident[:, :])
                nc.tensor.transpose(ps[:, 2, ZW:ZW + NH], win_dt[:, :], m.ident[0:NH, 0:NH]
                                    ).then_inc(s["z_ps"].sem, 1)
                for b in range(CB):
                    last = nc.tensor.transpose(ps[:, 3, b * P:(b + 1) * P], win[:, 2 + b, :], m.ident[:, :])
                last.then_inc(s["chan_ps"].sem, 1)
                pe.wait_ge(s["small_in"].sem, 16 * 12)
                nc.tensor.transpose(ps[:, 0, 0:N_COLS], col_rows[:, :], m.ident[0:N_COLS, 0:N_COLS]
                                    ).then_inc(s["cols_ps"].sem, 1)
                nc.tensor.matmul(ps[:, 1, 0:N_ROWS], m.ones[0:1, :], row_vals[:, :], start=True, stop=True
                                 ).then_inc(s["rows_ps"].sem, 1)
                for b in range(DI // P):
                    last = nc.tensor.transpose(ps[:, 7, b * P:(b + 1) * P], wout_raw[:, b * P:(b + 1) * P],
                                               m.ident[:, :])
                last.then_inc(s["wout_ps"].sem, 1)
                pe.wait_ge(s["cols"].sem, 1)
                nc.tensor.matmul(ps[:, 0, 0:1], sb2_rows[:, :], m.ones[0:ES, 0:1], start=True, stop=True
                                 ).then_inc(s["sb2_ps"].sem, 1)

            @block.vector
            def _(dve):
                dve.wait_ge(s["z_hi"].sem, 1)
                nc.vector.tensor_tensor(m.wz_lo[:, :], ps[:, 2, 0:ZW + NH], m.wz_hi[:, :].bitcast(F32),
                                        ALU.subtract)
                dve.wait_ge(s["chan_hi"].sem, 1)
                nc.vector.tensor_tensor(m.wc_lo[:, :], ps[:, 3, :], m.wc_hi[:, :].bitcast(F32),
                                        ALU.subtract)
                dve.wait_ge(s["exp_a"].sem, 1)
                nc.vector.tensor_scalar(m.a_neg[:, :], m.a_neg[:, :], -1.0, None, ALU.mult)
                dve.wait_ge(s["wout_ps"].sem, 1)
                dve.wait_ge(s["cols"].sem, 1)
                for b in range(DI // P):
                    c = BLOCKS + CB + b
                    nc.vector.tensor_scalar(m.wout[:, b, :], ps[:, 7, b * P:(b + 1) * P],
                                            m.cols[:, c:c + 1], None, ALU.mult)
                dve.wait_ge(s["sb2_ps"].sem, 1)
                nc.vector.tensor_scalar(m.half_sb2[:, :], ps[:, 0, 0:1], 0.5, None, ALU.mult)


SLOTS = 2 * BLOCKS
TAIL = LAG + 3
FILL_AT = [16, 17, 6, 9, 11, 13]
FILLS = 2 + CB
FILL_BANK = "daadac"
SEG_BANK = "cdac"
TILE_SLOTS = 4
AT = dict(w1_hi=0, w1_lo=6, w2_hi=9, w2_lo=12, weights_used=39,
          stats=34, moments=35, rstd=36, xn=38,
          xnT=2, xT_lo=3, dt=6, neg_abs=7, softplus=13, time=13, sums=17,
          taps=[1, 1, 2], conv_silu=4,
          seg_rhs=[15, 15, 16, 16], seg=[18, 18, 18, 19], decays=18,
          pre=20, mix=21, main=23, y=23, state_dec=21, yT=26, rms=27, out=28,
          r_stats0=1, r_stats1=1, r_moments=1, r_rstd=2, r_xn0=5, r_xn1=4, r_xnT0=8, r_xnT1=8,
          logits=10, peak=10, shifted=10, exp=12,
          top0=19, rest0=20, top_probs0=21, cwq0=26, cwT0=30, xn_hi0=22,
          top1=16, rest1=16, top_probs1=16, cwq1=16, cwT1=19, xn_hi1=16,
          ffn_y0=BLOCKS + LAG, ffn_y1=2 * BLOCKS + LAG)
AT_END = dict(AT, xn_hi1=9, cwT1=21)
USES = {
    "a": [(name, "ssm") for name in ("xnT", "fill2", "fill4", "fill1", "seg2",
                                     "state0", "state1", "out0", "state2", "out1", "out2", "out3")],
    "b": [("sums", "ssm"), ("cwT1", "router1"), ("ffn_yT0", "ffn0"), ("cwT0", "router0"),
          ("ffn_yT1", "ffn1")],
    "c": [("r_xnT1", "router1"), ("logits", "router")] + [
        (name, "ssm") for name in ("fill5", "seg0", "seg3", "tok0", "tok1", "yT0", "tok2", "yT1", "tok3", "yT2", "yT3")],
    "d": [("dt", "ssm"), ("r_xnT0", "router0")] + [
        (name, "ssm") for name in ("fill3", "fill0", "seg1", "y0", "y1", "y2", "y3")],
}


def parts(i):
    p = {"ssm": 0 <= i < BATCHES, "router0": i + 2 < BATCHES, "router1": i >= 1,
         "ffn0": 0 <= i + 1 < BATCHES, "ffn1": i >= 1,
         "first": i == -2}
    p["router"] = p["router0"] or p["router1"]
    return p


def counts(i):
    p = parts(i)
    ffns = p["ffn0"] + p["ffn1"]
    return {"blocks": ffns * BLOCKS, "gates": ffns * ROUTED, "shared": ffns * SHARED, "runs": ffns,
            **{bank: sum(p[part] for _, part in USES[bank]) for bank in USES}}


class Iteration:

    def __init__(self, eng, like, i=None):
        self.i = like if i is None else i
        self.has = parts(like)
        self.at = AT_END if like >= BATCHES - 1 else AT
        self.sides = [side for side in range(2) if self.has[f"router{side}"]]
        self.uses = {bank: [name for name, part in USES[bank] if self.has[part]] for bank in USES}

        def before(kind):
            size, count = counts(like)[kind], sum(counts(k)[kind] for k in range(-2, like))
            return count if i is None else eng.snap(i * size + (count - like * size))

        self.blocks, self.runs = before("blocks"), before("runs")
        self.gates, self.before_shared = before("gates"), before("shared")
        self.used = {bank: before(bank) for bank in USES}

    def block(self, n):
        if 0 <= n < 2 * BLOCKS and self.has[f"ffn{n // BLOCKS}"]:
            side = n // BLOCKS
            return n % BLOCKS, self.blocks + (n if self.has["ffn0"] else n - BLOCKS), side
        return None

    def gate(self, n):
        k, _, side = self.block(n)
        before = ROUTED if side and self.has["ffn0"] else 0
        return self.gates + (before + sum(kind == "routed" for kind, _ in ORDER[:k]))

    def shared(self, n):
        k, _, side = self.block(n)
        before = SHARED if side and self.has["ffn0"] else 0
        return self.before_shared + (before + sum(kind == "shared" for kind, _ in ORDER[:k]))

    def run(self, side):
        return self.runs + (1 if side and self.has["ffn0"] else 0)

    def last_block(self, side):
        return self.blocks + (BLOCKS * (1 + (side and self.has["ffn0"])) - 1)

    def ffn_batch(self, side):
        return self.i - 1 if side else self.i + 1

    def router_batch(self, side):
        return self.i - 1 if side else self.i + 2

    def ssm_tile(self, t):
        return self.i * TPB + t

    def use(self, bank, name):
        return self.used[bank] + self.uses[bank].index(name)


def main_phase(nc, m, out):
    with ExitStack() as ctx:
        def sb(name, shape, dt=F32):
            return ctx.enter_context(nc.sbuf_tensor(name, shape, dt))

        def bank(name):
            return ctx.enter_context(nc.psum_tensor(name, [P, 512], F32))

        xn_hi, xn_lo = sb("xn_hi", [P, 2, SEQ], F32R), sb("xn_lo", [P, 2, SEQ], F32R)
        weights = sb("weights", [P, 2, SEQ])
        hidden, hid_hi, hid_lo = m.hidden, m.hid_hi, m.hid_lo
        ffn_y = sb("ffn_y", [P, SEQ])
        r_stats = sb("r_stats", [P, 2 * TPB, 6])
        r_moments = sb("r_moments", [P, 2 * TPB, 2])
        r_var = sb("r_var", [P, 2 * TPB])
        r_rstd = sb("r_rstd", [P, 2 * TPB])
        r_xn = sb("r_xn", [P, 2, TPB, D])
        r_xT = sb("r_xT", [P, 2, SEQ])
        logits = sb("logits_sb", [P, 2 * TPB, E])
        peak = sb("peak", [P, 2 * TPB])
        probs = sb("probs", [P, 2 * TPB, E])
        top = sb("top", [P, 2 * TPB, TOPK])
        rest = sb("rest", [P, 2 * TPB, E])
        top_sum = sb("top_sum", [P, 2 * TPB])
        top_inv = sb("top_inv", [P, 2 * TPB])
        cwq = sb("cwq", [P, 2 * TPB, 4, 32])
        stats = sb("stats", [P, TPB, 6])
        moments = sb("moments", [P, TPB, 2])
        var_eps = sb("var_eps", [P, TPB])
        rstd = sb("rstd", [P, TPB])
        xn = sb("xn", [P, TPB, D])
        xT_hi, xT_lo = sb("xT_hi", [P, SEQ], F32R), sb("xT_lo", [P, SEQ], F32R)
        chan = m.gate_chan[:, 0:CB * SEQ].rearrange("p (c n) -> p c n", c=CB)
        gate = m.gate_chan[:, CB * SEQ:].rearrange("p (t c) -> p t c", t=TPB)
        dt_raw = sb("dt_raw", [P, TPB * NH])
        neg_abs, exp_na, u = sb("neg_abs", [P, TPB * NH]), sb("exp_na", [P, TPB * NH]), sb("u", [P, TPB * NH])
        u_err, u_inv, ln_u = sb("u_err", [P, TPB * NH]), sb("u_inv", [P, TPB * NH]), sb("ln_u", [P, TPB * NH])
        dt, dA = sb("dt", [P, TPB, NH]), sb("dA", [P, TPB, NH])
        decay = sb("decay", [P, 3, TPB, NH])
        dt_after = sb("dt_after", [P, TPB, NH])
        seg_rhs = sb("seg_rhs", [P, TPB, NH, P])
        seg = sb("seg", [P, TPB, NH, P])
        cb_mask = sb("cb_mask", [P, 2, P])
        mix = sb("mix", [P, 2, NH, P])
        tok = sb("tok", [P, 2, DI + NS + P])
        dx, dx_after = sb("dx", [P, 2, DI]), sb("dx_after", [P, 2, DI])
        skip, y_in, y = sb("skip", [P, 2, DI]), sb("y_in", [P, DI]), sb("y", [P, 2, DI])
        square = sb("square", [P, DI])
        sum_sq, mean_sq, inv_rms = sb("sum_sq", [P, TPB]), sb("mean_sq", [P, TPB]), sb("inv_rms", [P, TPB])
        yT = sb("yT", [P, 2, DI])
        state, state_dec = sb("state", [P, 2, DI]), sb("state_dec", [P, DI])

        up_ps = [bank("up0_ps"), bank("up1_ps")]
        acc_ps, cw_ps = bank("acc_ps"), bank("cw_ps")
        a_ps, b_ps, c_ps, d_ps = bank("a_ps"), bank("b_ps"), bank("c_ps"), bank("d_ps")
        shared = {"a": a_ps, "b": b_ps, "c": c_ps, "d": d_ps}

        s = Signals(nc, ctx, "main", [
            "dve_held", "pool_held",
            "zeroed", "w1_hi", "w1_lo", "w2_hi", "w2_lo",
            "up_ready", "hi_routed", "hi_shared", "shuffled", "stored",
            "a_ready", "b_ready", "c_ready", "d_ready",
            "r_stats0", "r_stats1", "r_moments", "r_var", "r_rstd", "r_xn0", "r_xn1", "xn_hi0", "xn_hi1",
            "xn_lo0", "xn_lo1", "weights0", "weights1",
            "logits", "peak", "shifted", "probs",
            "top0", "top1", "rest0", "rest1", "top_sum0", "top_sum1", "top_inv0", "top_inv1",
            "top_probs0", "top_probs1",
            "cwq0", "cwq1",
            "stats", "moments", "var_eps", "rstd", "xn", "xT_hi",
            "tap0", "tap", "chan",
            "neg_abs", "exp_na", "ln_u", "u", "u_inv", "u_fix", "ln1p", "dt", "dA", "dt_after",
            "seg_rhs", "dx", "dx_after", "skip", "cb_mask", "mix", "state", "y_sum", "yg", "state_dec",
            "mean_sq", "inv_rms", "x_updated"],
            {"silu_done": 2, "gated": 1, "lo_routed": ROUTED, "lo_shared": SHARED, "down_done": RING, "ffn_y": 1,
             "a_read": 1, "b_read": 1, "c_read": 1, "d_read": 1, "sum_sq": 1})

        out_v = out.rearrange("b (t p) d -> b p t d", p=P)

        def heads(ap):
            return ap.unsqueeze(2).to_broadcast([P, NH, HD])

        def by_head(ap):
            return ap.rearrange("p (h d) -> p h d", h=NH)

        def x_of(b, t):
            return m.x[:, bass.ds(b * SEQ + t * D, D)]

        def x_batch(b):
            return m.x[:, bass.ds(b * SEQ, SEQ)]

        def tiles_of(it):
            return slice(it.sides[0] * TPB, (it.sides[-1] + 1) * TPB)

        def tile_at(n, at):
            t, odd = divmod(n - at, TILE_SLOTS)
            return t if not odd and 0 <= t < TPB else None

        def routed(it, n):
            return it.block(n) is not None and ORDER[it.block(n)[0]][0] == "routed"

        def part(name, it, n):
            if routed(it, n):
                return done(s[name + "_routed"], it.gate(n))
            return done(s[name + "_shared"], it.shared(n))

        def in_ring_before(name, it, n):
            if ORDER[(n - RING) % BLOCKS][0] == "routed":
                k = sum(kind == "routed" for kind, _ in ORDER[:n % BLOCKS])
                back = sum(ORDER[(n - r) % BLOCKS][0] == "routed" for r in range(1, RING + 1))
                side = n // BLOCKS
                first = it.gates + (ROUTED if side and it.has["ffn0"] else 0)
                return done(s[name + "_routed"], first + (k - back))
            k = sum(kind == "shared" for kind, _ in ORDER[:n % BLOCKS])
            back = sum(ORDER[(n - r) % BLOCKS][0] == "shared" for r in range(1, RING + 1))
            first = it.before_shared + (SHARED if n // BLOCKS and it.has["ffn0"] else 0)
            return done(s[name + "_shared"], first + (k - back))

        def iterations(eng, step):
            def run(it, prev):
                for n in range(SLOTS):
                    if prev and n < TAIL:
                        step(prev, SLOTS + n)
                    step(it, n)

            first, last = 2, BATCHES - 3
            prev = None
            for i in range(-2, first):
                it = Iteration(eng, i)
                run(it, prev)
                prev = it
            with eng.Fori(first, last + 1) as i:
                run(Iteration(eng, first, i), Iteration(eng, first, i - 1))
            prev = Iteration(eng, last)
            for i in range(last + 1, BATCHES + 1):
                it = Iteration(eng, i)
                run(it, prev)
                prev = it
            for n in range(TAIL):
                step(prev, SLOTS + n)

        with nc.Block() as block:
            @block.sync
            def _(sp):
                def step(it, n):
                    if n == it.at["ffn_y1"] + 2 and it.has["ffn1"]:
                        sp.wait_ge(*done(s["x_updated"], it.run(1)))
                        sp.dma_start(out_v[it.ffn_batch(1)], x_batch(it.ffn_batch(1)).rearrange(
                            "p (t d) -> p t d", d=D)).then_inc(s["stored"].sem, 16)

                iterations(sp, step)
                sp.wait_ge(s["stored"].sem, 16 * BATCHES)

            @block.tensor
            def _(pe):
                def up(it, n):
                    k, i, side = it.block(n)
                    j = ORDER[k][1]
                    wh, wl = m.w1_hi[:, j * P:(j + 1) * P], m.w1_lo[:, j * P:(j + 1) * P]
                    if k == 0:
                        pe.wait_ge(*done(s[f"xn_lo{side}"], it.ffn_batch(side)))
                    pe.wait_ge(*done(s["silu_done"], i - 2))
                    o = up_ps[n % 2][:, :]
                    nc.tensor.matmul(o, wh, xn_hi[:, side, :], start=True, stop=False)
                    nc.tensor.matmul(o, wh, xn_lo[:, side, :], start=False, stop=False)
                    nc.tensor.matmul(o, wl, xn_hi[:, side, :], start=False, stop=True
                                     ).then_inc(s["up_ready"].sem, 1)

                def down(it, n):
                    k, i, side = it.block(n)
                    j = ORDER[k][1]
                    wh, wl = m.w2_hi[:, j * P:(j + 1) * P], m.w2_lo[:, j * P:(j + 1) * P]
                    if k == 0:
                        pe.wait_ge(*done(s[f"weights{side}"], it.ffn_batch(side)))
                        pe.wait_ge(*done(s["ffn_y"], it.run(side) - 1))
                        nc.tensor.matmul(acc_ps[:, :], m.b2q[:, :], weights[:, side, :],
                                         start=True, stop=False)
                    pe.wait_ge(*part("lo", it, n))
                    nc.tensor.matmul(acc_ps[:, :], wh, hid_hi[:, n % RING, :], start=False, stop=False)
                    nc.tensor.matmul(acc_ps[:, :], wh, hid_lo[:, n % RING, :], start=False, stop=False)
                    nc.tensor.matmul(acc_ps[:, :], wl, hid_hi[:, n % RING, :], start=False,
                                     stop=k == BLOCKS - 1).then_inc(s["down_done"].sem, 1)

                def bank_free(it, bank, name):
                    pe.wait_ge(*done(s[bank + "_read"], it.use(bank, name) - 1))

                def transposed(o, tiles, sem):
                    for t, tile in enumerate(tiles):
                        last = nc.tensor.transpose(o[:, t * P:(t + 1) * P], tile, m.ident[:, :])
                    last.then_inc(sem, 1)

                def router(it, n):
                    for side in it.sides:
                        if n == it.at[f"r_xnT{side}"]:
                            bank_free(it, "dc"[side], f"r_xnT{side}")
                            pe.wait_ge(*done(s[f"r_xn{side}"], it.router_batch(side)))
                            transposed(c_ps if side else d_ps, [r_xn[:, side, t, :] for t in range(TPB)],
                                       s["dc"[side] + "_ready"].sem)
                        if n == it.at[f"cwT{side}"]:
                            bank_free(it, "b", f"cwT{side}")
                            pe.wait_ge(*done(s[f"cwq{side}"], it.router_batch(side)))
                            transposed(b_ps, [cwq[:, side * TPB + t, :, :].rearrange("p q j -> p (q j)")
                                              for t in range(TPB)], s["b_ready"].sem)
                    if it.sides and n == it.at["logits"]:
                        bank_free(it, "c", "logits")
                        for side in it.sides:
                            pe.wait_ge(*done(s["dc"[side] + "_read"], it.use("dc"[side], f"r_xnT{side}")))
                        for side in it.sides:
                            for t in range(TPB):
                                o = (side * TPB + t) * E
                                last = nc.tensor.matmul(c_ps[:, o:o + E], r_xT[:, side, t * P:(t + 1) * P],
                                                        m.router_w[:, :], start=True, stop=True)
                        last.then_inc(s["c_ready"].sem, 1)

                def fill(it, f):
                    bank = FILL_BANK[f]
                    ps = shared[bank]
                    bank_free(it, bank, f"fill{f}")
                    if f < 2:
                        for i in range(2):
                            c = slice((2 * f + i) * P, (2 * f + i + 1) * P)
                            o = ps[:, i * ZW:(i + 1) * ZW]
                            nc.tensor.matmul(o, xT_hi[:, c], m.wz_hi[:, 0:ZW], start=True, stop=False)
                            nc.tensor.matmul(o, xT_lo[:, c], m.wz_hi[:, 0:ZW], start=False, stop=False)
                            last = nc.tensor.matmul(o, xT_hi[:, c], m.wz_lo[:, 0:ZW], start=False, stop=True)
                    else:
                        w = slice((f - 2) * P, (f - 1) * P)
                        nc.tensor.matmul(ps[:, :], m.wc_hi[:, w], xT_hi[:, :], start=True, stop=False)
                        nc.tensor.matmul(ps[:, :], m.wc_hi[:, w], xT_lo[:, :], start=False, stop=False)
                        last = nc.tensor.matmul(ps[:, :], m.wc_lo[:, w], xT_hi[:, :], start=False, stop=True)
                    last.then_inc(s[bank + "_ready"].sem, 1)

                def ssm(it, n):
                    b = it.i
                    if n == it.at["xnT"]:
                        bank_free(it, "a", "xnT")
                        pe.wait_ge(*done(s["xn"], b))
                        transposed(a_ps, [xn[:, t, :] for t in range(TPB)], s["a_ready"].sem)
                    if n == it.at["dt"]:
                        bank_free(it, "d", "dt")
                        pe.wait_ge(*done(s["a_read"], it.use("a", "xnT")))
                        for t in range(TPB):
                            c = slice(t * P, (t + 1) * P)
                            o = d_ps[:, t * NH:(t + 1) * NH]
                            nc.tensor.matmul(o, xT_hi[:, c], m.wz_hi[:, ZW:], start=True, stop=False)
                            nc.tensor.matmul(o, xT_lo[:, c], m.wz_hi[:, ZW:], start=False, stop=False)
                            last = nc.tensor.matmul(o, xT_hi[:, c], m.wz_lo[:, ZW:], start=False, stop=True)
                        last.then_inc(s["d_ready"].sem, 1)
                    for f in range(FILLS):
                        if n == FILL_AT[f]:
                            fill(it, f)
                    if n == it.at["sums"]:
                        bank_free(it, "b", "sums")
                        pe.wait_ge(*done(s["dA"], b))
                        dA16 = dA[:, :, :].rearrange("p t h -> p (t h)")
                        for i, w in enumerate((m.upto, m.after, m.ones)):
                            last = nc.tensor.matmul(b_ps[:, i * TPB * NH:(i + 1) * TPB * NH], w[:, :], dA16,
                                                    start=True, stop=True)
                        last.then_inc(s["b_ready"].sem, 1)
                    for t in range(TPB):
                        if n == it.at["seg"][t]:
                            bank = SEG_BANK[t]
                            bank_free(it, bank, f"seg{t}")
                            pe.wait_ge(*done(s["seg_rhs"], it.ssm_tile(t)))
                            nc.tensor.matmul(shared[bank][:, :], m.after[:, :],
                                             seg_rhs[:, t, :, :].rearrange("p h t -> p (h t)"),
                                             start=True, stop=True).then_inc(s[bank + "_ready"].sem, 1)
                    t = tile_at(n, it.at["pre"])
                    if t is not None:
                        c = slice(t * P, (t + 1) * P)
                        bank_free(it, "c", f"tok{t}")
                        pe.wait_ge(*done(s["chan"], it.i * CB + (CB - 1)))
                        for i in range(3):
                            nc.tensor.transpose(c_ps[:, i * P:(i + 1) * P], chan[:, i, c], m.ident[:, :])
                        nc.tensor.matmul(c_ps[:, 3 * P:], chan[:, 2, c], chan[:, 3, c], start=True, stop=True
                                         ).then_inc(s["c_ready"].sem, 1)
                    t = tile_at(n, it.at["main"])
                    if t is not None:
                        main(it, t)
                    t = tile_at(n, it.at["yT"])
                    if t is not None:
                        bank_free(it, "c", f"yT{t}")
                        pe.wait_ge(*done(s["yg"], it.ssm_tile(t)))
                        transposed(c_ps, [y[:, t % 2, i * P:(i + 1) * P] for i in range(DI // P)],
                                   s["c_ready"].sem)
                    t = tile_at(n, it.at["out"])
                    if t is not None:
                        bank_free(it, "a", f"out{t}")
                        pe.wait_ge(*done(s["c_read"], it.use("c", f"yT{t}")))
                        for i in range(DI // P):
                            last = nc.tensor.matmul(a_ps[:, 0:D], yT[:, t % 2, i * P:(i + 1) * P],
                                                    m.wout[:, i, :], start=i == 0, stop=i == DI // P - 1)
                        last.then_inc(s["a_ready"].sem, 1)

                def main(it, t):
                    c = slice(t * P, (t + 1) * P)
                    if t < TPB - 1:
                        bank_free(it, "a", f"state{t}")
                        pe.wait_ge(*done(s["dx_after"], it.i * (TPB - 1) + t))
                        nc.tensor.matmul(a_ps[:, 0:DI], tok[:, t % 2, DI:DI + NS], dx_after[:, t % 2, :],
                                         start=True, stop=True).then_inc(s["a_ready"].sem, 1)
                    bank_free(it, "d", f"y{t}")
                    if t:
                        pe.wait_ge(*done(s["state"], it.i * (TPB - 1) + (t - 1)))
                        nc.tensor.matmul(d_ps[:, DI:], chan[:, 3, c], state[:, (t - 1) % 2, :],
                                         start=True, stop=True)
                    pe.wait_ge(*done(s["dx"], it.ssm_tile(t)))
                    pe.wait_ge(*done(s["mix"], it.ssm_tile(t)))
                    for h in range(NH):
                        last = nc.tensor.matmul(d_ps[:, h * HD:(h + 1) * HD], mix[:, t % 2, h, :],
                                                dx[:, t % 2, h * HD:(h + 1) * HD], start=True, stop=True)
                    last.then_inc(s["d_ready"].sem, 1)

                def step(it, n):
                    if it.has["first"] and n == it.at["weights_used"]:
                        pe.wait_ge(*done(s["w1_lo"], 0))
                        pe.wait_ge(*done(s["w2_lo"], 0))
                    if it.block(n):
                        up(it, n)
                    if it.has["ssm"]:
                        ssm(it, n)
                    router(it, n)
                    for side in range(2):
                        if n == it.at[f"ffn_y{side}"] + 2 and it.has[f"ffn{side}"]:
                            bank_free(it, "b", f"ffn_yT{side}")
                            pe.wait_ge(*done(s["ffn_y"], it.run(side)))
                            transposed(b_ps, [ffn_y[:, t * P:(t + 1) * P] for t in range(TPB)],
                                       s["b_ready"].sem)
                    if it.block(n - LAG):
                        down(it, n - LAG)

                iterations(pe, step)

            @block.scalar
            def _(act):
                def exps(it):
                    nc.scalar.preload_act_table_set("natural_log_exp_and_others")
                    if it.sides:
                        r = tiles_of(it)
                        act.wait_ge(*done(s["shifted"], it.i + 2))
                        nc.scalar.activation(probs[:, r, :], logits[:, r, :], ACT.Exp
                                             ).then_inc(s["probs"].sem, 1)
                    if it.has["ssm"]:
                        act.wait_ge(*done(s["neg_abs"], it.i))
                        nc.scalar.activation(exp_na[:, :], neg_abs[:, :], ACT.Exp).then_inc(s["exp_na"].sem, 1)
                        act.wait_ge(*done(s["exp_na"], it.i))
                        nc.scalar.activation(ln_u[:, :], exp_na[:, :], ACT.Ln, bias=1.0
                                             ).then_inc(s["ln_u"].sem, 1)
                    nc.scalar.preload_act_table(ACT.Silu)

                def decays(it):
                    nc.scalar.preload_act_table(ACT.Exp)
                    act.wait_ge(*done(s["b_ready"], it.use("b", "sums")))
                    nc.scalar.activation(decay[:, :, :, :].rearrange("p i t h -> p (i t h)"),
                                         b_ps[:, 0:3 * TPB * NH], ACT.Exp).then_inc(s["b_read"].sem, 1)
                    for t in range(TPB):
                        bank = SEG_BANK[t]
                        act.wait_ge(*done(s[bank + "_ready"], it.use(bank, f"seg{t}")))
                        nc.scalar.activation(seg[:, t, :, :].rearrange("p h t -> p (h t)"),
                                             shared[bank][:, :], ACT.Exp
                                             ).then_inc(s[bank + "_read"].sem, 1)
                    nc.scalar.preload_act_table(ACT.Silu)

                def router(it, n):
                    for side in it.sides:
                        batch = it.router_batch(side)
                        if n == it.at[f"r_xnT{side}"]:
                            bank = "dc"[side]
                            act.wait_ge(*done(s[bank + "_ready"], it.use(bank, f"r_xnT{side}")))
                            nc.scalar.activation(r_xT[:, side, :], (c_ps if side else d_ps)[:, :], ACT.Copy
                                                 ).then_inc(s[bank + "_read"].sem, 1)
                        if n == it.at[f"xn_hi{side}"]:
                            act.wait_ge(*done(s["dc"[side] + "_read"], it.use("dc"[side], f"r_xnT{side}")))
                            nc.scalar.activation(xn_hi[:, side, :], r_xT[:, side, :], ACT.Copy
                                                 ).then_inc(s[f"xn_hi{side}"].sem, 1)
                        if n == it.at[f"cwT{side}"]:
                            act.wait_ge(*done(s["b_ready"], it.use("b", f"cwT{side}")))
                            nc.scalar.activation(weights[:, side, :], b_ps[:, :], ACT.Copy
                                                 ).then_inc(s[f"weights{side}"].sem, 1)
                            act.wait_ge(*done(s[f"weights{side}"], batch))
                            act.sem_inc(s["b_read"].sem, 1)

                def ssm(it, n):
                    if n == it.at["xnT"]:
                        act.wait_ge(*done(s["a_ready"], it.use("a", "xnT")))
                        nc.scalar.activation(xT_hi[:, :], a_ps[:, :], ACT.Copy).then_inc(s["xT_hi"].sem, 1)
                    for f in range(FILLS):
                        bank, ps = FILL_BANK[f], shared[FILL_BANK[f]]
                        if n == FILL_AT[f]:
                            act.wait_ge(*done(s[bank + "_ready"], it.use(bank, f"fill{f}")))
                            if f < 2:
                                nc.scalar.activation(gate[:, 2 * f:2 * f + 2, :].rearrange("p t c -> p (t c)"),
                                                     ps[:, :], ACT.Silu).then_inc(s[bank + "_read"].sem, 1)
                            else:
                                c = BLOCKS + f - 2
                                nc.scalar.activation(chan[:, f - 2, :], ps[:, :], ACT.Identity,
                                                     bias=m.cols[:, c:c + 1],
                                                     scale=m.conv_w[:, f - 2, TAPS - 1:TAPS]
                                                     ).then_inc(s["tap0"].sem, 1)
                        if f >= 2 and n == FILL_AT[f] + it.at["conv_silu"]:
                            act.wait_ge(*done(s[bank + "_read"], it.use(bank, f"fill{f}")))
                            nc.scalar.activation(chan[:, f - 2, :], chan[:, f - 2, :], ACT.Silu
                                                 ).then_inc(s["chan"].sem, 1)
                    t = tile_at(n, it.at["pre"])
                    if t is not None:
                        if t >= 2:
                            act.wait_ge(*done(s["skip"], it.ssm_tile(t - 2)))
                        act.wait_ge(*done(s["c_ready"], it.use("c", f"tok{t}")))
                        nc.scalar.activation(tok[:, t % 2, :], c_ps[:, :], ACT.Copy).then_inc(s["c_read"].sem, 1)
                    t = tile_at(n, it.at["yT"])
                    if t is not None:
                        act.wait_ge(*done(s["sum_sq"], it.ssm_tile(t - 1)))
                        act.wait_ge(*done(s["c_ready"], it.use("c", f"yT{t}")))
                        nc.scalar.activation(yT[:, t % 2, :], c_ps[:, 0:DI], ACT.Copy
                                             ).then_inc(s["c_read"].sem, 1)
                        nc.scalar.activation(square[:, :], y[:, t % 2, :], ACT.Square,
                                             accum_out=sum_sq[:, t:t + 1]).then_inc(s["sum_sq"].sem, 1)

                def step(it, n):
                    if it.has["first"] and n == it.at["w1_hi"]:
                        act.wait_ge(m.w1_in, 32)
                        nc.scalar.activation(m.w1_hi[:, :], m.w1_raw, ACT.Copy).then_inc(s["w1_hi"].sem, 1)
                    if it.has["first"] and n == it.at["w2_hi"]:
                        act.wait_ge(m.w2_in, 32)
                        nc.scalar.activation(m.w2_hi[:, :], m.w2_raw, ACT.Copy).then_inc(s["w2_hi"].sem, 1)
                    for side in range(2):
                        if n == it.at[f"ffn_y{side}"] and it.has[f"ffn{side}"]:
                            act.wait_ge(*done(s["down_done"], it.last_block(side)))
                            nc.scalar.activation(ffn_y[:, :], acc_ps[:, :], ACT.Identity,
                                                 bias=m.half_sb2[:, 0:1], scale=0.5).then_inc(s["ffn_y"].sem, 1)
                    if it.block(n):
                        k, i, _ = it.block(n)
                        j = ORDER[k][1]
                        act.wait_ge(*in_ring_before("lo", it, n))
                        act.wait_ge(*done(s["up_ready"], i))
                        nc.scalar.activation(hidden[:, n % RING, :], up_ps[n % 2][:, :], ACT.Silu,
                                             bias=m.cols[:, j:j + 1]).then_inc(s["silu_done"].sem, 1)
                    if it.block(n - HI_LAG):
                        k, i, _ = it.block(n - HI_LAG)
                        if ORDER[k][0] == "routed":
                            act.wait_ge(*done(s["gated"], it.gate(n - HI_LAG)))
                        else:
                            act.wait_ge(*done(s["silu_done"], i))
                        act.wait_ge(*done(s["down_done"], i - RING))
                        nc.scalar.activation(hid_hi[:, (n - HI_LAG) % RING, :], hidden[:, (n - HI_LAG) % RING, :],
                                             ACT.Copy).then_inc(
                                                 s["hi_routed" if routed(it, n - HI_LAG) else "hi_shared"].sem, 1)
                    if n == it.at["exp"]:
                        exps(it)
                    if n == it.at["decays"] and it.has["ssm"]:
                        decays(it)
                    if it.has["ssm"]:
                        ssm(it, n)
                    router(it, n)

                iterations(act, step)

            @block.vector
            def _(dve):
                def aggregate(stats, moments, tiles, moments_done):
                    dve.sem_inc(s["dve_held"].sem, 1)
                    for t in tiles:
                        last = nc.vector.bn_aggr(moments[:, t, :], stats[:, t, :])
                    last.then_inc(moments_done.sem, 1)

                def normed(out_of, x, moments, rstd, tiles, sem):
                    for t, tile in enumerate(tiles):
                        last = nc.vector.tensor_scalar(out_of(t), x(t), moments[:, tile, 0:1],
                                                       rstd[:, tile:tile + 1], ALU.subtract, ALU.mult)
                    last.then_inc(sem, 1)

                def router(it, n):
                    r = tiles_of(it)
                    run = it.i + 2
                    for side in it.sides:
                        if n == it.at[f"r_stats{side}"]:
                            if side:
                                dve.wait_ge(*done(s["a_read"], it.used["a"] - 1))
                                dve.sem_inc(s["dve_held"].sem, 1)
                            for t in range(TPB):
                                last = nc.vector.bn_stats(r_stats[:, side * TPB + t, :],
                                                          x_of(it.router_batch(side), t))
                            last.then_inc(s[f"r_stats{side}"].sem, 1)
                    if n == it.at["r_moments"]:
                        if it.has["router0"]:
                            dve.wait_ge(*done(s["r_stats0"], it.router_batch(0)))
                        if it.has["router1"]:
                            dve.wait_ge(*done(s["r_stats1"], it.router_batch(1)))
                        aggregate(r_stats, r_moments, range(r.start, r.stop), s["r_moments"])
                    for side in it.sides:
                        if n == it.at[f"r_xn{side}"]:
                            batch = it.router_batch(side)
                            dve.wait_ge(*done(s["r_rstd"], run))
                            normed(lambda t: r_xn[:, side, t, :], lambda t: x_of(batch, t), r_moments, r_rstd,
                                   range(side * TPB, (side + 1) * TPB), s[f"r_xn{side}"].sem)
                    width = r.stop - r.start
                    if n == it.at["logits"]:
                        dve.wait_ge(*done(s["c_ready"], it.use("c", "logits")))
                        nc.vector.tensor_tensor(
                            logits[:, r, :],
                            c_ps[:, r.start * E:r.stop * E].rearrange("p (t e) -> p t e", e=E),
                            m.rows[:, 0:E].unsqueeze(1).to_broadcast([P, width, E]), ALU.add
                            ).then_inc(s["c_read"].sem, 1)
                    if n == it.at["peak"]:
                        dve.wait_ge(*done(s["c_read"], it.use("c", "logits")))
                        nc.vector.tensor_reduce(peak[:, r], logits[:, r, :], AX.X, ALU.max
                                                ).then_inc(s["peak"].sem, 1)
                    for side in it.sides:
                        tiles = range(side * TPB, (side + 1) * TPB)
                        r = slice(tiles.start, tiles.stop)
                        batch = it.router_batch(side)
                        if n == it.at[f"top{side}"]:
                            dve.wait_ge(*done(s["probs"], run))
                            dve.sem_inc(s["dve_held"].sem, 1)
                            for t in tiles:
                                last = nc.vector.max(top[:, t, :], probs[:, t, :])
                            last.then_inc(s[f"top{side}"].sem, 1)
                        if n == it.at[f"rest{side}"]:
                            dve.wait_ge(*done(s[f"top{side}"], batch))
                            dve.sem_inc(s["dve_held"].sem, 1)
                            for t in tiles:
                                last = nc.vector.match_replace(rest[:, t, :], top[:, t, :], probs[:, t, :],
                                                               0.0)
                            last.then_inc(s[f"rest{side}"].sem, 1)
                            nc.vector.tensor_reduce(top_sum[:, r], top[:, r, :], AX.X, ALU.add
                                                    ).then_inc(s[f"top_sum{side}"].sem, 1)
                            dve.wait_ge(*done(s[f"top_sum{side}"], batch))
                            nc.vector.reciprocal(top_inv[:, r], top_sum[:, r]
                                                 ).then_inc(s[f"top_inv{side}"].sem, 1)

                def softplus(b):
                    dve.wait_ge(*done(s["exp_na"], b))
                    nc.vector.tensor_scalar(u[:, :], exp_na[:, :], 1.0, None, ALU.add
                                            ).then_inc(s["u"].sem, 1)
                    dve.wait_ge(*done(s["u"], b))
                    nc.vector.scalar_tensor_tensor(u_err[:, :], u[:, :], 1.0, exp_na[:, :],
                                                   ALU.subtract, ALU.subtract)
                    nc.vector.reciprocal(u_inv[:, :], u[:, :]).then_inc(s["u_inv"].sem, 1)
                    dve.wait_ge(*done(s["u_inv"], b))
                    nc.vector.tensor_tensor(u_err[:, :], u_err[:, :], u_inv[:, :], ALU.mult
                                            ).then_inc(s["u_fix"].sem, 1)

                def time_steps(b):
                    dve.wait_ge(*done(s["u_fix"], b))
                    dve.wait_ge(*done(s["ln_u"], b))
                    nc.vector.tensor_tensor(ln_u[:, :], ln_u[:, :], u_err[:, :], ALU.subtract
                                            ).then_inc(s["ln1p"].sem, 1)
                    dve.wait_ge(*done(s["ln1p"], b))
                    nc.vector.scalar_tensor_tensor(dt[:, :, :].rearrange("p t h -> p (t h)"),
                                                   dt_raw[:, :], 0.0, ln_u[:, :], ALU.max, ALU.add
                                                   ).then_inc(s["dt"].sem, 1)
                    dve.wait_ge(*done(s["dt"], b))
                    nc.vector.tensor_tensor(dA[:, :, :], dt[:, :, :],
                                            m.a_neg[:, :].unsqueeze(1).to_broadcast([P, TPB, NH]), ALU.mult
                                            ).then_inc(s["dA"].sem, 1)

                def ssm(it, n):
                    b = it.i
                    for f in range(2, FILLS):
                        for back in range(1, TAPS):
                            if n == FILL_AT[f] + it.at["taps"][back - 1]:
                                tap(it, f, back)
                    if n == it.at["xT_lo"]:
                        dve.wait_ge(*done(s["xT_hi"], b))
                        nc.vector.tensor_tensor(xT_lo[:, :], a_ps[:, :], xT_hi[:, :].bitcast(F32),
                                                ALU.subtract).then_inc(s["a_read"].sem, 1)
                    if n == it.at["dt"]:
                        dve.wait_ge(*done(s["d_ready"], it.use("d", "dt")))
                        nc.vector.tensor_tensor(
                            dt_raw[:, :].rearrange("p (t h) -> p t h", h=NH),
                            d_ps[:, 0:TPB * NH].rearrange("p (t h) -> p t h", h=NH),
                            m.rows[:, E:E + NH].unsqueeze(1).to_broadcast([P, TPB, NH]), ALU.add
                            ).then_inc(s["d_read"].sem, 1)
                    if n == it.at["neg_abs"]:
                        dve.wait_ge(*done(s["d_read"], it.use("d", "dt")))
                        nc.vector.scalar_tensor_tensor(neg_abs[:, :], dt_raw[:, :], -1.0, dt_raw[:, :],
                                                       ALU.mult, ALU.min).then_inc(s["neg_abs"].sem, 1)
                    if n == it.at["softplus"]:
                        softplus(b)
                    if n == it.at["time"]:
                        time_steps(b)
                    t = tile_at(n, it.at["mix"])
                    if t is not None:
                        i = it.ssm_tile(t)
                        dve.wait_ge(*done(s["c_read"], it.use("c", f"tok{t}")))
                        nc.vector.tensor_tensor(cb_mask[:, t % 2, :], tok[:, t % 2, DI + NS:], m.upto[:, :],
                                                ALU.mult).then_inc(s["cb_mask"].sem, 1)
                        dve.wait_ge(*done(s["cb_mask"], i))
                        nc.vector.tensor_tensor(mix[:, t % 2, :, :], seg[:, t, :, :],
                                                cb_mask[:, t % 2, :].unsqueeze(1).to_broadcast([P, NH, P]),
                                                ALU.mult).then_inc(s["mix"].sem, 1)
                    t = tile_at(n, it.at["main"])
                    if t is not None and t < TPB - 1:
                        dve.wait_ge(*done(s["a_ready"], it.use("a", f"state{t}")))
                        if t == 0:
                            nc.vector.tensor_copy(state[:, t % 2, :], a_ps[:, 0:DI]
                                                  ).then_inc(s["state"].sem, 1)
                        else:
                            dve.wait_ge(*done(s["state_dec"], b * (TPB - 2) + (t - 1)))
                            nc.vector.tensor_tensor(state[:, t % 2, :], state_dec[:, :], a_ps[:, 0:DI],
                                                    ALU.add).then_inc(s["state"].sem, 1)
                        dve.wait_ge(*done(s["state"], b * (TPB - 1) + t))
                        dve.sem_inc(s["a_read"].sem, 1)
                    t = tile_at(n, it.at["y"])
                    if t is not None:
                        y_of(it, t)
                    t = tile_at(n, it.at["out"])
                    if t is not None:
                        dve.wait_ge(*done(s["inv_rms"], it.ssm_tile(t)))
                        dve.wait_ge(*done(s["a_ready"], it.use("a", f"out{t}")))
                        nc.vector.scalar_tensor_tensor(x_of(b, t), a_ps[:, 0:D], inv_rms[:, t:t + 1],
                                                       x_of(b, t), ALU.mult, ALU.add
                                                       ).then_inc(s["a_read"].sem, 1)

                def tap(it, f, back):
                    bank, ps = FILL_BANK[f], shared[FILL_BANK[f]]
                    i = (it.i * CB + (f - 2)) * (TAPS - 2) + (back - 1)
                    if back == 1:
                        dve.wait_ge(*done(s["tap0"], it.i * CB + (f - 2)))
                    else:
                        dve.wait_ge(*done(s["tap"], i - 1))
                    signal = s["tap"] if back < TAPS - 1 else s[bank + "_read"]
                    nc.vector.scalar_tensor_tensor(
                        chan[:, f - 2, back:], ps[:, 0:SEQ - back],
                        m.conv_w[:, f - 2, TAPS - 1 - back:TAPS - back], chan[:, f - 2, back:],
                        ALU.mult, ALU.add).then_inc(signal.sem, 1)

                def norm_next(it, n):
                    b = it.i + 1
                    if n == it.at["stats"]:
                        dve.wait_ge(*done(s["x_updated"], it.run(0)))
                        dve.sem_inc(s["dve_held"].sem, 1)
                        for t in range(TPB):
                            last = nc.vector.bn_stats(stats[:, t, :], x_of(b, t))
                        last.then_inc(s["stats"].sem, 1)
                    if n == it.at["moments"]:
                        dve.wait_ge(*done(s["stats"], b))
                        aggregate(stats, moments, range(TPB), s["moments"])
                    if n == it.at["xn"]:
                        dve.wait_ge(*done(s["rstd"], b))
                        normed(lambda t: xn[:, t, :], lambda t: x_of(b, t), moments, rstd, range(TPB),
                               s["xn"].sem)

                def y_of(it, t):
                    b = it.i
                    dve.wait_ge(*done(s["d_ready"], it.use("d", f"y{t}")))
                    if t:
                        nc.vector.tensor_tensor(by_head(y_in[:, :]), by_head(d_ps[:, DI:]),
                                                heads(decay[:, 0, t, :]), ALU.mult)
                    dve.wait_ge(*done(s["skip"], it.ssm_tile(t)))
                    nc.vector.tensor_tensor(y[:, t % 2, :], skip[:, t % 2, :], d_ps[:, 0:DI], ALU.add
                                            ).then_inc(s["d_read"].sem, 1)
                    dve.wait_ge(*done(s["d_read"], it.use("d", f"y{t}")))
                    if t:
                        nc.vector.tensor_tensor(y[:, t % 2, :], y[:, t % 2, :], y_in[:, :], ALU.add
                                                ).then_inc(s["y_sum"].sem, 1)
                        dve.wait_ge(*done(s["y_sum"], b * (TPB - 1) + (t - 1)))
                    nc.vector.tensor_tensor(y[:, t % 2, :], y[:, t % 2, :], gate[:, t, :], ALU.mult
                                            ).then_inc(s["yg"].sem, 1)

                def step(it, n):
                    if it.has["first"] and n == it.at["w2_lo"]:
                        dve.wait_ge(*done(s["w2_hi"], 0))
                        nc.vector.tensor_tensor(m.w2_lo[:, :], m.w2_raw, m.w2_hi[:, :].bitcast(F32),
                                                ALU.subtract).then_inc(s["w2_lo"].sem, 1)
                    if it.has["first"] and n == it.at["w1_lo"]:
                        dve.wait_ge(*done(s["w1_hi"], 0))
                        nc.vector.tensor_tensor(m.w1_lo[:, :], m.w1_raw, m.w1_hi[:, :].bitcast(F32),
                                                ALU.subtract).then_inc(s["w1_lo"].sem, 1)
                    if routed(it, n):
                        k, i, side = it.block(n)
                        if ORDER[k] == ("routed", 0):
                            dve.wait_ge(*done(s[f"weights{side}"], it.ffn_batch(side)))
                        dve.wait_ge(*done(s["gated"], it.gate(n) - 1))
                        dve.sem_inc(s["dve_held"].sem, 1)
                        nc.vector.stream_shuffle(cw_ps[:, :], weights[:, side, :], [ORDER[k][1]] * 32
                                                 ).then_inc(s["shuffled"].sem, 1)
                    if it.block(n - HI_LAG) and not routed(it, n - HI_LAG):
                        dve.wait_ge(*part("hi", it, n - HI_LAG))
                        nc.vector.tensor_tensor(hid_lo[:, (n - HI_LAG) % RING, :], hidden[:, (n - HI_LAG) % RING, :],
                                                hid_hi[:, (n - HI_LAG) % RING, :].bitcast(F32), ALU.subtract
                                                ).then_inc(s["lo_shared"].sem, 1)
                    if routed(it, n):
                        dve.wait_ge(*done(s["shuffled"], it.gate(n)))
                        dve.wait_ge(*done(s["silu_done"], i))
                        nc.vector.tensor_tensor(hidden[:, n % RING, :], hidden[:, n % RING, :], cw_ps[:, :],
                                                ALU.mult).then_inc(s["gated"].sem, 1)
                    if it.has["ffn0"]:
                        norm_next(it, n)
                    if it.has["ssm"]:
                        ssm(it, n)
                    if it.sides:
                        router(it, n)
                    for side in range(2):
                        if n == it.at[f"ffn_y{side}"] + 2 and it.has[f"ffn{side}"]:
                            dve.wait_ge(*done(s["b_ready"], it.use("b", f"ffn_yT{side}")))
                            nc.vector.tensor_tensor(x_batch(it.ffn_batch(side)), b_ps[:, :],
                                                    x_batch(it.ffn_batch(side)), ALU.add
                                                    ).then_inc(s["x_updated"].sem, 1)
                            dve.wait_ge(*done(s["x_updated"], it.run(side)))
                            dve.sem_inc(s["b_read"].sem, 1)

                iterations(dve, step)

            @block.gpsimd
            def _(pool):
                s.give_credits(pool)
                nc.gpsimd.memset(cwq[:, :, :, :], 0.0).then_inc(s["zeroed"].sem, 1)
                pool.wait_ge(s["zeroed"].sem, 1)

                def inverse_root(var, moments, out, tiles, moments_done, var_done, out_done, n):
                    pool.wait_ge(*done(moments_done, n))
                    pool.sem_inc(s["pool_held"].sem, 1)
                    nc.gpsimd.tensor_scalar(var[:, tiles], moments[:, tiles, 1], 1.0, EPS, ALU.mult, ALU.add
                                            ).then_inc(var_done.sem, 1)
                    pool.wait_ge(*done(var_done, n))
                    nc.gpsimd.tensor_tensor(out[:, tiles], var[:, tiles], m.minus_half[:, tiles], ALU.pow
                                            ).then_inc(out_done.sem, 1)

                def router(it, n):
                    r, run = tiles_of(it), it.i + 2
                    if n == it.at["r_rstd"]:
                        inverse_root(r_var, r_moments, r_rstd, r, s["r_moments"], s["r_var"], s["r_rstd"], run)
                    if n == it.at["shifted"]:
                        pool.wait_ge(*done(s["peak"], run))
                        nc.gpsimd.tensor_tensor(logits[:, r, :], logits[:, r, :],
                                                peak[:, r].unsqueeze(2).to_broadcast([P, r.stop - r.start, E]),
                                                ALU.subtract).then_inc(s["shifted"].sem, 1)
                    for side in it.sides:
                        batch = it.router_batch(side)
                        r = slice(side * TPB, (side + 1) * TPB)
                        if n == it.at[f"top_probs{side}"]:
                            pool.wait_ge(*done(s[f"rest{side}"], batch))
                            nc.gpsimd.tensor_tensor(probs[:, r, :], probs[:, r, :], rest[:, r, :],
                                                    ALU.subtract).then_inc(s[f"top_probs{side}"].sem, 1)
                        if n == it.at[f"cwq{side}"]:
                            pool.wait_ge(*done(s[f"top_inv{side}"], batch))
                            pool.wait_ge(*done(s[f"top_probs{side}"], batch))
                            for t in range(side * TPB, (side + 1) * TPB):
                                last = nc.gpsimd.tensor_tensor(
                                    cwq[:, t, :, 0:E // 4], probs[:, t, :].rearrange("p (j q) -> p q j", q=4),
                                    top_inv[:, t:t + 1].unsqueeze(2).to_broadcast([P, 4, E // 4]), ALU.mult)
                            last.then_inc(s[f"cwq{side}"].sem, 1)
                        if n == it.at[f"xn_hi{side}"]:
                            pool.wait_ge(*done(s[f"xn_hi{side}"], it.router_batch(side)))
                            nc.gpsimd.tensor_tensor(xn_lo[:, side, :], r_xT[:, side, :],
                                                    xn_hi[:, side, :].bitcast(F32), ALU.subtract
                                                    ).then_inc(s[f"xn_lo{side}"].sem, 1)

                def ssm(it, n):
                    b = it.i
                    for t in range(TPB):
                        if n == it.at["seg_rhs"][t]:
                            pool.wait_ge(*done(s["dA"], b))
                            nc.gpsimd.tensor_tensor(seg_rhs[:, t, :, :],
                                                    dA[:, t, :].unsqueeze(2).to_broadcast([P, NH, P]),
                                                    m.upto[:, :].unsqueeze(1).to_broadcast([P, NH, P]),
                                                    ALU.mult).then_inc(s["seg_rhs"].sem, 1)
                    if n == it.at["decays"] + 1:
                        pool.wait_ge(*done(s["b_read"], it.use("b", "sums")))
                        nc.gpsimd.tensor_tensor(dt_after[:, :, :], dt[:, :, :], decay[:, 1, :, :], ALU.mult
                                                ).then_inc(s["dt_after"].sem, 1)
                    t = tile_at(n, it.at["pre"])
                    if t is not None:
                        x_tok = by_head(tok[:, t % 2, 0:DI])
                        pool.wait_ge(*done(s["dt_after"], b))
                        pool.wait_ge(*done(s["c_read"], it.use("c", f"tok{t}")))
                        if t < TPB - 1:
                            nc.gpsimd.tensor_tensor(by_head(dx_after[:, t % 2, :]), x_tok,
                                                    heads(dt_after[:, t, :]), ALU.mult
                                                    ).then_inc(s["dx_after"].sem, 1)
                        nc.gpsimd.tensor_tensor(by_head(dx[:, t % 2, :]), x_tok, heads(dt[:, t, :]), ALU.mult
                                                ).then_inc(s["dx"].sem, 1)
                        nc.gpsimd.tensor_tensor(by_head(skip[:, t % 2, :]), x_tok,
                                                heads(m.rows[:, E + 2 * NH:E + 3 * NH]), ALU.mult
                                                ).then_inc(s["skip"].sem, 1)
                    t = tile_at(n, it.at["state_dec"])
                    if t is not None and 1 <= t < TPB - 1:
                        pool.wait_ge(*done(s["state"], b * (TPB - 1) + (t - 1)))
                        nc.gpsimd.tensor_tensor(by_head(state_dec[:, :]), by_head(state[:, (t - 1) % 2, :]),
                                                heads(decay[:, 2, t, :]), ALU.mult
                                                ).then_inc(s["state_dec"].sem, 1)
                    t = tile_at(n, it.at["rms"])
                    if t is not None:
                        i = slice(t, t + 1)
                        pool.wait_ge(*done(s["sum_sq"], it.ssm_tile(t)))
                        pool.sem_inc(s["pool_held"].sem, 1)
                        nc.gpsimd.tensor_scalar(mean_sq[:, i], sum_sq[:, i], 1.0 / DI, EPS, ALU.mult, ALU.add
                                                ).then_inc(s["mean_sq"].sem, 1)
                        pool.wait_ge(*done(s["mean_sq"], it.ssm_tile(t)))
                        nc.gpsimd.tensor_tensor(inv_rms[:, i], mean_sq[:, i], m.minus_half[:, 0:1], ALU.pow
                                                ).then_inc(s["inv_rms"].sem, 1)

                def step(it, n):
                    if routed(it, n - HI_LAG):
                        pool.wait_ge(*part("hi", it, n - HI_LAG))
                        nc.gpsimd.tensor_tensor(hid_lo[:, (n - HI_LAG) % RING, :], hidden[:, (n - HI_LAG) % RING, :],
                                                hid_hi[:, (n - HI_LAG) % RING, :].bitcast(F32), ALU.subtract
                                                ).then_inc(s["lo_routed"].sem, 1)
                    if it.has["ffn0"] and n == it.at["rstd"]:
                        inverse_root(var_eps, moments, rstd, slice(0, TPB), s["moments"], s["var_eps"],
                                     s["rstd"], it.i + 1)
                    if it.has["ssm"]:
                        ssm(it, n)
                    if it.sides:
                        router(it, n)

                iterations(pool, step)




def program(nc, arrays, out):
    with ExitStack() as ctx:
        m = Tensors()

        def sb(name, shape, dt=F32):
            return ctx.enter_context(nc.sbuf_tensor(name, shape, dt))

        m.x = sb("x_res", [P, TOKENS // P * D])
        m.w1_hi, m.w1_lo = sb("w1_hi", [P, BLOCKS * P], F32R), sb("w1_lo", [P, BLOCKS * P], F32R)
        m.w2_hi, m.w2_lo = sb("w2_hi", [P, BLOCKS * P], F32R), sb("w2_lo", [P, BLOCKS * P], F32R)
        m.hidden = sb("hidden", [P, RING, SEQ])
        m.hid_hi, m.hid_lo = sb("hid_hi", [P, RING, SEQ], F32R), sb("hid_lo", [P, RING, SEQ], F32R)
        m.gate_chan = sb("gate_chan", [P, CB * SEQ + TPB * DI])
        m.w1_raw = m.hidden[:, :, :].rearrange("p r n -> p (r n)")
        m.w2_raw = m.gate_chan[:, 0:BLOCKS * P]
        m.w1_in = ctx.enter_context(nc.semaphore("w1_in"))
        m.w2_in = ctx.enter_context(nc.semaphore("w2_in"))
        m.wz_hi, m.wz_lo = sb("wz_hi", [P, ZW + NH], F32R), sb("wz_lo", [P, ZW + NH], F32R)
        m.wc_hi, m.wc_lo = sb("wc_hi", [P, CB * P], F32R), sb("wc_lo", [P, CB * P], F32R)
        m.conv_w = sb("conv_w", [P, CB, TAPS])
        m.wout = sb("wout", [P, DI // P, D])
        m.router_w = sb("router_w", [P, E])
        m.cols = sb("cols", [P, N_COLS])
        m.rows = sb("rows", [P, N_ROWS])
        m.a_neg = sb("a_neg", [P, NH])
        m.b2q = sb("b2q", [P, D])
        m.half_sb2 = sb("half_sb2", [P, 1])
        m.ident, m.upto, m.after = sb("ident", [P, P]), sb("upto", [P, P]), sb("after", [P, P])
        m.ones, m.minus_half = sb("ones", [P, P]), sb("minus_half", [P, 2 * TPB])
        prepare_phase(nc, m, arrays)
        main_phase(nc, m, out)


_NAMES = {"L0_attn_u": "u", "L0_attn_W_in": "W_in", "L0_attn_conv_w": "conv_w", "L0_attn_conv_b": "conv_b",
          "L0_attn_dt_bias": "dt_bias", "L0_attn_A_log": "A_log", "L0_attn_D_param": "D_param",
          "L0_attn_norm_w": "norm_w", "L0_attn_W_out": "W_out", "L0_ffn_router_w": "router_w",
          "L0_ffn_router_b": "router_b", "L0_ffn_w1": "w1", "L0_ffn_b1": "b1", "L0_ffn_w2": "w2",
          "L0_ffn_b2": "b2", "L0_ffn_sw1": "sw1", "L0_ffn_sb1": "sb1", "L0_ffn_sw2": "sw2",
          "L0_ffn_sb2": "sb2"}


def kernel(**inputs):
    import numpy as _np
    import concourse.bacc as _bacc
    from concourse import mybir as _mybir
    from concourse.bass_utils import run_bass_kernel_spmd as _run

    nc = _bacc.Bacc("TRN2", target_bir_lowering=False, num_devices=1)
    arrays, aps = {}, {}
    for name, short in _NAMES.items():
        arr = _np.ascontiguousarray(inputs[name])
        arrays[f"in_{short}"] = arr
        aps[short] = nc.dram_tensor(f"in_{short}", arr.shape, _mybir.dt.from_np(arr.dtype),
                                    kind="ExternalInput").ap()
    out = nc.dram_tensor("out_x", (BATCHES, SEQ, D), _mybir.dt.float32, kind="ExternalOutput").ap()
    program(nc, aps, out)
    r = _run(nc, [arrays], core_ids=[0])
    return r.results[0]["out_x"]
```
